# Optimizing a Trainium2 kernel written in Bass

```python
import numpy as np
import jax
import jax.numpy as jnp

def _softmax(x, axis=-1):
    return jax.nn.softmax(x, axis=axis)

def _gelu(x):
    return jax.nn.gelu(x, approximate=True)

def _silu(x):
    return jax.nn.silu(x)

def _sigmoid(x):
    return jax.nn.sigmoid(x)

def _layernorm(x, axis=-1, eps=1e-05):
    m = jnp.mean(x, axis=axis, keepdims=True)
    v = jnp.var(x, axis=axis, keepdims=True)
    return (x - m) / jnp.sqrt(v + eps)

def _scatter_add(tgt, idx, src, axis=0):
    return tgt.at[idx].add(src)

def _segment_sum(src, seg, n):
    return jax.ops.segment_sum(src, seg, n)
kernel_name = 'mk_hybrid_d2_jaxref_r8_922352'

def setup_inputs(seed: int=0):
    np.random.seed(seed)
    _w = jnp.asarray

    def _L0_attn_a_setup():
        import jax, jax.numpy as jnp
        import numpy as np
        D_MODEL = 128
        N_HEADS = 16
        N_KV = 4
        HEAD_DIM = D_MODEL // N_HEADS
        SEQ = 256
        BATCH = 2
        CAP = 50.0
        EPS = 1e-05
        THETA = 10000.0

        def _rms_norm(x, eps=EPS):
            return x * jax.lax.rsqrt(jnp.mean(jnp.square(x), axis=-1, keepdims=True) + eps)

        def _rope_cos_sin(seq_len, head_dim, theta=THETA):
            inv_freq = 1.0 / theta ** (jnp.arange(0, head_dim, 2, dtype=jnp.float32) / head_dim)
            freqs = jnp.arange(seq_len, dtype=jnp.float32)[:, None] * inv_freq[None, :]
            return (jnp.cos(freqs)[None, :, None, :], jnp.sin(freqs)[None, :, None, :])

        def _apply_rope(x, cos, sin):
            d = x.shape[-1] // 2
            x1, x2 = (x[..., :d], x[..., d:])
            return jnp.concatenate([x1 * cos - x2 * sin, x2 * cos + x1 * sin], axis=-1).astype(x.dtype)
        key = jax.random.key(seed)
        ks = jax.random.split(key, 5)
        s = 0.02
        return {'x': jax.random.normal(ks[0], (BATCH, SEQ, D_MODEL), dtype=jnp.float32), 'w_q': jax.random.normal(ks[1], (D_MODEL, N_HEADS * HEAD_DIM), dtype=jnp.float32) * s, 'w_k': jax.random.normal(ks[2], (D_MODEL, N_KV * HEAD_DIM), dtype=jnp.float32) * s, 'w_v': jax.random.normal(ks[3], (D_MODEL, N_KV * HEAD_DIM), dtype=jnp.float32) * s, 'w_o': jax.random.normal(ks[4], (N_HEADS * HEAD_DIM, D_MODEL), dtype=jnp.float32) * s}
    _L0_attn_a_in = _L0_attn_a_setup()

    def _L0_attn_b_setup():
        import jax, jax.numpy as jnp
        import numpy as np
        B, S, D, H = (2, 256, 128, 16)
        DH = D // H
        RD = DH // 2
        EPS = 1e-05

        def _rope(x):
            seq = x.shape[-2]
            inv_freq = 1.0 / 10000.0 ** (jnp.arange(0, RD, 2, dtype=jnp.float32) / RD)
            t = jnp.arange(seq, dtype=jnp.float32)
            freqs = t[:, None] * inv_freq[None, :]
            freqs = jnp.repeat(freqs, 2, axis=-1)
            cosf, sinf = (jnp.cos(freqs), jnp.sin(freqs))
            xr, xp = (x[..., :RD], x[..., RD:])
            pairs = xr.reshape(*xr.shape[:-1], RD // 2, 2)
            rot = jnp.stack([-pairs[..., 1], pairs[..., 0]], axis=-1).reshape(xr.shape)
            return jnp.concatenate([xr * cosf + rot * sinf, xp], axis=-1)
        key = jax.random.key(seed)
        ks = jax.random.split(key, 4)
        s = 0.02
        return {'X': jax.random.normal(ks[0], (B, S, D), jnp.float32), 'W_in': jax.random.normal(ks[1], (D, 3 * D), jnp.float32) * s, 'b_in': jnp.zeros((3 * D,), jnp.float32), 'W_out': jax.random.normal(ks[2], (D, D), jnp.float32) * s, 'b_out': jnp.zeros((D,), jnp.float32), 'gamma': jnp.ones((D,), jnp.float32), 'beta': jnp.zeros((D,), jnp.float32)}
    _L0_attn_b_in = _L0_attn_b_setup()

    def _L0_ffn_setup():
        import jax, jax.numpy as jnp
        import numpy as np
        B, S, D, O, E, R, TOP_K = (4, 128, 128, 128, 8, 16, 2)
        SCALING = 32.0 / 16.0
        NEG_INF = -1000000000.0
        key = jax.random.key(seed)
        ks = jax.random.split(key, 6)
        return {'x': jax.random.normal(ks[0], (B, S, D), jnp.float32), 'base_w': jax.random.normal(ks[1], (O, D), jnp.float32) * 0.02, 'base_b': jnp.zeros((O,), jnp.float32), 'lora_A': jax.random.normal(ks[2], (E, D, R), jnp.float32) * 0.02, 'lora_B': jax.random.normal(ks[3], (E, R, O), jnp.float32) * 0.02, 'router_w': jax.random.normal(ks[4], (E, D), jnp.float32) * 0.02, 'router_b': jnp.zeros((E,), jnp.float32)}
    _L0_ffn_in = _L0_ffn_setup()

    def _L1_attn_a_setup():
        import jax, jax.numpy as jnp
        import numpy as np
        B, L, D, H = (2, 128, 128, 8)
        HD = D // H

        def _deltanet(x, Wq, Wk, Wv, Wb, ln_w, ln_b):
            Bb, Ll, Dd = x.shape
            q = (x @ Wq).reshape(Bb, Ll, H, HD)
            k = (x @ Wk).reshape(Bb, Ll, H, HD)
            k = k / jnp.maximum(jnp.linalg.norm(k, axis=-1, keepdims=True), 1e-12)
            v = jax.nn.silu(x @ Wv).reshape(Bb, Ll, H, HD)
            beta = jax.nn.sigmoid(x @ Wb)
            qs = jnp.moveaxis(q, 1, 0)
            ks_ = jnp.moveaxis(k, 1, 0)
            vs = jnp.moveaxis(v, 1, 0)
            bs = jnp.moveaxis(beta, 1, 0)

            def step(S, inp):
                qt, kt, vt, bt = inp
                Sk = jnp.einsum('bhk,bhkv->bhv', kt, S)
                S = S + jnp.einsum('bh,bhk,bhv->bhkv', bt, kt, vt - Sk)
                ot = jnp.einsum('bhk,bhkv->bhv', qt, S)
                return (S, ot)
            S0 = jnp.zeros((Bb, H, HD, HD), x.dtype)
            _, os_ = jax.lax.scan(step, S0, (qs, ks_, vs, bs))
            o = jnp.moveaxis(os_, 0, 1).reshape(Bb, Ll, Dd)
            mu = jnp.mean(o, axis=-1, keepdims=True)
            var = jnp.var(o, axis=-1, keepdims=True)
            return (o - mu) / jnp.sqrt(var + 1e-05) * ln_w + ln_b
        key = jax.random.key(seed)
        ks = jax.random.split(key, 5)
        s = 1.0 / np.sqrt(D)
        x = jax.random.normal(ks[0], (B, L, D), jnp.float32)
        Wq = jax.random.uniform(ks[1], (D, D), jnp.float32, -s, s)
        Wk = jax.random.uniform(ks[2], (D, D), jnp.float32, -s, s)
        Wv = jax.random.uniform(ks[3], (D, D), jnp.float32, -s, s)
        Wb = jax.random.uniform(ks[4], (D, H), jnp.float32, -s, s)
        ln_w = jnp.ones((D,), jnp.float32)
        ln_b = jnp.zeros((D,), jnp.float32)
        return {'x': x, 'Wq': Wq, 'Wk': Wk, 'Wv': Wv, 'Wb': Wb, 'ln_w': ln_w, 'ln_b': ln_b}
    _L1_attn_a_in = _L1_attn_a_setup()

    def _L1_attn_b_setup():
        import jax, jax.numpy as jnp
        import numpy as np
        DIM = 128
        HID = 192
        K = 4
        B = 2
        T = 512
        C_CONST = 8.0

        def _hawk(x, W_proj, conv_w, conv_b, W_in, b_in, W_gate, b_gate, forget_lambda, W_out):
            gu = jnp.einsum('btc,hc->bth', x, W_proj)
            gate, u = jnp.split(gu, 2, axis=-1)
            u_nct = jnp.transpose(u, (0, 2, 1))
            u_c = jax.lax.conv_general_dilated(u_nct, conv_w, window_strides=(1,), padding=[(K - 1, 0)], dimension_numbers=('NCH', 'OIH', 'NCH'), feature_group_count=HID)
            u = jnp.transpose(u_c + conv_b[None, :, None], (0, 2, 1))
            input_gate = jnp.einsum('bth,gh->btg', u, W_in) + b_in
            rec_gate = jnp.einsum('bth,gh->btg', u, W_gate) + b_gate
            alpha = jnp.exp(-C_CONST * jax.nn.softplus(forget_lambda) * jax.nn.sigmoid(rec_gate))
            beta = jnp.sqrt(1.0 - alpha ** 2 + 1e-06)
            xbeta = beta * jax.nn.sigmoid(input_gate) * u

            def combine(e1, e2):
                a1, b1 = e1
                a2, b2 = e2
                return (a1 * a2, a2 * b1 + b2)
            _, h = jax.lax.associative_scan(combine, (alpha, xbeta), axis=1)
            return jnp.einsum('bth,ch->btc', jax.nn.gelu(gate, approximate=False) * h, W_out)
        key = jax.random.key(seed)
        ks = jax.random.split(key, 8)
        x = jax.random.normal(ks[0], (B, T, DIM), dtype=jnp.float32)
        W_proj = jax.random.normal(ks[1], (2 * HID, DIM), dtype=jnp.float32) * DIM ** (-0.5)
        conv_w = jax.random.normal(ks[2], (HID, 1, K), dtype=jnp.float32) * K ** (-0.5)
        conv_b = jax.random.normal(ks[3], (HID,), dtype=jnp.float32) * 0.02
        W_in = jax.random.normal(ks[4], (HID, HID), dtype=jnp.float32) * HID ** (-0.5)
        b_in = jnp.zeros((HID,), dtype=jnp.float32)
        W_gate = jax.random.normal(ks[5], (HID, HID), dtype=jnp.float32) * HID ** (-0.5)
        b_gate = jnp.zeros((HID,), dtype=jnp.float32)
        forget_lambda = jnp.linspace(-4.323, -9.0, HID, dtype=jnp.float32)
        W_out = jax.random.normal(ks[6], (DIM, HID), dtype=jnp.float32) * HID ** (-0.5)
        return {'x': x, 'W_proj': W_proj, 'conv_w': conv_w, 'conv_b': conv_b, 'W_in': W_in, 'b_in': b_in, 'W_gate': W_gate, 'b_gate': b_gate, 'forget_lambda': forget_lambda, 'W_out': W_out}
    _L1_attn_b_in = _L1_attn_b_setup()

    def _L1_ffn_setup():
        import jax, jax.numpy as jnp
        import numpy as np
        D = 128
        H = 16
        HD = D // H
        L = 64
        E = 8
        B, T = (4, 256)
        EPS = 1e-06

        def _glorot(k, shape):
            fan_in, fan_out = (shape[-2], shape[-1])
            lim = np.sqrt(6.0 / (fan_in + fan_out)).astype(np.float32)
            return jax.random.uniform(k, shape, jnp.float32, -lim, lim)

        def _rmsnorm(x, gamma):
            return gamma * x * jax.lax.rsqrt(jnp.mean(x * x, axis=-1, keepdims=True) + EPS)
        key = jax.random.key(seed)
        ks = jax.random.split(key, 8)
        return {'x': jax.random.normal(ks[0], (B, T, D), jnp.float32), 'gamma1': jnp.ones((D,), jnp.float32), 'Wq': _glorot(ks[1], (D, D)), 'bq': jnp.zeros((D,), jnp.float32), 'Wdown': _glorot(ks[2], (D, L)), 'bdown': jnp.zeros((L,), jnp.float32), 'Wup': _glorot(ks[3], (L, 2 * D)), 'bup': jnp.zeros((2 * D,), jnp.float32), 'Wo': _glorot(ks[4], (D, D)), 'bo': jnp.zeros((D,), jnp.float32), 'gamma2': jnp.ones((D,), jnp.float32), 'Wg': _glorot(ks[5], (D, E)), 'bg': jnp.zeros((E,), jnp.float32), 'We': _glorot(ks[6], (E, D, D))}
    _L1_ffn_in = _L1_ffn_setup()
    _d = {'L0_attn_a_x': _L0_attn_a_in['x'], 'L0_attn_a_w_q': _L0_attn_a_in['w_q'], 'L0_attn_a_w_k': _L0_attn_a_in['w_k'], 'L0_attn_a_w_v': _L0_attn_a_in['w_v'], 'L0_attn_a_w_o': _L0_attn_a_in['w_o'], 'L0_attn_b_W_in': _L0_attn_b_in['W_in'], 'L0_attn_b_b_in': _L0_attn_b_in['b_in'], 'L0_attn_b_W_out': _L0_attn_b_in['W_out'], 'L0_attn_b_b_out': _L0_attn_b_in['b_out'], 'L0_attn_b_gamma': _L0_attn_b_in['gamma'], 'L0_attn_b_beta': _L0_attn_b_in['beta'], 'L0_ffn_base_w': _L0_ffn_in['base_w'], 'L0_ffn_base_b': _L0_ffn_in['base_b'], 'L0_ffn_lora_A': _L0_ffn_in['lora_A'], 'L0_ffn_lora_B': _L0_ffn_in['lora_B'], 'L0_ffn_router_w': _L0_ffn_in['router_w'], 'L0_ffn_router_b': _L0_ffn_in['router_b'], 'L1_attn_a_Wq': _L1_attn_a_in['Wq'], 'L1_attn_a_Wk': _L1_attn_a_in['Wk'], 'L1_attn_a_Wv': _L1_attn_a_in['Wv'], 'L1_attn_a_Wb': _L1_attn_a_in['Wb'], 'L1_attn_a_ln_w': _L1_attn_a_in['ln_w'], 'L1_attn_a_ln_b': _L1_attn_a_in['ln_b'], 'L1_attn_b_W_proj': _L1_attn_b_in['W_proj'], 'L1_attn_b_conv_w': _L1_attn_b_in['conv_w'], 'L1_attn_b_conv_b': _L1_attn_b_in['conv_b'], 'L1_attn_b_W_in': _L1_attn_b_in['W_in'], 'L1_attn_b_b_in': _L1_attn_b_in['b_in'], 'L1_attn_b_W_gate': _L1_attn_b_in['W_gate'], 'L1_attn_b_b_gate': _L1_attn_b_in['b_gate'], 'L1_attn_b_forget_lambda': _L1_attn_b_in['forget_lambda'], 'L1_attn_b_W_out': _L1_attn_b_in['W_out'], 'L1_ffn_gamma1': _L1_ffn_in['gamma1'], 'L1_ffn_Wq': _L1_ffn_in['Wq'], 'L1_ffn_bq': _L1_ffn_in['bq'], 'L1_ffn_Wdown': _L1_ffn_in['Wdown'], 'L1_ffn_bdown': _L1_ffn_in['bdown'], 'L1_ffn_Wup': _L1_ffn_in['Wup'], 'L1_ffn_bup': _L1_ffn_in['bup'], 'L1_ffn_Wo': _L1_ffn_in['Wo'], 'L1_ffn_bo': _L1_ffn_in['bo'], 'L1_ffn_gamma2': _L1_ffn_in['gamma2'], 'L1_ffn_Wg': _L1_ffn_in['Wg'], 'L1_ffn_bg': _L1_ffn_in['bg'], 'L1_ffn_We': _L1_ffn_in['We']}
    _x0 = _d['L0_attn_a_x']
    _d['L0_attn_a_x'] = jax.random.normal(jax.random.fold_in(jax.random.key(seed), 1), (32, 256, 128), dtype=_x0.dtype)
    del _x0
    return _d

def reference(L0_attn_a_x, L0_attn_a_w_q, L0_attn_a_w_k, L0_attn_a_w_v, L0_attn_a_w_o, L0_attn_b_W_in, L0_attn_b_b_in, L0_attn_b_W_out, L0_attn_b_b_out, L0_attn_b_gamma, L0_attn_b_beta, L0_ffn_base_w, L0_ffn_base_b, L0_ffn_lora_A, L0_ffn_lora_B, L0_ffn_router_w, L0_ffn_router_b, L1_attn_a_Wq, L1_attn_a_Wk, L1_attn_a_Wv, L1_attn_a_Wb, L1_attn_a_ln_w, L1_attn_a_ln_b, L1_attn_b_W_proj, L1_attn_b_conv_w, L1_attn_b_conv_b, L1_attn_b_W_in, L1_attn_b_b_in, L1_attn_b_W_gate, L1_attn_b_b_gate, L1_attn_b_forget_lambda, L1_attn_b_W_out, L1_ffn_gamma1, L1_ffn_Wq, L1_ffn_bq, L1_ffn_Wdown, L1_ffn_bdown, L1_ffn_Wup, L1_ffn_bup, L1_ffn_Wo, L1_ffn_bo, L1_ffn_gamma2, L1_ffn_Wg, L1_ffn_bg, L1_ffn_We):

    def _L0_attn_a_ref(x, w_q, w_k, w_v, w_o):
        import jax, jax.numpy as jnp
        import numpy as np
        D_MODEL = 128
        N_HEADS = 16
        N_KV = 4
        HEAD_DIM = D_MODEL // N_HEADS
        SEQ = 256
        BATCH = 2
        CAP = 50.0
        EPS = 1e-05
        THETA = 10000.0

        def _rms_norm(x, eps=EPS):
            return x * jax.lax.rsqrt(jnp.mean(jnp.square(x), axis=-1, keepdims=True) + eps)

        def _rope_cos_sin(seq_len, head_dim, theta=THETA):
            inv_freq = 1.0 / theta ** (jnp.arange(0, head_dim, 2, dtype=jnp.float32) / head_dim)
            freqs = jnp.arange(seq_len, dtype=jnp.float32)[:, None] * inv_freq[None, :]
            return (jnp.cos(freqs)[None, :, None, :], jnp.sin(freqs)[None, :, None, :])

        def _apply_rope(x, cos, sin):
            d = x.shape[-1] // 2
            x1, x2 = (x[..., :d], x[..., d:])
            return jnp.concatenate([x1 * cos - x2 * sin, x2 * cos + x1 * sin], axis=-1).astype(x.dtype)
        B, S, _ = x.shape
        q = (x @ w_q).reshape(B, S, N_HEADS, HEAD_DIM)
        k = (x @ w_k).reshape(B, S, N_KV, HEAD_DIM)
        v = (x @ w_v).reshape(B, S, N_KV, HEAD_DIM)
        q = _rms_norm(q)
        k = _rms_norm(k)
        cos, sin = _rope_cos_sin(S, HEAD_DIM)
        q = _apply_rope(q, cos, sin)
        k = _apply_rope(k, cos, sin)
        rep = N_HEADS // N_KV
        k = jnp.repeat(k, rep, axis=2)
        v = jnp.repeat(v, rep, axis=2)
        scores = jnp.einsum('bqhd,bkhd->bhqk', q, k) / np.sqrt(HEAD_DIM).astype(np.float32)
        scores = jnp.tanh(scores.astype(jnp.float32) / CAP) * CAP
        causal = jnp.tril(jnp.ones((S, S), dtype=bool))
        scores = jnp.where(causal[None, None], scores, -jnp.inf)
        probs = jax.nn.softmax(scores, axis=-1)
        y = jnp.einsum('bhqk,bkhd->bqhd', probs, v).reshape(B, S, N_HEADS * HEAD_DIM)
        return y @ w_o

    def _L0_attn_b_ref(X, W_in, b_in, W_out, b_out, gamma, beta):
        import jax, jax.numpy as jnp
        import numpy as np
        B, S, D, H = (2, 256, 128, 16)
        DH = D // H
        RD = DH // 2
        EPS = 1e-05

        def _rope(x):
            seq = x.shape[-2]
            inv_freq = 1.0 / 10000.0 ** (jnp.arange(0, RD, 2, dtype=jnp.float32) / RD)
            t = jnp.arange(seq, dtype=jnp.float32)
            freqs = t[:, None] * inv_freq[None, :]
            freqs = jnp.repeat(freqs, 2, axis=-1)
            cosf, sinf = (jnp.cos(freqs), jnp.sin(freqs))
            xr, xp = (x[..., :RD], x[..., RD:])
            pairs = xr.reshape(*xr.shape[:-1], RD // 2, 2)
            rot = jnp.stack([-pairs[..., 1], pairs[..., 0]], axis=-1).reshape(xr.shape)
            return jnp.concatenate([xr * cosf + rot * sinf, xp], axis=-1)
        b, s, d = X.shape
        mu = jnp.mean(X, axis=-1, keepdims=True)
        var = jnp.var(X, axis=-1, keepdims=True)
        xn = (X - mu) * jax.lax.rsqrt(var + EPS) * gamma + beta
        qkv = xn @ W_in + b_in
        q, k, v = jnp.split(qkv, 3, axis=-1)

        def to_heads(t):
            return t.reshape(b, s, H, DH).transpose(0, 2, 1, 3)
        q, k, v = (to_heads(q), to_heads(k), to_heads(v))
        q, k = (_rope(q), _rope(k))
        scores = jnp.einsum('bhqd,bhkd->bhqk', q, k) / jnp.sqrt(jnp.float32(DH))
        attn = jax.nn.softmax(scores, axis=-1)
        ctx = jnp.einsum('bhqk,bhkd->bhqd', attn, v)
        ctx = ctx.transpose(0, 2, 1, 3).reshape(b, s, d)
        return ctx @ W_out + b_out + X

    def _L0_ffn_ref(x, base_w, base_b, lora_A, lora_B, router_w, router_b):
        import jax, jax.numpy as jnp
        import numpy as np
        B, S, D, O, E, R, TOP_K = (4, 128, 128, 128, 8, 16, 2)
        SCALING = 32.0 / 16.0
        NEG_INF = -1000000000.0
        result = jnp.einsum('bsd,od->bso', x, base_w) + base_b
        ax = jnp.einsum('bsd,edr->bser', x, lora_A)
        bax = jnp.einsum('bser,ero->bseo', ax, lora_B)
        logits = jnp.einsum('bsd,ed->bse', x, router_w) + router_b
        kth = jax.lax.top_k(logits, TOP_K)[0][..., -1:]
        masked = jnp.where(logits < kth, NEG_INF, logits)
        expert_weights = jax.nn.softmax(masked, axis=-1)
        return result + SCALING * jnp.einsum('bse,bseo->bso', expert_weights, bax)

    def _L1_attn_a_ref(x, Wq, Wk, Wv, Wb, ln_w, ln_b):
        import jax, jax.numpy as jnp
        import numpy as np
        B, L, D, H = (2, 128, 128, 8)
        HD = D // H

        def _deltanet(x, Wq, Wk, Wv, Wb, ln_w, ln_b):
            Bb, Ll, Dd = x.shape
            q = (x @ Wq).reshape(Bb, Ll, H, HD)
            k = (x @ Wk).reshape(Bb, Ll, H, HD)
            k = k / jnp.maximum(jnp.linalg.norm(k, axis=-1, keepdims=True), 1e-12)
            v = jax.nn.silu(x @ Wv).reshape(Bb, Ll, H, HD)
            beta = jax.nn.sigmoid(x @ Wb)
            qs = jnp.moveaxis(q, 1, 0)
            ks_ = jnp.moveaxis(k, 1, 0)
            vs = jnp.moveaxis(v, 1, 0)
            bs = jnp.moveaxis(beta, 1, 0)

            def step(S, inp):
                qt, kt, vt, bt = inp
                Sk = jnp.einsum('bhk,bhkv->bhv', kt, S)
                S = S + jnp.einsum('bh,bhk,bhv->bhkv', bt, kt, vt - Sk)
                ot = jnp.einsum('bhk,bhkv->bhv', qt, S)
                return (S, ot)
            S0 = jnp.zeros((Bb, H, HD, HD), x.dtype)
            _, os_ = jax.lax.scan(step, S0, (qs, ks_, vs, bs))
            o = jnp.moveaxis(os_, 0, 1).reshape(Bb, Ll, Dd)
            mu = jnp.mean(o, axis=-1, keepdims=True)
            var = jnp.var(o, axis=-1, keepdims=True)
            return (o - mu) / jnp.sqrt(var + 1e-05) * ln_w + ln_b
        return _deltanet(x, Wq, Wk, Wv, Wb, ln_w, ln_b)

    def _L1_attn_b_ref(x, W_proj, conv_w, conv_b, W_in, b_in, W_gate, b_gate, forget_lambda, W_out):
        import jax, jax.numpy as jnp
        import numpy as np
        DIM = 128
        HID = 192
        K = 4
        B = 2
        T = 512
        C_CONST = 8.0

        def _hawk(x, W_proj, conv_w, conv_b, W_in, b_in, W_gate, b_gate, forget_lambda, W_out):
            gu = jnp.einsum('btc,hc->bth', x, W_proj)
            gate, u = jnp.split(gu, 2, axis=-1)
            u_nct = jnp.transpose(u, (0, 2, 1))
            u_c = jax.lax.conv_general_dilated(u_nct, conv_w, window_strides=(1,), padding=[(K - 1, 0)], dimension_numbers=('NCH', 'OIH', 'NCH'), feature_group_count=HID)
            u = jnp.transpose(u_c + conv_b[None, :, None], (0, 2, 1))
            input_gate = jnp.einsum('bth,gh->btg', u, W_in) + b_in
            rec_gate = jnp.einsum('bth,gh->btg', u, W_gate) + b_gate
            alpha = jnp.exp(-C_CONST * jax.nn.softplus(forget_lambda) * jax.nn.sigmoid(rec_gate))
            beta = jnp.sqrt(1.0 - alpha ** 2 + 1e-06)
            xbeta = beta * jax.nn.sigmoid(input_gate) * u

            def combine(e1, e2):
                a1, b1 = e1
                a2, b2 = e2
                return (a1 * a2, a2 * b1 + b2)
            _, h = jax.lax.associative_scan(combine, (alpha, xbeta), axis=1)
            return jnp.einsum('bth,ch->btc', jax.nn.gelu(gate, approximate=False) * h, W_out)
        return _hawk(x, W_proj, conv_w, conv_b, W_in, b_in, W_gate, b_gate, forget_lambda, W_out)

    def _L1_ffn_ref(x, gamma1, Wq, bq, Wdown, bdown, Wup, bup, Wo, bo, gamma2, Wg, bg, We):
        import jax, jax.numpy as jnp
        import numpy as np
        D = 128
        H = 16
        HD = D // H
        L = 64
        E = 8
        B, T = (4, 256)
        EPS = 1e-06

        def _glorot(k, shape):
            fan_in, fan_out = (shape[-2], shape[-1])
            lim = np.sqrt(6.0 / (fan_in + fan_out)).astype(np.float32)
            return jax.random.uniform(k, shape, jnp.float32, -lim, lim)

        def _rmsnorm(x, gamma):
            return gamma * x * jax.lax.rsqrt(jnp.mean(x * x, axis=-1, keepdims=True) + EPS)
        b, t = (x.shape[0], x.shape[1])
        h = _rmsnorm(x, gamma1)
        q = (h @ Wq + bq).reshape(b, t, H, HD)
        kv = ((h @ Wdown + bdown) @ Wup + bup).reshape(b, t, H, 2 * HD)
        k, v = jnp.split(kv, 2, axis=-1)
        att = jnp.einsum('bthd,btgd->bthg', q, k) / np.sqrt(HD).astype(np.float32)
        att = jax.nn.softmax(att, axis=-1)
        out = jnp.einsum('bthg,btgd->bthd', att, v).reshape(b, t, D)
        x = x + (out @ Wo + bo)
        h2 = _rmsnorm(x, gamma2)
        gate = jax.nn.softmax(h2 @ Wg + bg, axis=-1)
        combined = jnp.einsum('btd,edf,bte->btf', h2, We, gate)
        return x + combined
    x = L0_attn_a_x
    x = x + _L0_attn_a_ref(_layernorm(x, axis=-1), L0_attn_a_w_q, L0_attn_a_w_k, L0_attn_a_w_v, L0_attn_a_w_o)
    x = x + _L0_ffn_ref(_layernorm(x, axis=-1), L0_ffn_base_w, L0_ffn_base_b, L0_ffn_lora_A, L0_ffn_lora_B, L0_ffn_router_w, L0_ffn_router_b)
    x = x + _L0_attn_b_ref(_layernorm(x, axis=-1), L0_attn_b_W_in, L0_attn_b_b_in, L0_attn_b_W_out, L0_attn_b_b_out, L0_attn_b_gamma, L0_attn_b_beta)
    x = x + _L0_ffn_ref(_layernorm(x, axis=-1), L0_ffn_base_w, L0_ffn_base_b, L0_ffn_lora_A, L0_ffn_lora_B, L0_ffn_router_w, L0_ffn_router_b)
    x = x + _L1_attn_a_ref(_layernorm(x, axis=-1), L1_attn_a_Wq, L1_attn_a_Wk, L1_attn_a_Wv, L1_attn_a_Wb, L1_attn_a_ln_w, L1_attn_a_ln_b)
    x = x + _L1_ffn_ref(_layernorm(x, axis=-1), L1_ffn_gamma1, L1_ffn_Wq, L1_ffn_bq, L1_ffn_Wdown, L1_ffn_bdown, L1_ffn_Wup, L1_ffn_bup, L1_ffn_Wo, L1_ffn_bo, L1_ffn_gamma2, L1_ffn_Wg, L1_ffn_bg, L1_ffn_We)
    x = x + _L1_attn_b_ref(_layernorm(x, axis=-1), L1_attn_b_W_proj, L1_attn_b_conv_w, L1_attn_b_conv_b, L1_attn_b_W_in, L1_attn_b_b_in, L1_attn_b_W_gate, L1_attn_b_b_gate, L1_attn_b_forget_lambda, L1_attn_b_W_out)
    x = x + _L1_ffn_ref(_layernorm(x, axis=-1), L1_ffn_gamma1, L1_ffn_Wq, L1_ffn_bq, L1_ffn_Wdown, L1_ffn_bdown, L1_ffn_Wup, L1_ffn_bup, L1_ffn_Wo, L1_ffn_bo, L1_ffn_gamma2, L1_ffn_Wg, L1_ffn_bg, L1_ffn_We)
    return x

_drawn_inputs = setup_inputs


def setup_inputs(seed=0):
    import zlib

    import numpy as np

    out = dict(_drawn_inputs(seed))
    spreads = {'L0_attn_b_b_in': (0.0, 0.521),
     'L0_attn_b_b_out': (0.0, 0.1),
     'L0_attn_b_gamma': (1.0, 0.6),
     'L0_attn_b_beta': (0.0, 0.8),
     'L0_ffn_base_b': (0.0, 0.1),
     'L0_ffn_router_b': (0.0, 0.366),
     'L1_attn_a_ln_w': (1.0, 0.2),
     'L1_attn_a_ln_b': (0.0, 0.1),
     'L1_attn_b_b_in': (0.0, 0.8),
     'L1_attn_b_b_gate': (0.0, 2.0),
     'L1_ffn_gamma1': (1.0, 0.2),
     'L1_ffn_bq': (0.0, 0.67),
     'L1_ffn_bdown': (0.0, 0.518),
     'L1_ffn_bup': (0.0, 0.311),
     'L1_ffn_bo': (0.0, 0.1),
     'L1_ffn_gamma2': (1.0, 0.2),
     'L1_ffn_bg': (0.0, 0.42)}
    factors = {'L0_attn_a_w_q': 5.751,
     'L0_attn_a_w_k': 5.818,
     'L0_attn_a_w_v': 3.568,
     'L0_attn_a_w_o': 3.566,
     'L0_attn_b_W_in': 8.0,
     'L0_attn_b_W_out': 2.974,
     'L1_attn_b_conv_b': 4.058}
    for name, (base, spread) in spreads.items():
        noise = np.random.default_rng([zlib.crc32(name.encode()), seed]).standard_normal(out[name].shape)
        drawn = base * np.exp(spread * noise) if base else spread * noise
        out[name] = jnp.asarray(drawn.astype(out[name].dtype))
    for name, factor in factors.items():
        out[name] = (out[name] * factor).astype(out[name].dtype)
    return out
```

```python
from contextlib import ExitStack

import numpy as np

import concourse.bass as bass
from concourse import mybir

F32 = mybir.dt.float32
BF16 = mybir.dt.bfloat16
ALU = mybir.AluOpType
ACT = mybir.ActivationFunctionType
AX_X = mybir.AxisListType.X
LN_EXP_SET = "natural_log_exp_and_others"

P = 128
SEQS, SEQ = 32, 256
G = 2
TOK = G * SEQ
TT = TOK // P
TURNS = SEQS // G
HEADS, HD = 16, 8
KV_A = 4
DH, DD = 8, 16
EXPERTS = 8
RANK = 16
LATENT = 64
HID, HH = 192, 96
TAPS = 4
PARTS = 3
Q_BANDS = ((0, 0, 1), (1, 0, 1), (2, 0, 1), (3, 1, 2), (5, 1, 1))
K_BANDS = ((0, 0, 3), (3, 0, 1), (4, 0, 1), (5, 1, 1))
K_LOADS = sum(n for _, _, n in K_BANDS)
SHIFT_ROW = 96
SROWS = SHIFT_ROW + PARTS
PAIRS = G * HEADS // 2
QUADS = PAIRS // 2
SCAN_STEPS = 6
CAP = 50.0
STRIP = 32

WEIGHTS = dict(a_q=P, a_q2=P, a_k=32, a_k2=32, a_v=32, a_o=P,
               f_base=P, f_A=P, f_B=P, f_r=EXPERTS,
               b_q=P, b_q2=P, b_k=P, b_k2=P, b_v=P, b_o=P,
               d_q=P, d_k=P, d_v=P, d_b=DH,
               g_q=P, g_down=LATENT, g_up=2 * P, g_o=P, g_g=EXPERTS, g_e=EXPERTS * P,
               h_proj=2 * HID, h_in=2 * HID, h_gate=2 * HID, h_out=2 * P)
COLUMNS = dict(f_bb=1, b_bq=1, b_bq2=1, b_bk=1, b_bk2=1, b_bo=1, b_gamma=1, b_beta=1,
               d_lnw=1, d_lnb=1, g_gamma1=1, g_bdown=1, g_bo=1, g_gamma2=1,
               h_conv=2 * TAPS, h_cb=2, h_bin=2, h_bgate=2, h_lambda=2)
ROWS = dict(f_rb=EXPERTS, b_bv=P, g_bq=P, g_bup=2 * P, g_bg=EXPERTS)
CONSTS = dict(ident=P, center=P, mean=P, head_mean=P, kv_mean=KV_A * HD, head_sum=P,
              cos_a=SEQ, sin_a=SEQ, cos_ak=SEQ, sin_ak=SEQ, cos_b=SEQ, sin_b=SEQ,
              causal=3 * P, den=4 * STRIP)


def offsets(table):
    out, at = {}, 0
    for name, n in table.items():
        out[name] = (at, n)
        at += n
    return out, at


PER_TURN = dict(
    A_act_chain=24, A_centered=6, A_copied=6, A_dve_chain=33, A_loaded=16, A_rstd=6,
    A_squared=6, A_variance=6, C_act_chain=9, C_centered=4, C_copied=4, C_dve_chain=35,
    C_loaded=176, C_rstd=8, C_squared=8, C_stored=16, C_variance=8, a_exp=16, a_k_out=16,
    a_k_rest=2, a_k_round=2, a_kx=96, a_masked=16, a_q_out=16, a_q_part=3, a_qx=80,
    a_scores_t=16, a_sq=2, a_vx=4, a_weighed=8, b_exp=16, b_k_out=16, b_k_rest=2, b_k_round=2,
    b_kx=96, b_m_out=16, b_q_out=16, b_q_part=3, b_qx=80, b_row_max=16, b_scores=16,
    b_scores_t=16, b_shift=16, b_vx=4, b_weighed=8, d_stored=80, g1_experts=4, g1_gated=4,
    g1_mixed=4, g1_score=4, g1_score_odd=2, g1_value=4, g1_value_odd=2, h_conv=2, h_exps=2,
    h_gates=2, r_masked=8, r_read=4, r_ux=2, r_w=8)


def build(nc, x_in, weights, columns, rows, consts, out):
    W_AT, W_N = offsets(WEIGHTS)
    C_AT, C_N = offsets(COLUMNS)
    R_AT, R_N = offsets(ROWS)
    K_AT, K_N = offsets(CONSTS)
    ctx = ExitStack()

    def sb(name, shape, dt=F32):
        return ctx.enter_context(nc.sbuf_tensor(name, shape, dt))

    with ctx:
        w_sb = sb("w_sb", [P, W_N])
        col_sb = sb("col_sb", [P, C_N])
        row_sb = sb("row_sb", [P, R_N])
        const_sb = sb("const_sb", [P, K_N])

        def W(name, lo=0, hi=None, rows_=P):
            at, n = W_AT[name]
            return w_sb[0:rows_, at + lo:at + (n if hi is None else hi)]

        def C(name, i=0, rows_=P):
            return col_sb[0:rows_, C_AT[name][0] + i:C_AT[name][0] + i + 1]

        def R(name):
            at, n = R_AT[name]
            return row_sb[:, at:at + n]

        def K(name, rows_=P):
            at, n = K_AT[name]
            return const_sb[0:rows_, at:at + n]

        ident_b = sb("ident_b", [P, P], BF16)
        eps = sb("eps", [P, 4])
        EPS5, EPS6, ZERO = eps[:, 0:1], eps[:, 1:2], eps[:, 2:3]
        neg_bias = sb("neg_bias", [P, 4])
        decay = sb("decay", [P, 2])
        dec_t = sb("dec_t", [P, 8])

        QX = sb("QX", [P, HEADS, TOK], BF16)
        KX = sb("KX", [P, HEADS, TOK], BF16)
        PR = sb("PR", [P, 4, 2, TOK])
        VX = sb("VX", [P, TT, HEADS * STRIP])
        UX = sb("UX", [P, TT, DH * STRIP])
        q_parts = sb("q_parts", [P, PARTS, TOK], BF16)
        k_parts = sb("k_parts", [P, PARTS, TOK], BF16)
        neg_max = sb("neg_max", [P, TT, HEADS])
        max_parts = sb("max_parts", [P, TT, PARTS, HEADS], BF16)
        max_rest = sb("max_rest", [P, 2, TT, HEADS])
        max_rows = sb("max_rows", [PARTS * HEADS, TOK], BF16)

        x = sb("x", [P, TOK])
        x1 = sb("x1", [P, TOK])
        xc = sb("xc", [P, TOK])
        xn = sb("xn", [P, TOK])
        sq = sb("sq", [P, TOK])
        lnv = sb("lnv", [P, TOK])
        rstd = sb("rstd", [P, TOK])
        ta = sb("ta", [P, TOK])
        tb = sb("tb", [P, TOK])
        tc = sb("tc", [P, TOK])
        qf = sb("qf", [P, TOK])
        kf = sb("kf", [P, TOK])
        rq = sb("rq", [P, TOK])
        rk = sb("rk", [P, TOK])
        y = sb("y", [P, TOK])
        x_tok = sb("x_tok", [P, TT, P])
        small = sb("small", [P, 8, TT * EXPERTS])
        top8 = sb("top8", [P, TT, 8])
        stat = sb("stat", [P, 4, TT])
        v_sig = sb("v_sig", [P, TOK])
        beta_sb = sb("beta_sb", [DH, TOK])

        scan_k = sb("scan_k", [P, 2, DD, SEQ])
        scan_v = sb("scan_v", [P, 2, DD, SEQ])
        scan_b = sb("scan_b", [P, 2, SEQ])
        state = rq[:, :].rearrange("p (j v k) -> p j v k", j=2, v=DD)
        outer = tb[:, :].rearrange("p (j v k) -> p j v k", j=2, v=DD)
        s_k = sb("s_k", [P, 2, DD])

        arena = scan_k[:, :, :, :].rearrange("p a b c -> p (a b c)")
        arena2 = scan_v[:, :, :, :].rearrange("p a b c -> p (a b c)")
        KZ = arena[:, 0:DH * TOK].rearrange("p (h t) -> p h t", h=DH)
        prod = arena[:, DH * TOK:DH * TOK + EXPERTS * P].rearrange("p (e f) -> p e f", e=EXPERTS)
        HW = 2 * TOK

        def hawk_tile(i):
            return arena2[0:HH, i * HW:(i + 1) * HW].rearrange("p (a t) -> p a t", a=2)

        h_gelu, h_u, h_sig_in, h_sig_rec, h_alpha, h_beta = [hawk_tile(i) for i in range(6)]
        u_pad = arena[0:HH, 5120:5120 + 4 * (SEQ + TAPS - 1)].rearrange(
            "p (a b t) -> p a b t", a=2, b=G)
        u_rows = arena2[:, 6 * HW:6 * HW + TOK]
        q_rows = arena2[:, 6 * HW + TOK:6 * HW + 2 * TOK]
        o_rows = arena2[:, 7 * HW:7 * HW + TOK]

        ps = ctx.enter_context(nc.psum_tensor("ps", [P, 8, 512], F32))

        q_dram = nc.dram_tensor("q_dram", [SEQS, P, SEQ], F32).ap()
        k_dram = nc.dram_tensor("k_dram", [SEQS, P, SEQ], F32).ap()
        v_dram = nc.dram_tensor("v_dram", [SEQS, P, SEQ], F32).ap()
        b_dram = nc.dram_tensor("b_dram", [SEQS, DH, SEQ], F32).ap()
        x_dram = nc.dram_tensor("x_dram", [SEQS, P, SEQ], F32).ap()
        q_scratch = nc.dram_tensor("q_scratch", [PARTS, P, TOK], BF16).ap()
        k_scratch = nc.dram_tensor("k_scratch", [PARTS, P, TOK], BF16).ap()
        m_scratch = nc.dram_tensor("m_scratch", [PARTS * HEADS, TOK], BF16).ap()
        u_dram = nc.dram_tensor("u_dram", [SEQS, P, SEQ], F32).ap()

        sems = {}

        def sem(name):
            kind, signal = name.partition("_")[::2]
            if kind in ("f1", "f2", "g1", "g2"):
                name = kind[0] + "_" + signal
            if name not in sems:
                sems[name] = ctx.enter_context(nc.semaphore(name))
            return sems[name]

        turn = [0]

        def after(name, k=1):
            kind, signal = name.partition("_")[::2]
            if kind not in ("f1", "f2", "g1", "g2"):
                return sem(name), turn[0] * PER_TURN.get(name, 1) + k
            per = PER_TURN.get(kind[0] + "1_" + signal, 1)
            return sem(name), turn[0] * (2 * per) + ((per if kind[1] == "2" else 0) + k)

        def settle(eng):
            eng.nop(nofuse=True)

        chain = {}

        def link(eng, name, ins):
            chain[name] = chain.get(name, 0) + 1
            ins.then_inc(sem(name), 1)
            eng.wait_ge(*after(name, chain[name]))

        def pair(n):
            return 2 * (n % 3)

        def seq2(ap):
            return ap.rearrange("p (b t) -> p b t", b=G)

        def both(ap):
            return ap.unsqueeze(1).broadcast_to([ap.shape[0], G, SEQ])

        def heads_of(n):
            m = n % (PAIRS // G)
            i, half = m // 2, m % 2
            return [4 * (2 * half + j) + i for j in range(2)]


        def pe_norm(pe, ph, n, src, ready, centered=True):
            pe.wait_ge(*after(*ready))
            if centered:
                pe.matmul(ps[:, 6, :], K("center"), src, start=True, stop=True).then_inc(sem(ph + "centered"), 1)
            pe.wait_ge(*after(ph + "squared", n + 1))
            pe.matmul(ps[:, 7, :], K("mean"), sq[:, :], start=True, stop=True).then_inc(sem(ph + "variance"), 1)

        def act_norm(act, ph, n, nc_n, src=None, ready=None, e=None):
            if src is None:
                act.wait_ge(*after(ph + "copied", nc_n + 1))
                act.activation(sq[:, :], xc[:, :], ACT.Square).then_inc(sem(ph + "squared"), 1)
            else:
                act.wait_ge(*after(*ready))
                act.activation(sq[:, :], src, ACT.Square).then_inc(sem(ph + "squared"), 1)
            act.wait_ge(*after(ph + "variance", n + 1))
            link(act, ph + "act_chain", act.activation(lnv[:, :], ps[:, 7, :], ACT.Ln, bias=e))
            act.activation(rstd[:, :], lnv[:, :], ACT.Exp, scale=-0.5, bias=ZERO).then_inc(sem(ph + "rstd"), 1)

        def dve_norm(dve, ph, n, nc_n, dst, name, src=None, gamma=None, beta=None):
            if src is None:
                dve.wait_ge(*after(ph + "centered", nc_n + 1))
                dve.tensor_copy(xc[:, :], ps[:, 6, :]).then_inc(sem(ph + "copied"), 1)
                src = xc[:, :]
            dve.wait_ge(*after(ph + "rstd", n + 1))
            if gamma is None:
                dve.tensor_tensor(dst, src, rstd[:, :], ALU.mult).then_inc(sem(name), 1)
            elif beta is None:
                dve.scalar_tensor_tensor(dst, src, gamma, rstd[:, :], ALU.mult, ALU.mult).then_inc(sem(name), 1)
            else:
                link(dve, ph + "dve_chain", dve.tensor_tensor(xc[:, :], src, rstd[:, :], ALU.mult))
                dve.tensor_scalar(dst, xc[:, :], gamma, beta, ALU.mult, ALU.add).then_inc(sem(name), 1)


        def dve_split_q(dve, ph, L):
            c = ph + "dve_chain"
            ins = dve.tensor_copy(q_parts[:, 0, :], qf[:, :])
            ins.then_inc(sem(L + "q_part"), 1)
            dve.wait_ge(*after(L + "q_part", 1))
            link(dve, c, dve.tensor_tensor(ta[:, :], qf[:, :], q_parts[:, 0, :], ALU.subtract))
            dve.tensor_copy(q_parts[:, 1, :], ta[:, :]).then_inc(sem(L + "q_part"), 1)
            dve.wait_ge(*after(L + "q_part", 2))
            dve.tensor_tensor(q_parts[:, 2, :], ta[:, :], q_parts[:, 1, :], ALU.subtract).then_inc(sem(L + "q_part"), 1)

        def act_split_k(act, L, n=P):
            act.wait_ge(*after(L + "kf"))
            act.activation(k_parts[0:n, 0, :], kf[0:n, :], ACT.Copy).then_inc(sem(L + "k_round"), 1)
            act.wait_ge(*after(L + "k_rest", 1))
            act.activation(k_parts[0:n, 1, :], tc[0:n, :], ACT.Copy).then_inc(sem(L + "k_round"), 1)

        def pool_split_k(pool, L, n=P):
            pool.wait_ge(*after(L + "k_round", 1))
            pool.tensor_tensor(tc[0:n, :], kf[0:n, :], k_parts[0:n, 0, :], ALU.subtract).then_inc(sem(L + "k_rest"), 1)
            pool.wait_ge(*after(L + "k_round", 2))
            pool.tensor_tensor(k_parts[0:n, 2, :], tc[0:n, :], k_parts[0:n, 1, :], ALU.subtract).then_inc(sem(L + "k_rest"), 1)

        def sp_spread(sp, L, kv=HEADS):
            sp.wait_ge(*after(L + "k_rest", 2))
            k_of = k_scratch[:, 0:kv * HD, :]
            sp.dma_start(k_of.rearrange("c p t -> p c t"), k_parts[0:kv * HD, :, :]).then_inc(sem(L + "k_out"), 16)
            sp.wait_ge(*after(L + "q_part", PARTS))
            sp.dma_start(q_scratch.rearrange("c p t -> p c t"), q_parts[:, :, :]).then_inc(sem(L + "q_out"), 16)
            sp.wait_ge(*after(L + "k_out", 16))
            for band, part, n in K_BANDS:
                for i in range(n):
                    src = k_scratch[part + i, 0:kv * HD, :].rearrange("(d h) t -> d h t", d=HD)
                    lo = HD * (band + i)
                    sp.dma_start(KX[lo:lo + HD, 0:kv, :], src).then_inc(sem(L + "kx"), 16)
            sp.wait_ge(*after(L + "q_out", 16))
            for band, part, n in Q_BANDS:
                src = q_scratch[part:part + n].rearrange("c (d h) t -> (c d) h t", d=HD)
                sp.dma_start(QX[HD * band:HD * (band + n), :, :], src).then_inc(sem(L + "qx"), 16)

        def pe_scores(pe, L):
            for n in range(PAIRS):
                b = n // (PAIRS // G)
                if n == 0:
                    pe.wait_ge(*after(L + "kx", 16 * K_LOADS))
                    pe.wait_ge(*after(L + "qx", 16 * len(Q_BANDS)))
                if n >= 3:
                    pe.wait_ge(*after(L + "row_max", n - 2))
                for j, h in enumerate(heads_of(n)):
                    for t in range(2):
                        ins = pe.matmul(ps[:, pair(n) + j, t * SEQ:(t + 1) * SEQ],
                                        QX[0:SHIFT_ROW, h, b * SEQ + t * P:b * SEQ + (t + 1) * P],
                                        KX[0:SHIFT_ROW, h, b * SEQ:(b + 1) * SEQ], start=True, stop=True)
                ins.then_inc(sem(L + "scores"), 1)

        def dve_max(dve, ph, L):
            for n in range(PAIRS):
                b, h = n // (PAIRS // G), heads_of(n)[0]
                dve.wait_ge(*after(L + "scores", n + 1))
                dve.tensor_reduce(
                    neg_max[:, 2 * b:2 * b + 2, h:h + 5:4].rearrange("p t j -> p j t"),
                    ps[:, pair(n):pair(n) + 2, :].rearrange("p j (t k) -> p j t k", t=2),
                    AX_X, ALU.max, negate=True).then_inc(sem(L + "row_max"), 1)
            dve.wait_ge(*after(L + "row_max", PAIRS))
            c = ph + "dve_chain"
            link(dve, c, dve.tensor_copy(max_parts[:, :, 0, :], neg_max[:, :, :]))
            link(dve, c, dve.tensor_tensor(max_rest[:, 0], neg_max[:, :, :], max_parts[:, :, 0, :], ALU.subtract))
            link(dve, c, dve.tensor_copy(max_parts[:, :, 1, :], max_rest[:, 0]))
            dve.tensor_tensor(max_parts[:, :, 2, :], max_rest[:, 0], max_parts[:, :, 1, :], ALU.subtract).then_inc(sem(L + "max_parts"), 1)

        def pe_max_rows(pe, L):
            pe.wait_ge(*after(L + "max_parts"))
            settle(pe)
            psb = ps[0:PARTS * HEADS, 7, :].bitcast(BF16)
            for t in range(TT):
                ins = pe.transpose(psb[:, t * P:(t + 1) * P],
                                   max_parts[:, t, :, :].rearrange("p c h -> p (c h)"), ident_b[:, :])
            ins.then_inc(sem(L + "max_turned"), 1)

        def act_max_rows(act, L):
            act.wait_ge(*after(L + "max_turned"))
            act.activation(max_rows[:, :], ps[0:PARTS * HEADS, 7, :].bitcast(BF16)[:, 0:TOK], ACT.Copy).then_inc(sem(L + "max_rows"), 1)

        def sp_max_rows(sp, L):
            sp.wait_ge(*after(L + "max_rows"))
            sp.dma_start(m_scratch, max_rows[:, :]).then_inc(sem(L + "m_out"), 16)
            sp.wait_ge(*after(L + "m_out", 16))
            sp.dma_start(QX[SHIFT_ROW:SROWS, :, :], m_scratch.rearrange("(c h) t -> c h t", c=PARTS)).then_inc(sem(L + "shift"), 16)

        def pe_attend(pe, L, causal):
            for m in range(QUADS + 1):
                for n in (2 * m, 2 * m + 1) if m < QUADS else ():
                    b = n // (PAIRS // G)
                    if n == 0 and causal:
                        pe.wait_ge(*after(L + "kx", 16 * K_LOADS))
                        pe.wait_ge(*after(L + "qx", 16 * len(Q_BANDS)))
                        pe.wait_ge(*after(L + "rope_done"))
                    if n == 0 and not causal:
                        pe.wait_ge(*after(L + "shift", 16))
                    if n >= 3:
                        pe.wait_ge(*after(L + "exp", n - 2))
                    for j, h in enumerate(heads_of(n)):
                        for t in range(2):
                            lo = t * P if causal else 0
                            hk = h // (HEADS // KV_A) if causal else h
                            rows_ = SHIFT_ROW if causal else SROWS
                            ins = pe.matmul(ps[:, pair(n) + j, t * SEQ:(t + 1) * SEQ - lo],
                                            KX[0:rows_, hk, b * SEQ + t * P:b * SEQ + (t + 1) * P],
                                            QX[0:rows_, h, b * SEQ + lo:(b + 1) * SEQ], start=True, stop=True)
                    ins.then_inc(sem(L + "scores_t"), 1)
                if m == 0:
                    continue
                pe.wait_ge(*after(L + ("masked" if causal else "exp"), 2 * m))
                if m == 1:
                    pe.wait_ge(*after(L + "vx", 4))
                b = (m - 1) // (QUADS // G)
                i = (m - 1) % (QUADS // G)
                for bank in (6, 7):
                    for t in range(2):
                        lo = t * P if causal else 0
                        for g in range(4):
                            h, n = 4 * g + i, 2 * (m - 1) + g // 2
                            lhs = VX[:, 2 * b + t, h * STRIP:(h + 1) * STRIP] if bank == 6 else \
                                K("den")[:, i * STRIP:(i + 1) * STRIP]
                            ins = pe.matmul(ps[STRIP * g:STRIP * (g + 1), bank, b * SEQ + lo:(b + 1) * SEQ], lhs,
                                            PR[:, n % 4, g % 2, t * SEQ:(t + 1) * SEQ - lo],
                                            start=(i == 0 and t == 0), stop=(i == 3 and t == 1),
                                            skip_group_check=True)
                ins.then_inc(sem(L + "weighed"), 1)

        def act_attend(act, ph, L, causal):
            scale = float(HD) ** -0.5
            for n in range(PAIRS):
                act.wait_ge(*after(L + "scores_t", n + 1))
                if causal:
                    v = ps[:, pair(n):pair(n) + 2, 0:SEQ + P]
                    link(act, ph + "act_chain", act.activation(v, v, ACT.Tanh, scale=scale / CAP))
                if n >= 4:
                    act.wait_ge(*after(L + "weighed", (n - 4) // 2 + 1))
                if causal:
                    act.activation(PR[:, n % 4, :, 0:SEQ + P], v, ACT.Exp, scale=CAP, bias=ZERO).then_inc(sem(L + "exp"), 1)
                else:
                    act.activation(PR[:, n % 4, :, :], ps[:, pair(n):pair(n) + 2, :], ACT.Exp, scale=scale, bias=ZERO).then_inc(sem(L + "exp"), 1)

        def dve_attend(dve, ph, L):
            dve.wait_ge(*after(L + "weighed", QUADS))
            link(dve, ph + "dve_chain", dve.reciprocal(tb[:, :], ps[:, 7, :]))
            dve.tensor_tensor(y[:, :], ps[:, 6, :], tb[:, :], ALU.mult).then_inc(sem(L + "y"), 1)

        def dve_values(dve, L, bank, bias):
            dst = VX[:, :, :].rearrange("p t (g c) -> p t g c", g=4)
            for i in range(4):
                d = dst[:, :, :, 40 * i:40 * i + 8]
                if bias is None:
                    s = ps[:, bank, 0:TT * 32].rearrange("p (t g d) -> p t g d", t=TT, g=4)
                    dve.tensor_copy(d, s).then_inc(sem(L + "vx"), 1)
                else:
                    s = ps[:, bank, :].rearrange("p (t g i d) -> p t g i d", t=TT, g=4, i=4)[:, :, :, i, :]
                    r = bias.rearrange("p (g i d) -> p g i d", g=4, i=4)[:, :, i, :].unsqueeze(1)\
                        .broadcast_to([P, TT, 4, HD])
                    dve.tensor_tensor(d, s, r, ALU.add).then_inc(sem(L + "vx"), 1)

        def a_layer(e, eng, n):
            ph, L = "A_", "a_"
            if eng == "pe":
                pe_norm(e, ph, n, x[:, :], ("A_x",))
                e.wait_ge(*after(L + "xn"))
                e.matmul(ps[:, 0, :], W("a_q"), xn[:, :], start=True, stop=True)
                e.matmul(ps[:, 1, :], W("a_q2"), xn[:, :], start=True, stop=True).then_inc(sem(L + "q"), 1)
                e.matmul(ps[0:32, 2, :], W("a_k"), xn[:, :], start=True, stop=True)
                e.matmul(ps[0:32, 3, :], W("a_k2"), xn[:, :], start=True, stop=True).then_inc(sem(L + "k"), 1)
                for t in range(TT):
                    ins = e.matmul(ps[:, 4, t * 32:(t + 1) * 32], xn[:, t * P:(t + 1) * P], W("a_v"),
                                   start=True, stop=True)
                ins.then_inc(sem(L + "v"), 1)
                e.wait_ge(*after(L + "sq", 2))
                e.matmul(ps[:, 6, :], K("head_mean"), sq[:, :], start=True, stop=True)
                e.matmul(ps[0:32, 7, :], K("kv_mean", 32), tb[0:32, :], start=True, stop=True).then_inc(sem(L + "ms"), 1)
                pe_attend(e, L, True)
                e.wait_ge(*after(L + "y"))
                e.matmul(ps[:, 0, :], W("a_o"), y[:, :], start=True, stop=True).then_inc(sem(L + "o"), 1)
            if eng == "act":
                act_norm(e, ph, n, n, e=EPS5)
                e.wait_ge(*after(L + "q"))
                e.activation(sq[:, :], ps[:, 0, :], ACT.Square).then_inc(sem(L + "sq"), 1)
                e.wait_ge(*after(L + "k"))
                e.activation(tb[0:32, :], ps[0:32, 2, :], ACT.Square).then_inc(sem(L + "sq"), 1)
                e.wait_ge(*after(L + "ms"))
                e.activation(lnv[:, :], ps[:, 6, :], ACT.Ln, bias=EPS5)
                link(e, ph + "act_chain",
                     e.activation(rk[0:32, :], ps[0:32, 7, :], ACT.Ln, bias=eps[0:32, 0:1]))
                e.activation(rq[:, :], lnv[:, :], ACT.Exp, scale=-0.5, bias=ZERO)
                e.activation(rk[0:32, :], rk[0:32, :], ACT.Exp, scale=-0.5, bias=eps[0:32, 2:3]).then_inc(sem(L + "rms"), 1)
                act_split_k(e, L, 32)
                act_attend(e, ph, L, True)
                e.preload_act_table_set(LN_EXP_SET)
            if eng == "dve":
                c = ph + "dve_chain"
                dve_norm(e, ph, n, n, xn[:, :], L + "xn")
                e.wait_ge(*after(L + "sq", 2))
                k0, k1 = seq2(ps[0:32, 2, :]), seq2(ps[0:32, 3, :])
                e.tensor_tensor(seq2(kf[0:32, :]), k0, both(K("cos_ak", 32)), ALU.mult)
                link(e, c, e.tensor_tensor(seq2(ta[0:32, :]), k1, both(K("sin_ak", 32)), ALU.mult))
                link(e, c, e.tensor_tensor(kf[0:32, :], kf[0:32, :], ta[0:32, :], ALU.add))
                e.wait_ge(*after(L + "rms"))
                e.tensor_tensor(kf[0:32, :], kf[0:32, :], rk[0:32, :], ALU.mult).then_inc(sem(L + "kf"), 1)
                e.tensor_tensor(seq2(qf[:, :]), seq2(ps[:, 0, :]), both(K("cos_a")), ALU.mult)
                link(e, c, e.tensor_tensor(seq2(xc[:, :]), seq2(ps[:, 1, :]), both(K("sin_a")), ALU.mult))
                link(e, c, e.tensor_tensor(qf[:, :], qf[:, :], xc[:, :], ALU.add))
                link(e, c, e.tensor_tensor(qf[:, :], qf[:, :], rq[:, :], ALU.mult))
                dve_split_q(e, ph, L)
                e.wait_ge(*after(L + "v"))
                dst = VX[:, :, :].rearrange("p t (g c) -> p t g c", g=4)
                for i in range(4):
                    s = ps[:, 4, 0:TT * 32].rearrange("p (t g d) -> p t g d", t=TT, g=4)
                    ins = e.tensor_copy(dst[:, :, :, 40 * i:40 * i + 8], s)
                    ins.then_inc(sem(L + "vx"), 1)
                e.tensor_copy(stat[:, 3, :], stat[:, 2, :]).then_inc(sem(L + "rope_done"), 1)
                dve_attend(e, ph, L)
                e.wait_ge(*after(L + "o"))
                e.tensor_tensor(x[:, :], x[:, :], ps[:, 0, :], ALU.add).then_inc(sem(L + "x"), 1)
            if eng == "pool":
                pool_split_k(e, L, 32)
                tri = K("causal")[:, 0:P].unsqueeze(1).unsqueeze(1).broadcast_to([P, 2, 2, P])
                for n_ in range(PAIRS):
                    e.wait_ge(*after(L + "exp", n_ + 1))
                    v = PR[:, n_ % 4, :, :].rearrange("p j (t k) -> p j t k", t=2)[:, :, :, 0:P]
                    e.tensor_tensor(v, v, tri, ALU.mult).then_inc(sem(L + "masked"), 1)
            if eng == "sp":
                sp_spread(e, L, KV_A)

        def f_layer(e, eng, L, n, ready):
            ph = "A_"
            if eng == "pe":
                pe_norm(e, ph, n, x[:, :], ready)
                e.wait_ge(*after(L + "xn"))
                for t in range(TT):
                    ins = e.matmul(ps[:, 0, t * EXPERTS:(t + 1) * EXPERTS], xn[:, t * P:(t + 1) * P], W("f_r"),
                                   start=True, stop=True)
                ins.then_inc(sem(L + "logits"), 1)
                e.matmul(ps[:, 1, :], W("f_base"), xn[:, :], start=True, stop=False)
                e.matmul(ps[:, 2, :], W("f_A"), xn[:, :], start=True, stop=True).then_inc(sem(L + "ax"), 1)
                e.wait_ge(*after(L + "spread"))
                for t in range(TT):
                    ins = e.transpose(ps[:, 3, t * P:(t + 1) * P], y[:, t * P:(t + 1) * P], K("ident"))
                ins.then_inc(sem(L + "weights_t"), 1)
                e.wait_ge(*after(L + "axw"))
                e.matmul(ps[:, 1, :], W("f_B"), tb[:, :], start=False, stop=True).then_inc(sem(L + "o"), 1)
            if eng == "act":
                act_norm(e, ph, n, n, e=EPS5)
                e.wait_ge(*after(L + "ax"))
                e.activation(ta[:, :], ps[:, 2, :], ACT.Copy).then_inc(sem(L + "axs"), 1)
                e.wait_ge(*after(L + "e0"))
                e.activation(small[:, 2, :], small[:, 1, :], ACT.Exp, bias=ZERO).then_inc(sem(L + "e1"), 1)
            if eng == "dve":
                c = ph + "dve_chain"
                dve_norm(e, ph, n, n, xn[:, :], L + "xn")
                e.wait_ge(*after(L + "logits"))
                lg = small[:, 0, :].rearrange("p (t e) -> p t e", t=TT)

                def by_token(ap):
                    return ap.unsqueeze(2).broadcast_to([P, TT, EXPERTS])

                def tile(i):
                    return small[:, i, :].rearrange("p (t e) -> p t e", t=TT)

                link(e, c, e.tensor_tensor(lg, ps[:, 0, 0:TT * EXPERTS].rearrange("p (t e) -> p t e", t=TT),
                                           R("f_rb").unsqueeze(1).broadcast_to([P, TT, EXPERTS]), ALU.add))
                e.tensor_reduce(stat[:, 0, :], lg, AX_X, ALU.max)
                for t in range(TT):
                    ins = e.max(top8[:, t, :], small[:, 0, t * EXPERTS:(t + 1) * EXPERTS])
                link(e, c, ins)
                e.tensor_tensor(tile(1), lg, by_token(stat[:, 0, :]), ALU.subtract).then_inc(sem(L + "e0"), 1)
                e.tensor_tensor(tile(3), lg, top8[:, :, 1:2].broadcast_to([P, TT, EXPERTS]), ALU.is_ge)
                e.wait_ge(*after(L + "e1"))
                link(e, c, e.tensor_copy(small[:, 5, :], small[:, 2, :]))
                link(e, c, e.tensor_tensor(tile(4), tile(5), tile(3), ALU.mult))
                link(e, c, e.tensor_reduce(stat[:, 1, :], tile(4), AX_X, ALU.add))
                link(e, c, e.reciprocal(stat[:, 2, :], stat[:, 1, :]))
                link(e, c, e.scalar_tensor_tensor(tile(6), tile(4), 2.0, by_token(stat[:, 2, :]),
                                                  ALU.mult, ALU.mult))
                e.tensor_copy(y[:, :].rearrange("p (a r) -> p a r", r=RANK),
                                   small[:, 6, :].unsqueeze(2).broadcast_to([P, TT * EXPERTS, RANK])).then_inc(sem(L + "spread"), 1)
                e.wait_ge(*after(L + "axs"))
                e.wait_ge(*after(L + "weights_t"))
                e.tensor_tensor(tb[:, :], ps[:, 3, :], ta[:, :], ALU.mult).then_inc(sem(L + "axw"), 1)
                e.wait_ge(*after(L + "o"))
                e.scalar_tensor_tensor(x[:, :], ps[:, 1, :], C("f_bb"), x[:, :], ALU.add, ALU.add).then_inc(sem(L + "x"), 1)

        def b_layer(e, eng, n, ready):
            ph, L = "A_", "b_"
            if eng == "pe":
                pe_norm(e, ph, n, x[:, :], ready)
                pe_norm(e, ph, n + 1, x1[:, :], (L + "x1",))
                e.wait_ge(*after(L + "xn"))
                e.matmul(ps[:, 0, :], W("b_q"), xn[:, :], start=True, stop=True)
                e.matmul(ps[:, 1, :], W("b_q2"), xn[:, :], start=True, stop=True).then_inc(sem(L + "q"), 1)
                e.matmul(ps[:, 2, :], W("b_k"), xn[:, :], start=True, stop=True)
                e.matmul(ps[:, 3, :], W("b_k2"), xn[:, :], start=True, stop=True).then_inc(sem(L + "k"), 1)
                for t in range(TT):
                    ins = e.matmul(ps[:, 4, t * P:(t + 1) * P], xn[:, t * P:(t + 1) * P], W("b_v"),
                                   start=True, stop=True)
                ins.then_inc(sem(L + "v"), 1)
                e.wait_ge(*after(L + "vx", 4))
                pe_scores(e, L)
                pe_max_rows(e, L)
                pe_attend(e, L, False)
                e.wait_ge(*after(L + "y"))
                e.matmul(ps[:, 0, :], W("b_o"), y[:, :], start=True, stop=True).then_inc(sem(L + "o"), 1)
            if eng == "act":
                act_norm(e, ph, n, n, e=EPS5)
                act_norm(e, ph, n + 1, n + 1, e=EPS5)
                act_split_k(e, L)
                act_max_rows(e, L)
                act_attend(e, ph, L, False)
            if eng == "dve":
                c = ph + "dve_chain"
                dve_norm(e, ph, n, n, x1[:, :], L + "x1")
                dve_norm(e, ph, n + 1, n + 1, xn[:, :], L + "xn", gamma=C("b_gamma"), beta=C("b_beta"))
                e.wait_ge(*after(L + "k"))
                e.scalar_tensor_tensor(seq2(ta[:, :]), seq2(ps[:, 2, :]), C("b_bk"), both(K("cos_b")), ALU.add, ALU.mult)
                link(e, c, e.scalar_tensor_tensor(seq2(tb[:, :]), seq2(ps[:, 3, :]), C("b_bk2"), both(K("sin_b")),
                                                  ALU.add, ALU.mult))
                e.tensor_tensor(kf[:, :], ta[:, :], tb[:, :], ALU.add).then_inc(sem(L + "kf"), 1)
                e.scalar_tensor_tensor(seq2(xc[:, :]), seq2(ps[:, 0, :]), C("b_bq"), both(K("cos_b")), ALU.add, ALU.mult)
                link(e, c, e.scalar_tensor_tensor(seq2(y[:, :]), seq2(ps[:, 1, :]), C("b_bq2"), both(K("sin_b")),
                                                  ALU.add, ALU.mult))
                link(e, c, e.tensor_tensor(qf[:, :], xc[:, :], y[:, :], ALU.add))
                dve_split_q(e, ph, L)
                e.wait_ge(*after(L + "v"))
                dve_values(e, L, 4, R("b_bv"))
                dve_max(e, ph, L)
                dve_attend(e, ph, L)
                e.wait_ge(*after(L + "o"))
                link(e, c, e.scalar_tensor_tensor(ta[:, :], ps[:, 0, :], C("b_bo"), x1[:, :], ALU.add, ALU.add))
                e.tensor_tensor(x[:, :], x[:, :], ta[:, :], ALU.add).then_inc(sem(L + "x"), 1)
            if eng == "pool":
                pool_split_k(e, L)
            if eng == "sp":
                sp_spread(e, L)
                sp_max_rows(e, L)

        def d_layer(e, eng, n, ready):
            ph, L = "A_", "d_"
            if eng == "pe":
                pe_norm(e, ph, n, x[:, :], ready)
                e.wait_ge(*after(L + "xn"))
                e.matmul(ps[:, 1, :], W("d_k"), xn[:, :], start=True, stop=True)
                e.matmul(ps[:, 2, :], W("d_v"), xn[:, :], start=True, stop=True)
                e.matmul(ps[0:DH, 3, :], W("d_b"), xn[:, :], start=True, stop=True).then_inc(sem(L + "kvb"), 1)
                e.matmul(ps[:, 0, :], W("d_q"), xn[:, :], start=True, stop=True).then_inc(sem(L + "q"), 1)
                e.wait_ge(*after(L + "sq"))
                e.matmul(ps[:, 6, :], K("head_sum"), sq[:, :], start=True, stop=True).then_inc(sem(L + "norm2"), 1)
                e.wait_ge(*after(L + "stored", 80))
                settle(e)
            if eng == "act":
                act_norm(e, ph, n, n, e=EPS5)
                e.wait_ge(*after(L + "kvb"))
                e.activation(sq[:, :], ps[:, 1, :], ACT.Square).then_inc(sem(L + "sq"), 1)
                e.activation(ta[:, :], ps[:, 2, :], ACT.Exp, scale=-1.0, bias=ZERO)
                e.activation(beta_sb[:, :], ps[0:DH, 3, :], ACT.Exp, scale=-1.0, bias=eps[0:DH, 2:3]).then_inc(sem(L + "e"), 1)
                e.wait_ge(*after(L + "q"))
                e.activation(y[:, :], ps[:, 0, :], ACT.Copy).then_inc(sem(L + "qs"), 1)
                e.wait_ge(*after(L + "norm2c"))
                link(e, ph + "act_chain", e.activation(lnv[:, :], xc[:, :], ACT.Ln, bias=ZERO))
                e.activation(rk[:, :], lnv[:, :], ACT.Exp, scale=-0.5, bias=ZERO).then_inc(sem(L + "rk"), 1)
            if eng == "dve":
                c = ph + "dve_chain"
                dve_norm(e, ph, n, n, xn[:, :], L + "xn")
                e.wait_ge(*after(L + "e"))
                e.tensor_scalar(ta[:, :], ta[:, :], 1.0, None, ALU.add)
                link(e, c, e.tensor_scalar(beta_sb[:, :], beta_sb[:, :], 1.0, None, ALU.add))
                e.reciprocal(tb[:, :], ta[:, :])
                link(e, c, e.reciprocal(beta_sb[:, :], beta_sb[:, :]))
                e.tensor_tensor(v_sig[:, :], ps[:, 2, :], tb[:, :], ALU.mult)
                e.wait_ge(*after(L + "norm2"))
                e.tensor_scalar(xc[:, :], ps[:, 6, :], 1e-24, None, ALU.max).then_inc(sem(L + "norm2c"), 1)
                e.wait_ge(*after(L + "rk"))
                e.tensor_tensor(kf[:, :], ps[:, 1, :], rk[:, :], ALU.mult).then_inc(sem(L + "kvn"), 1)
            if eng == "sp":
                it = turn[0]

                def to(dram):
                    return dram.rearrange("(i b) p t -> i p b t", b=G)[it]

                e.wait_ge(*after(L + "qs"))
                settle(e)
                e.dma_start(to(q_dram), seq2(y[:, :])).then_inc(sem(L + "stored"), 16)
                e.wait_ge(*after(L + "kvn"))
                settle(e)
                e.dma_start(to(k_dram), seq2(kf[:, :])).then_inc(sem(L + "stored"), 16)
                e.dma_start(to(v_dram), seq2(v_sig[:, :])).then_inc(sem(L + "stored"), 16)
                e.dma_start(to(b_dram), seq2(beta_sb[:, :])).then_inc(sem(L + "stored"), 16)
                e.dma_start(to(x_dram), seq2(x[:, :])).then_inc(sem(L + "stored"), 16)
                e.wait_ge(*after(L + "stored", 80))
                settle(e)

        def r_layer(e, eng):
            ph, L = "C_", "r_"
            quads = G * 2

            def heads(n):
                m = n % 4
                i, half = m // 2, m % 2
                return [2 * (2 * half + j) + i for j in range(2)]

            if eng == "pe":
                e.wait_ge(*after("C_loaded", 16 * (3 + DH)))
                for t in range(TT):
                    ins = e.transpose(ps[:, 7, t * P:(t + 1) * P], u_rows[:, t * P:(t + 1) * P], K("ident"))
                ins.then_inc(sem(L + "u_t"), 1)
                for m in range(quads + 1):
                    for n in (2 * m, 2 * m + 1) if m < quads else ():
                        b = n // 4
                        if n >= 3:
                            e.wait_ge(*after(L + "masked", n - 2))
                        for j, h in enumerate(heads(n)):
                            for t in range(2):
                                ins = e.matmul(ps[:, pair(n) + j, t * SEQ:(t + 1) * SEQ - t * P],
                                               KZ[:, h, b * SEQ + t * P:b * SEQ + (t + 1) * P],
                                               q_rows[:, b * SEQ + t * P:(b + 1) * SEQ], start=True, stop=True)
                        ins.then_inc(sem(L + "w"), 1)
                    if m == 0:
                        continue
                    e.wait_ge(*after(L + "masked", 2 * m))
                    if m == 1:
                        e.wait_ge(*after(L + "ux", 2))
                    b, i = (m - 1) // 2, (m - 1) % 2
                    for t in range(2):
                        for g in range(4):
                            h, n = 2 * g + i, 2 * (m - 1) + g // 2
                            ins = e.matmul(ps[STRIP * g:STRIP * (g + 1), 6, b * SEQ + t * P:(b + 1) * SEQ],
                                           UX[:, 2 * b + t, h * STRIP:(h + 1) * STRIP],
                                           PR[:, n % 4, g % 2, t * SEQ:(t + 1) * SEQ - t * P],
                                           start=(i == 0 and t == 0), stop=(i == 1 and t == 1),
                                           skip_group_check=True)
                    ins.then_inc(sem(L + "read"), 1)
                pe_norm(e, ph, 0, o_rows, (L + "o",))
            if eng == "act":
                e.wait_ge(*after(L + "read", quads))
                e.activation(o_rows, ps[:, 6, :], ACT.Copy).then_inc(sem(L + "o"), 1)
                act_norm(e, ph, 0, 0, e=EPS5)
            if eng == "dve":
                c = ph + "dve_chain"
                e.wait_ge(*after(L + "u_t"))
                dst = UX[:, :, :].rearrange("p t (g c) -> p t g c", g=4)
                for i in range(2):
                    s = ps[:, 7, :].rearrange("p (t g i d) -> p t g i d", t=TT, g=4, i=2)[:, :, :, i, :]
                    e.tensor_copy(dst[:, :, :, 48 * i:48 * i + DD], s).then_inc(sem(L + "ux"), 1)
                for n in range(2 * quads):
                    e.wait_ge(*after(L + "w", n + 1))
                    if n >= 4:
                        e.wait_ge(*after(L + "read", (n - 4) // 2 + 1))
                    e.tensor_tensor(PR[:, n % 4, :, 0:3 * P], ps[:, pair(n):pair(n) + 2, 0:3 * P],
                                         K("causal").unsqueeze(1).broadcast_to([P, 2, 3 * P]), ALU.mult).then_inc(sem(L + "masked"), 1)
                dve_norm(e, ph, 0, 0, ta[:, :], L + "on", gamma=C("d_lnw"), beta=C("d_lnb"))
                e.wait_ge(*after(L + "on"))
                e.wait_ge(*after("C_loaded", 16 * (3 + DH)))
                e.tensor_tensor(x[:, :], x1[:, :], ta[:, :], ALU.add).then_inc(sem(L + "x"), 1)

        def g_layer(e, eng, L, n, nc_n, ready):
            ph = "C_"
            q_tok = qf[:, :].rearrange("p (t h d) -> p t h d", t=TT, h=HEADS)
            kv_tok = VX[:, 0:2, :].rearrange("p a (b g c) -> p (a b) g c", b=2, g=HEADS)
            scores = VX[:, 2:4, :].rearrange("p a (b h g) -> p (a b) h g", b=2, h=HEADS)
            products = [PR[:, 2 * i:2 * i + 2, :, :].rearrange("p a b c -> p (a b c)") for i in range(2)]

            def score_products(eng_, t):
                return eng_.tensor_tensor(
                    products[t % 2].rearrange("p (h g d) -> p h g d", h=HEADS, g=HEADS),
                    q_tok[:, t].unsqueeze(2).broadcast_to([P, HEADS, HEADS, HD]),
                    kv_tok[:, t, :, 0:HD].unsqueeze(1).broadcast_to([P, HEADS, HEADS, HD]), ALU.mult)

            def value_products(eng_, t):
                return eng_.tensor_tensor(
                    products[t % 2].rearrange("p (h d g) -> p h d g", h=HEADS, d=HD),
                    scores[:, t].unsqueeze(2).broadcast_to([P, HEADS, HD, HEADS]),
                    kv_tok[:, t, :, HD:2 * HD].rearrange("p g d -> p d g").unsqueeze(1)
                    .broadcast_to([P, HEADS, HD, HEADS]), ALU.mult)

            if eng == "pe":
                pe_norm(e, ph, n, x[:, :], ready)
                pe_norm(e, ph, n + 1, None, (L + "x1",), centered=False)
                e.wait_ge(*after(L + "xn"))
                e.matmul(ps[0:LATENT, 1, :], W("g_down"), xn[:, :], start=True, stop=True)
                for t in range(TT):
                    ins = e.matmul(ps[:, 0, t * P:(t + 1) * P], xn[:, t * P:(t + 1) * P], W("g_q"),
                                   start=True, stop=True)
                ins.then_inc(sem(L + "qd"), 1)
                e.wait_ge(*after(L + "down"))
                for t in range(TT):
                    ins = e.matmul(ps[:, 2 + t // 2, t % 2 * SEQ:(t % 2 + 1) * SEQ], tc[0:LATENT, t * P:(t + 1) * P],
                                   W("g_up", rows_=LATENT), start=True, stop=True)
                ins.then_inc(sem(L + "kv"), 1)
                e.wait_ge(*after(L + "heads"))
                for t in range(TT):
                    ins = e.transpose(ps[:, 4, t * P:(t + 1) * P], y[:, t * P:(t + 1) * P], K("ident"))
                ins.then_inc(sem(L + "heads_t"), 1)
                e.wait_ge(*after(L + "y"))
                e.matmul(ps[:, 5, :], W("g_o"), ta[:, :], start=True, stop=True).then_inc(sem(L + "o"), 1)
                pe_norm(e, ph, n + 2, None, (L + "x2",), centered=False)
                e.wait_ge(*after(L + "xm"))
                for t in range(TT):
                    ins = e.matmul(ps[:, 6, t * EXPERTS:(t + 1) * EXPERTS], xn[:, t * P:(t + 1) * P], W("g_g"),
                                   start=True, stop=True)
                ins.then_inc(sem(L + "logits"), 1)
                for t in range(TT):
                    if t == 3:
                        e.wait_ge(*after(L + "gated", 1))
                    for c in range(2):
                        ins = e.matmul(ps[:, pair(t) + c, :], xn[:, t * P:(t + 1) * P],
                                       W("g_e", c * 512, (c + 1) * 512), start=True, stop=True)
                    ins.then_inc(sem(L + "experts"), 1)
                e.wait_ge(*after(L + "mixed", TT))
                for t in range(TT):
                    ins = e.transpose(ps[:, 6, t * P:(t + 1) * P], y[:, t * P:(t + 1) * P], K("ident"))
                ins.then_inc(sem(L + "mixed_t"), 1)
            if eng == "act":
                act_norm(e, ph, n, nc_n, e=EPS5)
                act_norm(e, ph, n + 1, None, src=x1[:, :], ready=(L + "x1",), e=EPS6)
                e.wait_ge(*after(L + "qd"))
                e.activation(tc[0:LATENT, :], ps[0:LATENT, 1, :], ACT.Identity, bias=C("g_bdown", rows_=LATENT)).then_inc(sem(L + "down"), 1)
                e.wait_ge(*after(L + "shifted"))
                e.activation(scores, scores, ACT.Exp, scale=float(HD) ** -0.5, bias=ZERO).then_inc(sem(L + "exp"), 1)
                e.wait_ge(*after(L + "heads_t"))
                e.activation(ta[:, :], ps[:, 4, :], ACT.Copy).then_inc(sem(L + "y"), 1)
                act_norm(e, ph, n + 2, None, src=x1[:, :], ready=(L + "x2",), e=EPS6)
                e.wait_ge(*after(L + "e0"))
                e.activation(small[:, 2, :], small[:, 1, :], ACT.Exp, bias=ZERO).then_inc(sem(L + "e1"), 1)
            if eng == "dve":
                c = ph + "dve_chain"
                dve_norm(e, ph, n, nc_n, x1[:, :], L + "x1")
                e.wait_ge(*after(L + "x1"))
                dve_norm(e, ph, n + 1, None, xn[:, :], L + "xn", src=x1[:, :], gamma=C("g_gamma1"))
                e.wait_ge(*after(L + "qd"))
                e.tensor_tensor(qf[:, :].rearrange("p (t c) -> p t c", t=TT),
                                ps[:, 0, :].rearrange("p (t c) -> p t c", t=TT),
                                R("g_bq").unsqueeze(1).broadcast_to([P, TT, P]), ALU.add)
                e.wait_ge(*after(L + "kv"))
                e.tensor_tensor(VX[:, 0:2, :].rearrange("p a (b c) -> p (a b) c", b=2),
                                     ps[:, 2:4, :].rearrange("p a (b c) -> p (a b) c", b=2),
                                     R("g_bup").unsqueeze(1).broadcast_to([P, TT, 2 * P]), ALU.add).then_inc(sem(L + "qkv"), 1)
                e.wait_ge(*after(L + "qkv"))

                def sums(t, products_of, out_, sig):
                    if t % 2 == 0:
                        if t:
                            e.wait_ge(*after(sig, t - 1))
                        link(e, c, products_of(e, t))
                    else:
                        e.wait_ge(*after(sig + "_odd", (t + 1) // 2))
                    e.tensor_reduce(out_, products[t % 2].rearrange("p (a b) -> p a b", a=out_.shape[1]),
                                         AX_X, ALU.add).then_inc(sem(sig), 1)

                for t in range(TT):
                    sums(t, score_products, scores[:, t].rearrange("p h g -> p (h g)"), L + "score")
                e.wait_ge(*after(L + "score", TT))
                all_heads = scores.rearrange("p t h g -> p (t h) g")
                link(e, c, e.tensor_reduce(small[:, 4:6, :].rearrange("p a b -> p (a b)"), all_heads, AX_X, ALU.max))
                e.tensor_tensor(all_heads, all_heads,
                                     small[:, 4:6, :].rearrange("p a b -> p (a b)").unsqueeze(2)
                                     .broadcast_to([P, TT * HEADS, HEADS]), ALU.subtract).then_inc(sem(L + "shifted"), 1)
                e.wait_ge(*after(L + "exp"))
                link(e, c, e.tensor_reduce(small[:, 6:8, :].rearrange("p a b -> p (a b)"), all_heads, AX_X, ALU.add))
                link(e, c, e.reciprocal(small[:, 4:6, :], small[:, 6:8, :]))
                for t in range(TT):
                    sums(t, value_products, y[:, t * P:(t + 1) * P], L + "value")
                e.wait_ge(*after(L + "value", TT))
                heads = y[:, :].rearrange("p (a d) -> p a d", d=HD)
                e.tensor_tensor(heads, heads, small[:, 4:6, :].rearrange("p a b -> p (a b)").unsqueeze(2)
                                     .broadcast_to([P, TT * HEADS, HD]), ALU.mult).then_inc(sem(L + "heads"), 1)
                e.wait_ge(*after(L + "o"))
                e.scalar_tensor_tensor(x1[:, :], ps[:, 5, :], C("g_bo"), x1[:, :], ALU.add, ALU.add).then_inc(sem(L + "x2"), 1)
                e.wait_ge(*after(L + "x2"))
                dve_norm(e, ph, n + 2, None, xn[:, :], L + "xm", src=x1[:, :], gamma=C("g_gamma2"))
                e.tensor_tensor(x[:, :], x[:, :], x1[:, :], ALU.add)
                e.wait_ge(*after(L + "logits"))

                def by_token(ap):
                    return ap.unsqueeze(2).broadcast_to([P, TT, EXPERTS])

                def tile(i):
                    return small[:, i, :].rearrange("p (t e) -> p t e", t=TT)

                link(e, c, e.tensor_tensor(tile(0), ps[:, 6, 0:TT * EXPERTS].rearrange("p (t e) -> p t e", t=TT),
                                           R("g_bg").unsqueeze(1).broadcast_to([P, TT, EXPERTS]), ALU.add))
                link(e, c, e.tensor_reduce(stat[:, 0, :], tile(0), AX_X, ALU.max))
                e.tensor_tensor(tile(1), tile(0), by_token(stat[:, 0, :]), ALU.subtract).then_inc(sem(L + "e0"), 1)
                e.wait_ge(*after(L + "e1"))
                link(e, c, e.tensor_reduce(stat[:, 1, :], tile(2), AX_X, ALU.add))
                link(e, c, e.reciprocal(stat[:, 2, :], stat[:, 1, :]))
                link(e, c, e.tensor_tensor(tile(3), tile(2), by_token(stat[:, 2, :]), ALU.mult))
                for t in range(TT):
                    e.wait_ge(*after(L + "experts", t + 1))
                    if t:
                        e.wait_ge(*after(L + "mixed", t))
                    ins = e.tensor_tensor(prod, ps[:, pair(t):pair(t) + 2, :].rearrange("p c (e f) -> p (c e) f", e=4),
                                          tile(3)[:, t, :].unsqueeze(2).broadcast_to([P, EXPERTS, P]), ALU.mult)
                    ins.then_inc(sem(L + "gated"), 1)
                    e.wait_ge(*after(L + "gated", t + 1))
                    e.tensor_reduce(y[:, t * P:(t + 1) * P], prod.rearrange("p e f -> p f e"), AX_X, ALU.add).then_inc(sem(L + "mixed"), 1)
                e.wait_ge(*after(L + "mixed_t"))
                e.tensor_tensor(x[:, :], x[:, :], ps[:, 6, :], ALU.add).then_inc(sem(L + "x"), 1)
            if eng == "pool":
                for t in (1, 3):
                    e.wait_ge(*after(L + "qkv" if t == 1 else L + "score", 1 if t == 1 else 2))
                    score_products(e, t).then_inc(sem(L + "score_odd"), 1)
                for t in (1, 3):
                    e.wait_ge(*after(L + "exp" if t == 1 else L + "value", 1 if t == 1 else 2))
                    value_products(e, t).then_inc(sem(L + "value_odd"), 1)

        def h_layer(e, eng, n, nc_n, ready):
            ph, L = "C_", "h_"
            if eng == "pe":
                pe_norm(e, ph, n, x[:, :], ready)
                e.wait_ge(*after(L + "xn"))
                for i in range(4):
                    ins = e.matmul(ps[0:HH, i, :], W("h_proj", i * HH, (i + 1) * HH), xn[:, :], start=True, stop=True)
                ins.then_inc(sem(L + "proj"), 1)
                e.wait_ge(*after(L + "conv", 2))
                e.wait_ge(*after(L + "gelu"))
                for name, bank in (("h_gate", 2), ("h_in", 0)):
                    for o in range(2):
                        for k in range(2):
                            ins = e.matmul(ps[0:HH, bank + o, :],
                                           W(name, k * HID + o * HH, k * HID + (o + 1) * HH, HH), h_u[:, k, :],
                                           start=(k == 0), stop=(k == 1))
                    ins.then_inc(sem(L + "gates"), 1)
                e.wait_ge(*after(L + "m"))
                for k in range(2):
                    ins = e.matmul(ps[:, 6, :], W("h_out", k * P, (k + 1) * P, HH), h_gelu[:, k, :],
                                   start=(k == 0), stop=(k == 1))
                ins.then_inc(sem(L + "o"), 1)
            if eng == "act":
                act_norm(e, ph, n, nc_n, e=EPS5)
                e.wait_ge(*after(L + "proj"))
                e.activation(u_pad[:, :, :, TAPS - 1:], ps[0:HH, 2:4, :].rearrange("p a (b t) -> p a b t", b=G),
                                  ACT.Copy).then_inc(sem(L + "pad"), 1)
                e.activation(h_gelu, ps[0:HH, 0:2, :], ACT.Gelu).then_inc(sem(L + "gelu"), 1)
                e.preload_act_table_set(LN_EXP_SET)
                e.wait_ge(*after(L + "gates", 1))
                for o in range(2):
                    ins = e.activation(h_sig_rec[:, o, :], ps[0:HH, 2 + o, :], ACT.Exp, scale=-1.0,
                                       bias=neg_bias[0:HH, 2 + o:3 + o])
                ins.then_inc(sem(L + "exps"), 1)
                e.wait_ge(*after(L + "gates", 2))
                for o in range(2):
                    ins = e.activation(h_sig_in[:, o, :], ps[0:HH, o, :], ACT.Exp, scale=-1.0,
                                       bias=neg_bias[0:HH, o:o + 1])
                ins.then_inc(sem(L + "exps"), 1)
                e.wait_ge(*after(L + "sig_rec"))
                for o in range(2):
                    ins = e.activation(h_alpha[:, o, :], h_sig_rec[:, o, :], ACT.Exp, scale=decay[0:HH, o:o + 1],
                                       bias=eps[0:HH, 2:3])
                ins.then_inc(sem(L + "alpha"), 1)
                e.wait_ge(*after(L + "one_less"))
                link(e, ph + "act_chain", e.activation(h_beta, h_beta, ACT.Ln, bias=eps[0:HH, 1:2]))
                e.activation(h_beta, h_beta, ACT.Exp, scale=0.5, bias=eps[0:HH, 2:3]).then_inc(sem(L + "beta"), 1)
            if eng == "dve":
                c = ph + "dve_chain"
                dve_norm(e, ph, n, nc_n, xn[:, :], L + "xn")
                e.wait_ge(*after(L + "pad"))
                for k in range(TAPS):
                    for o in range(2):
                        src, dst = u_pad[:, o, :, k:k + SEQ], seq2(h_u[:, o, :])
                        tap = C("h_conv", o * TAPS + k, HH)
                        if k == 0:
                            ins = e.tensor_scalar(dst, src, tap, C("h_cb", o, HH), ALU.mult, ALU.add)
                        else:
                            ins = e.scalar_tensor_tensor(dst, src, tap, dst, ALU.mult, ALU.add)
                        if k == TAPS - 1:
                            ins.then_inc(sem(L + "conv"), 1)
                    if k < TAPS - 1:
                        link(e, c, ins)
                e.wait_ge(*after(L + "exps", 1))
                link(e, c, e.tensor_scalar(h_sig_rec, h_sig_rec, 1.0, None, ALU.add))
                e.reciprocal(h_sig_rec, h_sig_rec).then_inc(sem(L + "sig_rec"), 1)
                e.wait_ge(*after(L + "exps", 2))
                link(e, c, e.tensor_scalar(h_sig_in, h_sig_in, 1.0, None, ALU.add))
                link(e, c, e.reciprocal(h_sig_in, h_sig_in))
                link(e, c, e.tensor_tensor(h_sig_in, h_sig_in, h_u, ALU.mult))
                e.wait_ge(*after(L + "alpha"))
                link(e, c, e.tensor_tensor(h_beta, h_alpha, h_alpha, ALU.mult))
                e.tensor_scalar(h_beta, h_beta, -1.0, 1.0, ALU.mult, ALU.add).then_inc(sem(L + "one_less"), 1)
                e.wait_ge(*after(L + "beta"))
                link(e, c, e.tensor_tensor(h_beta, h_beta, h_sig_in, ALU.mult))
                for o in range(2):
                    for b in range(G):
                        s = slice(b * SEQ, (b + 1) * SEQ)
                        ins = e.tensor_tensor_scan(h_u[:, o, s], h_alpha[:, o, s], h_beta[:, o, s], 0.0,
                                                   ALU.mult, ALU.add)
                link(e, c, ins)
                e.tensor_tensor(h_gelu, h_gelu, h_u, ALU.mult).then_inc(sem(L + "m"), 1)
                e.wait_ge(*after(L + "o"))
                e.tensor_tensor(x[:, :], x[:, :], ps[:, 6, :], ALU.add).then_inc(sem(L + "x"), 1)

        def out_layer(e, eng, ready):
            if eng == "pe":
                e.wait_ge(*after(*ready))
                for t in range(TT):
                    ins = e.transpose(ps[:, 0, t * P:(t + 1) * P], x[:, t * P:(t + 1) * P], K("ident"))
                ins.then_inc(sem("C_out_t"), 1)
            if eng == "act":
                e.wait_ge(*after("C_out_t"))
                e.activation(x_tok[:, :, :].rearrange("p t d -> p (t d)"), ps[:, 0, :], ACT.Copy).then_inc(sem("C_out"), 1)
            if eng == "sp":
                e.wait_ge(*after("C_out"))
                settle(e)
                e.dma_start(out.rearrange("(i t p) d -> i p t d", t=TT, p=P)[turn[0]], x_tok[:, :, :]).then_inc(sem("C_stored"), 16)
                e.wait_ge(*after("C_stored", 16))
                settle(e)

        def front(e, eng):
            if eng == "pe":
                e.wait_ge(*after("A_loaded", 16))
                for t in range(TT):
                    ins = e.transpose(ps[:, 0, t * P:(t + 1) * P], x_tok[:, t, :], K("ident"))
                ins.then_inc(sem("A_x_t"), 1)
            if eng == "dve":
                e.wait_ge(*after("A_x_t"))
                e.tensor_copy(x[:, :], ps[:, 0, :]).then_inc(sem("A_x"), 1)
            if eng == "sp":
                e.wait_ge(*after("A_x_t"))
                settle(e)
                load_tokens(e, (turn[0] + 1) % TURNS)
            a_layer(e, eng, 0)
            f_layer(e, eng, "f1_", 1, ("a_x",))
            b_layer(e, eng, 2, ("f1_x",))
            f_layer(e, eng, "f2_", 4, ("b_x",))
            d_layer(e, eng, 5, ("f2_x",))

        def back(e, eng):
            r_layer(e, eng)
            g_layer(e, eng, "g1_", 1, 1, ("r_x",))
            h_layer(e, eng, 4, 2, ("g1_x",))
            g_layer(e, eng, "g2_", 5, 3, ("h_x",))
            out_layer(e, eng, ("g2_x",))
            if eng == "sp":
                load_readout(e, (turn[0] + 1) % TURNS)

        def load_tokens(sp, i):
            sp.dma_start(x_tok[:, :, :], x_in.rearrange("(i t p) d -> i p t d", t=TT, p=P)[i]).then_inc(sem("A_loaded"), 16)

        def load_readout(sp, i):
            def of(dram):
                return dram.rearrange("(i b) p t -> i p b t", b=G)[i]

            sp.dma_start(seq2(u_rows), of(u_dram)).then_inc(sem("C_loaded"), 16)
            sp.dma_start(seq2(q_rows), of(q_dram)).then_inc(sem("C_loaded"), 16)
            sp.dma_start(seq2(x1[:, :]), of(x_dram)).then_inc(sem("C_loaded"), 16)
            for h in range(DH):
                s = slice(DD * h, DD * (h + 1))
                sp.dma_start(seq2(KZ[s, h, :]), of(k_dram)[s]).then_inc(sem("C_loaded"), 16)

        def begin(n=0):
            turn[0] = n
            chain.clear()

        def loop(e, body, eng):
            with e.Fori(0, TURNS) as it:
                begin(it)
                body(e, eng)
            begin()

        last = TURNS - 1

        block = ctx.enter_context(nc.Block())

        @block.sync
        def _(sp):
            for dst, src in ((w_sb, weights), (col_sb, columns), (const_sb, consts)):
                sp.dma_start(dst[:, :], src).then_inc(sem("params"), 16)
            sp.dma_start(row_sb[:, :], rows.partition_broadcast(P)).then_inc(sem("params"), 16)
            load_tokens(sp, 0)
            loop(sp, front, "sp")
            sp.wait_ge(sem("A_loaded"), 16 * (TURNS + 1))
            for j in range(2):
                for dst, src in ((scan_k, k_dram), (scan_v, v_dram)):
                    sp.dma_start(dst[:, j, :, :], src.rearrange("(j b) (h d) t -> j (b h) d t", j=2, h=DH)[j])\
                        .then_inc(sem("scan_loaded"), 16)
                sp.dma_start(scan_b[:, j, :], b_dram.rearrange("(j b) h t -> j (b h) t", j=2)[j])\
                    .then_inc(sem("scan_loaded"), 16)
            sp.wait_ge(sem("scanned"), 1)
            for j in range(2):
                sp.dma_start(u_dram.rearrange("(j b) (h d) t -> j (b h) d t", j=2, h=DH)[j], scan_v[:, j, :, :])\
                    .then_inc(sem("updates_stored"), 16)
            sp.wait_ge(sem("updates_stored"), 32)
            sp.wait_ge(sem("zeroed"), 1)
            load_readout(sp, 0)
            loop(sp, back, "sp")
            sp.wait_ge(sem("C_loaded"), 16 * (3 + DH) * (TURNS + 1))

        @block.tensor
        def _(pe):
            pe.wait_ge(sem("params"), 64)
            pe.wait_ge(sem("ready"), 8)
            loop(pe, front, "pe")
            loop(pe, back, "pe")

        @block.scalar
        def _(act):
            act.wait_ge(sem("params"), 64)
            act.wait_ge(sem("ready"), 8)
            act.preload_act_table_set(LN_EXP_SET)
            act.activation(dec_t[:, 0:2], col_sb[:, C_AT["h_lambda"][0]:C_AT["h_lambda"][0] + 2], ACT.Abs)\
                .then_inc(sem("softplus"), 1)
            act.wait_ge(sem("softplus"), 1)
            act.activation(dec_t[:, 2:4], dec_t[:, 0:2], ACT.Exp, scale=-1.0, bias=ZERO).then_inc(sem("softplus"), 1)
            act.wait_ge(sem("softplus"), 2)
            act.activation(dec_t[:, 4:6], dec_t[:, 2:4], ACT.Ln, bias=eps[:, 3:4]).then_inc(sem("softplus"), 1)
            loop(act, front, "act")
            loop(act, back, "act")

        @block.gpsimd
        def _(pool):
            pool.memset(QX[:, :, :], 0.0).then_inc(sem("ready"), 1)
            pool.memset(VX[:, :, :], 0.0).then_inc(sem("ready"), 1)
            pool.memset(UX[:, :, :], 0.0).then_inc(sem("ready"), 1)
            loop(pool, front, "pool")
            loop(pool, back, "pool")

        @block.vector
        def _(dve):
            dve.memset(KX[:, :, :], 0.0).then_inc(sem("k_zeroed"), 1)
            dve.memset(eps[:, 0:1], 1e-5).then_inc(sem("ready"), 1)
            dve.memset(eps[:, 1:2], 1e-6).then_inc(sem("ready"), 1)
            dve.memset(eps[:, 2:3], 0.0)
            dve.memset(eps[:, 3:4], 1.0).then_inc(sem("ready"), 1)
            dve.wait_ge(sem("k_zeroed"), 1)
            dve.memset(KX[SHIFT_ROW:P, :, :], 1.0).then_inc(sem("ready"), 1)
            dve.memset(stat[:, :, :], 0.0).then_inc(sem("k_zeroed"), 1)
            dve.wait_ge(sem("params"), 64)
            dve.tensor_copy(ident_b[:, :], K("ident")).then_inc(sem("ready"), 1)
            lam = C_AT["h_lambda"][0]
            dve.tensor_scalar(dec_t[:, 6:8], col_sb[:, lam:lam + 2], 0.0, None, ALU.max).then_inc(sem("dec"), 1)
            dve.wait_ge(sem("softplus"), 3)
            dve.wait_ge(sem("dec"), 1)
            dve.tensor_tensor(dec_t[:, 6:8], dec_t[:, 6:8], dec_t[:, 4:6], ALU.add).then_inc(sem("dec"), 1)
            dve.wait_ge(sem("dec"), 2)
            dve.tensor_scalar(decay[:, :], dec_t[:, 6:8], -8.0, None, ALU.mult).then_inc(sem("dec"), 1)
            b_in = C_AT["h_bin"][0]
            dve.tensor_scalar(neg_bias[:, :], col_sb[:, b_in:b_in + 4], -1.0, None, ALU.mult).then_inc(sem("dec"), 1)
            dve.wait_ge(sem("k_zeroed"), 2)
            loop(dve, front, "dve")

            dve.memset(state[:, :, :, :], 0.0).then_inc(sem("scan_step"), 1)
            dve.wait_ge(sem("scan_loaded"), 96)
            with dve.Fori(0, SEQ) as t:
                def along(ap, axis):
                    return ap.unsqueeze(axis).broadcast_to([P, 2, DD, DD])

                k_t = scan_k[:, :, :, bass.ds(t, 1)].rearrange("p j d o -> p j (d o)")
                v_t = scan_v[:, :, :, bass.ds(t, 1)].rearrange("p j d o -> p j (d o)")
                b_t = scan_b[:, :, bass.ds(t, 1)].broadcast_to([P, 2, DD])
                done_before = t * SCAN_STEPS + 1
                dve.wait_ge(sem("scan_step"), done_before)
                dve.tensor_tensor(outer[:, :, :, :], state[:, :, :, :], along(k_t, 2), ALU.mult)\
                    .then_inc(sem("scan_step"), 1)
                dve.wait_ge(sem("scan_step"), done_before + 1)
                dve.tensor_reduce(s_k[:, :, :], outer[:, :, :, :], AX_X, ALU.add).then_inc(sem("scan_step"), 1)
                dve.wait_ge(sem("scan_step"), done_before + 2)
                dve.tensor_tensor(s_k[:, :, :], v_t, s_k[:, :, :], ALU.subtract).then_inc(sem("scan_step"), 1)
                dve.wait_ge(sem("scan_step"), done_before + 3)
                dve.tensor_tensor(v_t, s_k[:, :, :], b_t, ALU.mult).then_inc(sem("scan_step"), 1)
                dve.wait_ge(sem("scan_step"), done_before + 4)
                dve.tensor_tensor(outer[:, :, :, :], along(v_t, 3), along(k_t, 2), ALU.mult)\
                    .then_inc(sem("scan_step"), 1)
                dve.wait_ge(sem("scan_step"), done_before + 5)
                dve.tensor_tensor(state[:, :, :, :], state[:, :, :, :], outer[:, :, :, :], ALU.add)\
                    .then_inc(sem("scan_step"), 1)
            dve.wait_ge(sem("scan_step"), SEQ * SCAN_STEPS + 1)
            dve.tensor_copy(s_k[:, :, :], state[:, :, 0, :]).then_inc(sem("scanned"), 1)
            dve.memset(KZ, 0.0)
            dve.memset(u_pad, 0.0).then_inc(sem("zeroed"), 1)
            loop(dve, back, "dve")


def layouts(a):
    def heads_last(w):
        n = w.shape[-1] // HD
        return w.reshape(w.shape[:-1] + (n, HD)).swapaxes(-1, -2).reshape(w.shape)

    def partner(w, order):
        n = w.shape[-1] // HD
        return w.reshape(w.shape[:-1] + (n, HD))[..., order].reshape(w.shape)

    half = [4, 5, 6, 7, 0, 1, 2, 3]
    inter = [1, 0, 3, 2, 4, 5, 6, 7]
    wi, bi = a["L0_attn_b_W_in"], a["L0_attn_b_b_in"]
    w = dict(
        a_q=heads_last(a["L0_attn_a_w_q"]), a_q2=heads_last(partner(a["L0_attn_a_w_q"], half)),
        a_k=heads_last(a["L0_attn_a_w_k"]), a_k2=heads_last(partner(a["L0_attn_a_w_k"], half)),
        a_v=a["L0_attn_a_w_v"], a_o=a["L0_attn_a_w_o"],
        f_base=a["L0_ffn_base_w"].T, f_A=a["L0_ffn_lora_A"].transpose(1, 0, 2).reshape(P, -1),
        f_B=a["L0_ffn_lora_B"].reshape(-1, P), f_r=a["L0_ffn_router_w"].T,
        b_q=heads_last(wi[:, :P]), b_q2=heads_last(partner(wi[:, :P], inter)),
        b_k=heads_last(wi[:, P:2 * P]), b_k2=heads_last(partner(wi[:, P:2 * P], inter)),
        b_v=wi[:, 2 * P:], b_o=a["L0_attn_b_W_out"],
        d_q=a["L1_attn_a_Wq"], d_k=a["L1_attn_a_Wk"], d_v=a["L1_attn_a_Wv"], d_b=a["L1_attn_a_Wb"],
        g_q=a["L1_ffn_Wq"], g_down=a["L1_ffn_Wdown"], g_up=a["L1_ffn_Wup"],
        g_o=a["L1_ffn_Wo"], g_g=a["L1_ffn_Wg"], g_e=a["L1_ffn_We"].transpose(1, 0, 2).reshape(P, -1),
        h_proj=a["L1_attn_b_W_proj"].T,
        h_in=a["L1_attn_b_W_in"].T.reshape(2, HH, HID).transpose(1, 0, 2).reshape(HH, -1),
        h_gate=a["L1_attn_b_W_gate"].T.reshape(2, HH, HID).transpose(1, 0, 2).reshape(HH, -1),
        h_out=a["L1_attn_b_W_out"].T.reshape(2, HH, P).transpose(1, 0, 2).reshape(HH, -1))

    def halves(v):
        return v.reshape(2, HH, -1).transpose(1, 0, 2).reshape(HH, -1)

    c = dict(
        f_bb=a["L0_ffn_base_b"], b_bq=heads_last(bi[:P]), b_bq2=heads_last(partner(bi[:P], inter)),
        b_bk=heads_last(bi[P:2 * P]), b_bk2=heads_last(partner(bi[P:2 * P], inter)),
        b_bo=a["L0_attn_b_b_out"], b_gamma=a["L0_attn_b_gamma"], b_beta=a["L0_attn_b_beta"],
        d_lnw=a["L1_attn_a_ln_w"], d_lnb=a["L1_attn_a_ln_b"], g_gamma1=a["L1_ffn_gamma1"],
        g_bdown=a["L1_ffn_bdown"],
        g_bo=a["L1_ffn_bo"], g_gamma2=a["L1_ffn_gamma2"],
        h_conv=halves(a["L1_attn_b_conv_w"].reshape(HID, TAPS)), h_cb=halves(a["L1_attn_b_conv_b"]),
        h_bin=halves(a["L1_attn_b_b_in"]), h_bgate=halves(a["L1_attn_b_b_gate"]),
        h_lambda=halves(a["L1_attn_b_forget_lambda"]))
    r = dict(f_rb=a["L0_ffn_router_b"], b_bv=bi[2 * P:], g_bq=a["L1_ffn_bq"], g_bup=a["L1_ffn_bup"], g_bg=a["L1_ffn_bg"])

    def pack(table, parts):
        at, n = offsets(table)
        out = np.zeros((P, n), np.float32)
        for name, (lo, m) in at.items():
            v = np.asarray(parts[name])
            v = v.reshape(v.shape[0], -1)
            out[0:v.shape[0], lo:lo + m] = v
        return out

    row = np.concatenate([np.asarray(r[name]) for name in ROWS]).astype(np.float32)
    return pack(WEIGHTS, w), pack(COLUMNS, c), row


def constants():
    i = np.arange(P)
    pos = np.arange(SEQ, dtype=np.float32)

    def rotary(freq, sign, heads):
        cos = np.ones((HD, SEQ), np.float32)
        sin = np.zeros((HD, SEQ), np.float32)
        for d in range(HD):
            if freq[d] is not None:
                cos[d], sin[d] = np.cos(pos * freq[d]), sign[d] * np.sin(pos * freq[d])
        return np.repeat(cos, heads, 0), np.repeat(sin, heads, 0)

    fa = (1.0 / np.float32(10000.0) ** (np.arange(0, HD, 2, dtype=np.float32) / HD)).astype(np.float32)
    fb = (1.0 / np.float32(10000.0) ** (np.arange(0, 4, 2, dtype=np.float32) / 4)).astype(np.float32)
    sa = [-1] * 4 + [1] * 4
    cos_a, sin_a = rotary(list(fa) + list(fa), sa, HEADS)
    cos_ak, sin_ak = rotary(list(fa) + list(fa), sa, KV_A)
    cos_b, sin_b = rotary([fb[0], fb[0], fb[1], fb[1]] + [None] * 4, [-1, 1, -1, 1] + [0] * 4, HEADS)
    tri = (i[:, None] <= i[None, :]).astype(np.float32)
    den = np.zeros((P, 4, STRIP), np.float32)
    for n in range(4):
        den[:, n, HD * n:HD * n + HD] = 1.0
    j = np.arange(KV_A * HD)
    parts = dict(
        ident=np.eye(P), center=np.eye(P) - 1.0 / P, mean=np.full((P, P), 1.0 / P),
        head_mean=(i[:, None] % HEADS == i[None, :] % HEADS) / HD,
        kv_mean=(j[:, None] % KV_A == j[None, :] % KV_A) / HD,
        head_sum=(i[:, None] // DD == i[None, :] // DD),
        cos_a=cos_a, sin_a=sin_a, cos_ak=cos_ak, sin_ak=sin_ak, cos_b=cos_b, sin_b=sin_b,
        causal=np.concatenate([tri, np.ones((P, P)), tri], 1), den=den.reshape(P, -1))
    at, n = offsets(CONSTS)
    out = np.zeros((P, n), np.float32)
    for name, (lo, m) in at.items():
        v = parts[name]
        out[0:v.shape[0], lo:lo + m] = v
    return out


def kernel(**inputs):
    import concourse.bacc as bacc
    from concourse.bass_utils import run_bass_kernel_spmd

    a = {k: np.asarray(v) for k, v in inputs.items()}
    w, c, r = layouts(a)
    arrays = dict(x_dram_in=np.ascontiguousarray(a["L0_attn_a_x"]).reshape(SEQS * SEQ, P),
                  weights_dram=w, columns_dram=c, rows_dram=r, consts_dram=constants())
    nc = bacc.Bacc("TRN2", target_bir_lowering=False, num_devices=1)
    args = [nc.dram_tensor(n, v.shape, mybir.dt.from_np(v.dtype), kind="ExternalInput").ap()
            for n, v in arrays.items()]
    out = nc.dram_tensor("out_dram", (SEQS * SEQ, P), F32, kind="ExternalOutput").ap()
    build(nc, *args, out)
    got = run_bass_kernel_spmd(nc, [arrays], core_ids=[0]).results[0]["out_dram"]
    return got.reshape(SEQS, SEQ, P)
```

```python
from collections import namedtuple
from contextlib import ExitStack

import numpy as np

import concourse.bass as bass
from concourse import mybir

F32 = mybir.dt.float32
BF16 = mybir.dt.bfloat16
ALU = mybir.AluOpType
ACT = mybir.ActivationFunctionType
AX_X = mybir.AxisListType.X
LN_EXP_SET = "natural_log_exp_and_others"

P = 128
SEQS, SEQ = 32, 256
STREAMS = 2
G = 1
TOK = G * SEQ
TT = TOK // P
TURNS = SEQS // (G * STREAMS)
HEADS, HD = 16, 8
KV_A = 4
DH, DD = 8, 16
EXPERTS = 8
RANK = 16
LATENT = 64
HID, HH = 192, 96
TAPS = 4
PARTS = 3
Q_BANDS = ((0, 0, 1), (1, 0, 1), (2, 0, 1), (3, 1, 2), (5, 1, 1))
K_BANDS = ((0, 0, 3), (3, 0, 1), (4, 0, 1), (5, 1, 1))
K_LOADS = sum(n for _, _, n in K_BANDS)
SHIFT_ROW = 96
SROWS = SHIFT_ROW + PARTS
PAIRS = G * HEADS // 2
QUADS = PAIRS // 2
ATTEND_STEPS = 2 * QUADS + 2
A_STEPS, F_STEPS, B_STEPS, D_STEPS = 23 + ATTEND_STEPS, 14, 31 + PAIRS + ATTEND_STEPS, 14
R_STEPS, G_STEPS, H_STEPS, OUT_STEPS = 15, 38, 18, 5
LAG = 3
SCAN_STEPS = 6
CAP = 50.0
STRIP = 32

WEIGHTS = dict(a_q=P, a_q2=P, a_k=32, a_k2=32, a_v=32, a_o=P,
               f_base=P, f_A=P, f_B=P, f_r=EXPERTS,
               b_q=P, b_q2=P, b_k=P, b_k2=P, b_v=P, b_o=P,
               d_q=P, d_k=P, d_v=P, d_b=DH,
               g_q=P, g_down=LATENT, g_up=2 * P, g_o=P, g_g=EXPERTS, g_e=EXPERTS * P,
               h_proj=2 * HID, h_in=2 * HID, h_gate=2 * HID, h_out=2 * P)
COLUMNS = dict(f_bb=1, b_bq=1, b_bq2=1, b_bk=1, b_bk2=1, b_bo=1, b_gamma=1, b_beta=1,
               d_lnw=1, d_lnb=1, g_gamma1=1, g_bdown=1, g_bo=1, g_gamma2=1,
               h_conv=2 * TAPS, h_cb=2, h_bin=2, h_bgate=2, h_lambda=2)
ROWS = dict(f_rb=EXPERTS, b_bv=P, g_bq=P, g_bup=2 * P, g_bg=EXPERTS)
CONSTS = dict(ident=P, center=P, mean=P, head_mean=P, kv_mean=KV_A * HD, head_sum=P,
              cos_a=SEQ, sin_a=SEQ, cos_ak=SEQ, sin_ak=SEQ, cos_b=SEQ, sin_b=SEQ,
              causal=3 * P, den=4 * STRIP)


def offsets(table):
    out, at = {}, 0
    for name, n in table.items():
        out[name] = (at, n)
        at += n
    return out, at


PER_TURN = dict(
    A_tokens=16, A_x_t=1, A_centered=6, A_variance=6, A_squared=6, A_act_chain=16, A_rstd=6,
    A_x=1, A_copied=6, A_dve_chain=33, a_k_out=16, a_q_out=16, a_kx=96, a_qx=80, a_q=1, a_k=1,
    a_v=1, a_ms=1, a_scores_t=8, a_weighed=4, a_o=1, a_sq=2, a_rms=1, a_k_round=2, a_exp=8,
    a_k_rest=2, a_masked=8, a_xn=1, a_kf=1, a_q_part=3, a_vx=4, a_rope_done=1, a_y=1, a_x=1,
    f1_logits=1, f1_ax=1, f1_weights_t=1, f1_o=1, f1_axs=1, f1_e1=1, f1_xn=1, f1_e0=1,
    f1_spread=1, f1_axw=1, f1_x=1, b_k_out=16, b_q_out=16, b_kx=96, b_qx=80, b_m_out=16,
    b_shift=16, b_q=1, b_k=1, b_v=1, b_scores=8, b_max_turned=1, b_scores_t=8, b_weighed=4,
    b_o=1, b_k_round=2, b_max_rows=1, b_exp=8, b_k_rest=2, b_x1=1, b_xn=1, b_kf=1, b_q_part=3,
    b_vx=4, b_row_max=8, b_max_parts=1, b_y=1, b_x=1, f2_logits=1, f2_ax=1, f2_weights_t=1,
    f2_o=1, f2_axs=1, f2_e1=1, f2_xn=1, f2_e0=1, f2_spread=1, f2_axw=1, f2_x=1, d_x_out=16,
    d_stored=64, d_kvb=1, d_q=1, d_norm2=1, d_sq=1, d_e=1, d_qs=1, d_rk=1, d_xn=1, d_norm2c=1,
    d_kvn=1, C_readout=176, C_stored=16, C_centered=4, C_variance=8, C_out_t=1, C_squared=8,
    C_act_chain=9, C_rstd=8, C_out=1, C_copied=4, C_dve_chain=31, r_u_t=1, r_w=4, r_read=2,
    r_rows=1, r_ux=2, r_masked=4, r_on=1, r_x=1, g1_qd=1, g1_kv=1, g1_heads_t=1, g1_o=1,
    g1_logits=1, g1_experts=2, g1_mixed_t=1, g1_down=1, g1_exp=1, g1_y=1, g1_e1=1,
    g1_score_odd=1, g1_value_odd=1, g1_x1=1, g1_xn=1, g1_qkv=1, g1_score=2, g1_shifted=1,
    g1_value=2, g1_heads=1, g1_x2=1, g1_xm=1, g1_e0=1, g1_gated=2, g1_mixed=2, g1_x=1, h_proj=1,
    h_gates=2, h_o=1, h_pad=1, h_gelu=1, h_exps=2, h_alpha=1, h_beta=1, h_xn=1, h_conv=2,
    h_sig_rec=1, h_one_less=1, h_m=1, h_x=1, g2_qd=1, g2_kv=1, g2_heads_t=1, g2_o=1,
    g2_logits=1, g2_experts=2, g2_mixed_t=1, g2_down=1, g2_exp=1, g2_y=1, g2_e1=1,
    g2_score_odd=1, g2_value_odd=1, g2_x1=1, g2_xn=1, g2_qkv=1, g2_score=2, g2_shifted=1,
    g2_value=2, g2_heads=1, g2_x2=1, g2_xm=1, g2_e0=1, g2_gated=2, g2_mixed=2, g2_x=1)

FRONT, BACK = ("A", "a", "f1", "b", "f2", "d"), ("C", "r", "g1", "h", "g2")


def parts_of(name):
    return name.partition("_")[::2]


def signals_of(loop):
    return dict.fromkeys(parts_of(n)[1] for n in PER_TURN if parts_of(n)[0] in loop)


LOADS = ("tokens", "readout")
BACK_SHARES = dict(zip([n for n in signals_of(BACK) if n not in signals_of(FRONT) and n not in LOADS],
                       [n for n in signals_of(FRONT) if n not in signals_of(BACK) and n not in LOADS]))
FRONT_SHARED = {front: back for back, front in BACK_SHARES.items()}


def total(loop, what):
    return sum(PER_TURN[n] for n in PER_TURN if parts_of(n)[0] in loop and parts_of(n)[1] == what)


def before(name):
    layer, what = parts_of(name)
    loop = FRONT if layer in FRONT else BACK
    earlier = loop[:loop.index(layer)]
    front = 0 if loop is FRONT else TURNS * total(FRONT, BACK_SHARES.get(what, what))
    return front + total(earlier, what), total(loop, what)


def build(nc, x_in, weights, columns, rows, consts, out):
    W_AT, W_N = offsets(WEIGHTS)
    C_AT, C_N = offsets(COLUMNS)
    R_AT, R_N = offsets(ROWS)
    K_AT, K_N = offsets(CONSTS)
    ctx = ExitStack()

    def sb(name, shape, dt=F32):
        return ctx.enter_context(nc.sbuf_tensor(name, shape, dt))

    with ctx:
        w_sb = sb("w_sb", [P, W_N])
        col_sb = sb("col_sb", [P, C_N])
        row_sb = sb("row_sb", [P, R_N])
        const_sb = sb("const_sb", [P, K_N])

        def W(name, lo=0, hi=None, rows_=P):
            at, n = W_AT[name]
            return w_sb[0:rows_, at + lo:at + (n if hi is None else hi)]

        def C(name, i=0, rows_=P):
            return col_sb[0:rows_, C_AT[name][0] + i:C_AT[name][0] + i + 1]

        def R(name):
            at, n = R_AT[name]
            return row_sb[:, at:at + n]

        def K(name, rows_=P):
            at, n = K_AT[name]
            return const_sb[0:rows_, at:at + n]

        Stream = namedtuple("Stream", "front back load_tokens load_readout sem zeroed UX VX")
        ident_b = sb("ident_b", [P, P], BF16)
        eps = sb("eps", [P, 4])
        EPS5, EPS6, ZERO = eps[:, 0:1], eps[:, 1:2], eps[:, 2:3]
        neg_bias = sb("neg_bias", [P, 4])
        decay = sb("decay", [P, 2])
        dec_t = sb("dec_t", [P, 8])

        bands = sb("bands", [P, 2 * STREAMS, HEADS, TOK], BF16)
        scan_k = sb("scan_k", [P, 2, DD, SEQ])
        scan_v = sb("scan_v", [P, 2, DD, SEQ])
        scan_b = sb("scan_b", [P, 2, SEQ])
        state = sb("state", [P, 2, DD, DD])
        outer = sb("outer", [P, 2, DD, DD])
        s_k = sb("s_k", [P, 2, DD])

        ps = ctx.enter_context(nc.psum_tensor("ps", [P, 8, 512], F32))

        q_dram = nc.dram_tensor("q_dram", [SEQS, P, SEQ], F32).ap()
        k_dram = nc.dram_tensor("k_dram", [SEQS, P, SEQ], F32).ap()
        v_dram = nc.dram_tensor("v_dram", [SEQS, P, SEQ], F32).ap()
        b_dram = nc.dram_tensor("b_dram", [SEQS, DH, SEQ], F32).ap()
        x_dram = nc.dram_tensor("x_dram", [SEQS, P, SEQ], F32).ap()
        u_dram = nc.dram_tensor("u_dram", [SEQS, P, SEQ], F32).ap()

        sems = {}

        def sem(name):
            if name not in sems:
                sems[name] = ctx.enter_context(nc.semaphore(name))
            return sems[name]

        def signal(lane, name):
            what = parts_of(name)[1]
            what = BACK_SHARES.get(what, what)
            if what in FRONT_SHARED:
                return sem(f"s{lane}_{what}_then_{FRONT_SHARED[what]}")
            return sem(f"s{lane}_{what}")

        turn = [0]
        chains = [{} for _ in range(STREAMS)]

        def value(name, k):
            first, per = before(name)
            return turn[0] * per + (first + k)

        def stream(lane):
            def tile(name, shape, dt=F32):
                return sb(f"{name}_{lane}", shape, dt)

            QX, KX = bands[:, 2 * lane], bands[:, 2 * lane + 1]
            arena = (scan_k, scan_v)[lane][:, :, :, :].rearrange("p a b c -> p (a b c)")
            PR = arena[:, 0:4096].rearrange("p (a b c) -> p a b c", a=4, b=2)
            PRB = bands[:, 2 * lane:2 * lane + 2].rearrange("p a h t -> p (a h t)").bitcast(F32)\
                .rearrange("p (a b c) -> p a b c", a=4, b=2)
            VX = tile("VX", [P, TT, HEADS * STRIP])
            UX = tile("UX", [P, TT, DH * STRIP])
            q_parts = tile("q_parts", [P, PARTS, TOK], BF16)
            k_parts = tile("k_parts", [P, PARTS, TOK], BF16)
            neg_max = tile("neg_max", [P, TT, HEADS])
            max_parts = tile("max_parts", [P, TT, PARTS, HEADS], BF16)
            max_rest = tile("max_rest", [P, 2, TT, HEADS])
            max_rows = tile("max_rows", [PARTS * HEADS, TOK], BF16)
            x, x1, x_next, xc, xn, sq, lnv, rstd, ta, tb, tc, qf, kf, rq, rk, y, q_new, k_new, v_sig = [
                tile(n, [P, TOK]) for n in
                "x x1 x_next xc xn sq lnv rstd ta tb tc qf kf rq rk y q_new k_new v_sig".split()]
            x_tok = tile("x_tok", [P, TT, P])
            small = tile("small", [P, 8, TT * EXPERTS])
            top8 = tile("top8", [P, TT, 8])
            stat = tile("stat", [P, 4, TT])
            beta_sb = tile("beta_sb", [DH, TOK])

            cuts = [0]

            def piece(n, rows_=P):
                cuts[0] += n
                return arena[0:rows_, cuts[0] - n:cuts[0]]

            KZ = piece(DH * TOK).rearrange("p (h t) -> p h t", h=DH)
            prod = piece(EXPERTS * P).rearrange("p (e f) -> p e f", e=EXPERTS)
            h_gelu, h_u, h_sig_in, h_sig_rec, h_alpha, h_beta = [
                piece(2 * TOK, HH).rearrange("p (a t) -> p a t", a=2) for _ in range(6)]
            u_pad = piece(2 * G * (SEQ + TAPS - 1), HH).rearrange("p (a b t) -> p a b t", a=2, b=G)
            u_rows, q_rows, o_rows = [piece(TOK) for _ in range(3)]

            q_scratch = nc.dram_tensor(f"q_scratch_{lane}", [PARTS, P, TOK], BF16).ap()
            k_scratch = nc.dram_tensor(f"k_scratch_{lane}", [PARTS, P, TOK], BF16).ap()
            m_scratch = nc.dram_tensor(f"m_scratch_{lane}", [PARTS * HEADS, TOK], BF16).ap()

            def sem(name):
                return signal(lane, name)

            def after(name, k=1):
                return signal(lane, name), value(name, k)

            def settle(eng):
                eng.nop(nofuse=True)

            chain = chains[lane]

            def link(eng, name, ins):
                chain[name] = chain.get(name, 0) + 1
                ins.then_inc(sem(name), 1)
                eng.wait_ge(*after(name, chain[name]))

            BANK = 4 * lane

            def slot(n):
                return BANK

            def turns_of_two(n):
                return BANK + 2 * (n % 2)

            def half(bank, i, rows_=P):
                return ps[0:rows_, BANK + bank, i * TOK:(i + 1) * TOK]

            def seq2(ap):
                return ap.rearrange("p (b t) -> p b t", b=G)

            def both(ap):
                return ap.unsqueeze(1).broadcast_to([ap.shape[0], G, SEQ])

            def heads_of(n):
                m = n % (PAIRS // G)
                i, half = m // 2, m % 2
                return [4 * (2 * half + j) + i for j in range(2)]


            def pe_norm(pe, at, ph, n, src, ready, centered=True):
                yield at
                pe.wait_ge(*after(*ready))
                if centered:
                    pe.matmul(half(2, 0), K("center"), src, start=True, stop=True).then_inc(sem(ph + "centered"), 1)
                yield at + 3
                pe.wait_ge(*after(ph + "squared", n + 1))
                pe.matmul(half(3, 0), K("mean"), sq[:, :], start=True, stop=True).then_inc(sem(ph + "variance"), 1)

            def act_norm(act, at, ph, n, nc_n, src=None, ready=None, e=None):
                yield at + 2
                if src is None:
                    act.wait_ge(*after(ph + "copied", nc_n + 1))
                    act.activation(sq[:, :], xc[:, :], ACT.Square).then_inc(sem(ph + "squared"), 1)
                else:
                    act.wait_ge(*after(*ready))
                    act.activation(sq[:, :], src, ACT.Square).then_inc(sem(ph + "squared"), 1)
                yield at + 4
                act.wait_ge(*after(ph + "variance", n + 1))
                link(act, ph + "act_chain", act.activation(lnv[:, :], half(3, 0), ACT.Ln, bias=e))
                act.activation(rstd[:, :], lnv[:, :], ACT.Exp, scale=-0.5, bias=ZERO).then_inc(sem(ph + "rstd"), 1)

            def dve_norm(dve, at, ph, n, nc_n, dst, name, src=None, gamma=None, beta=None):
                yield at + 1
                if src is None:
                    dve.wait_ge(*after(ph + "centered", nc_n + 1))
                    dve.tensor_copy(xc[:, :], half(2, 0)).then_inc(sem(ph + "copied"), 1)
                    src = xc[:, :]
                yield at + 5
                dve.wait_ge(*after(ph + "rstd", n + 1))
                if gamma is None:
                    dve.tensor_tensor(dst, src, rstd[:, :], ALU.mult).then_inc(sem(name), 1)
                elif beta is None:
                    dve.scalar_tensor_tensor(dst, src, gamma, rstd[:, :], ALU.mult, ALU.mult).then_inc(sem(name), 1)
                else:
                    link(dve, ph + "dve_chain", dve.tensor_tensor(xc[:, :], src, rstd[:, :], ALU.mult))
                    dve.tensor_scalar(dst, xc[:, :], gamma, beta, ALU.mult, ALU.add).then_inc(sem(name), 1)


            def dve_split_q(dve, ph, L):
                c = ph + "dve_chain"
                ins = dve.tensor_copy(q_parts[:, 0, :], qf[:, :])
                ins.then_inc(sem(L + "q_part"), 1)
                dve.wait_ge(*after(L + "q_part", 1))
                link(dve, c, dve.tensor_tensor(ta[:, :], qf[:, :], q_parts[:, 0, :], ALU.subtract))
                dve.tensor_copy(q_parts[:, 1, :], ta[:, :]).then_inc(sem(L + "q_part"), 1)
                dve.wait_ge(*after(L + "q_part", 2))
                dve.tensor_tensor(q_parts[:, 2, :], ta[:, :], q_parts[:, 1, :], ALU.subtract).then_inc(sem(L + "q_part"), 1)

            def act_split_k(act, at, L, n=P):
                yield at
                act.wait_ge(*after(L + "kf"))
                act.activation(k_parts[0:n, 0, :], kf[0:n, :], ACT.Copy).then_inc(sem(L + "k_round"), 1)
                yield at + 2
                act.wait_ge(*after(L + "k_rest", 1))
                act.activation(k_parts[0:n, 1, :], tc[0:n, :], ACT.Copy).then_inc(sem(L + "k_round"), 1)

            def pool_split_k(pool, at, L, n=P):
                yield at + 1
                pool.wait_ge(*after(L + "k_round", 1))
                pool.tensor_tensor(tc[0:n, :], kf[0:n, :], k_parts[0:n, 0, :], ALU.subtract).then_inc(sem(L + "k_rest"), 1)
                yield at + 3
                pool.wait_ge(*after(L + "k_round", 2))
                pool.tensor_tensor(k_parts[0:n, 2, :], tc[0:n, :], k_parts[0:n, 1, :], ALU.subtract).then_inc(sem(L + "k_rest"), 1)

            def sp_spread(sp, at, L, kv=HEADS):
                yield at
                sp.wait_ge(*after(L + "k_rest", 2))
                k_of = k_scratch[:, 0:kv * HD, :]
                sp.dma_start(k_of.rearrange("c p t -> p c t"), k_parts[0:kv * HD, :, :]).then_inc(sem(L + "k_out"), 16)
                sp.wait_ge(*after(L + "q_part", PARTS))
                sp.dma_start(q_scratch.rearrange("c p t -> p c t"), q_parts[:, :, :]).then_inc(sem(L + "q_out"), 16)
                yield at + 2
                sp.wait_ge(*after(L + "k_out", 16))
                for band, part, n in K_BANDS:
                    for i in range(n):
                        src = k_scratch[part + i, 0:kv * HD, :].rearrange("(d h) t -> d h t", d=HD)
                        lo = HD * (band + i)
                        sp.dma_start(KX[lo:lo + HD, 0:kv, :], src).then_inc(sem(L + "kx"), 16)
                sp.wait_ge(*after(L + "q_out", 16))
                for band, part, n in Q_BANDS:
                    src = q_scratch[part:part + n].rearrange("c (d h) t -> (c d) h t", d=HD)
                    sp.dma_start(QX[HD * band:HD * (band + n), :, :], src).then_inc(sem(L + "qx"), 16)

            def pe_scores(pe, at, L):
                for n in range(PAIRS):
                    yield at + n
                    b = n // (PAIRS // G)
                    if n == 0:
                        pe.wait_ge(*after(L + "kx", 16 * K_LOADS))
                        pe.wait_ge(*after(L + "qx", 16 * len(Q_BANDS)))
                    if n >= 2:
                        pe.wait_ge(*after(L + "row_max", n - 1))
                    for j, h in enumerate(heads_of(n)):
                        for t in range(2):
                            ins = pe.matmul(ps[:, turns_of_two(n) + j, t * SEQ:(t + 1) * SEQ],
                                            QX[0:SHIFT_ROW, h, b * SEQ + t * P:b * SEQ + (t + 1) * P],
                                            KX[0:SHIFT_ROW, h, b * SEQ:(b + 1) * SEQ], start=True, stop=True)
                    ins.then_inc(sem(L + "scores"), 1)

            def dve_max(dve, at, ph, L):
                for n in range(PAIRS):
                    yield at + n
                    b, h = n // (PAIRS // G), heads_of(n)[0]
                    dve.wait_ge(*after(L + "scores", n + 1))
                    dve.tensor_reduce(
                        neg_max[:, 2 * b:2 * b + 2, h:h + 5:4].rearrange("p t j -> p j t"),
                        ps[:, turns_of_two(n):turns_of_two(n) + 2, :].rearrange("p j (t k) -> p j t k", t=2),
                        AX_X, ALU.max, negate=True).then_inc(sem(L + "row_max"), 1)
                yield at + PAIRS
                dve.wait_ge(*after(L + "row_max", PAIRS))
                c = ph + "dve_chain"
                link(dve, c, dve.tensor_copy(max_parts[:, :, 0, :], neg_max[:, :, :]))
                link(dve, c, dve.tensor_tensor(max_rest[:, 0], neg_max[:, :, :], max_parts[:, :, 0, :], ALU.subtract))
                link(dve, c, dve.tensor_copy(max_parts[:, :, 1, :], max_rest[:, 0]))
                dve.tensor_tensor(max_parts[:, :, 2, :], max_rest[:, 0], max_parts[:, :, 1, :], ALU.subtract).then_inc(sem(L + "max_parts"), 1)

            def pe_max_rows(pe, L):
                pe.wait_ge(*after(L + "max_parts"))
                settle(pe)
                psb = ps[0:PARTS * HEADS, BANK + 3, :].bitcast(BF16)
                for t in range(TT):
                    ins = pe.transpose(psb[:, t * P:(t + 1) * P],
                                       max_parts[:, t, :, :].rearrange("p c h -> p (c h)"), ident_b[:, :])
                ins.then_inc(sem(L + "max_turned"), 1)

            def act_max_rows(act, L):
                act.wait_ge(*after(L + "max_turned"))
                act.activation(max_rows[:, :], ps[0:PARTS * HEADS, BANK + 3, :].bitcast(BF16)[:, 0:TOK], ACT.Copy).then_inc(sem(L + "max_rows"), 1)

            def sp_max_rows(sp, at, L):
                yield at
                sp.wait_ge(*after(L + "max_rows"))
                sp.dma_start(m_scratch, max_rows[:, :]).then_inc(sem(L + "m_out"), 16)
                yield at + 1
                sp.wait_ge(*after(L + "m_out", 16))
                sp.dma_start(QX[SHIFT_ROW:SROWS, :, :], m_scratch.rearrange("(c h) t -> c h t", c=PARTS)).then_inc(sem(L + "shift"), 16)

            def pe_attend(pe, at, L, causal):
                for m in range(QUADS + 1):
                    for n in (2 * m, 2 * m + 1) if m < QUADS else ():
                        yield at + n
                        b = n // (PAIRS // G)
                        if n == 0 and causal:
                            pe.wait_ge(*after(L + "kx", 16 * K_LOADS))
                            pe.wait_ge(*after(L + "qx", 16 * len(Q_BANDS)))
                            pe.wait_ge(*after(L + "rope_done"))
                        if n == 0 and not causal:
                            pe.wait_ge(*after(L + "shift", 16))
                        if n >= 1:
                            pe.wait_ge(*after(L + "exp", n))
                        for j, h in enumerate(heads_of(n)):
                            for t in range(2):
                                lo = t * P if causal else 0
                                hk = h // (HEADS // KV_A) if causal else h
                                rows_ = SHIFT_ROW if causal else SROWS
                                ins = pe.matmul(ps[:, slot(n) + j, t * SEQ:(t + 1) * SEQ - lo],
                                                KX[0:rows_, hk, b * SEQ + t * P:b * SEQ + (t + 1) * P],
                                                QX[0:rows_, h, b * SEQ + lo:(b + 1) * SEQ], start=True, stop=True)
                        ins.then_inc(sem(L + "scores_t"), 1)
                    if m == 0:
                        continue
                    yield at + 2 * m + 1
                    pe.wait_ge(*after(L + ("masked" if causal else "exp"), 2 * m))
                    if m == 1:
                        pe.wait_ge(*after(L + "vx", 4))
                    b = (m - 1) // (QUADS // G)
                    i = (m - 1) % (QUADS // G)
                    for bank in (2, 3):
                        for t in range(2):
                            lo = t * P if causal else 0
                            for g in range(4):
                                h, n = 4 * g + i, 2 * (m - 1) + g // 2
                                lhs = VX[:, 2 * b + t, h * STRIP:(h + 1) * STRIP] if bank == 2 else \
                                    K("den")[:, i * STRIP:(i + 1) * STRIP]
                                ins = pe.matmul(ps[STRIP * g:STRIP * (g + 1), BANK + bank, b * SEQ + lo:(b + 1) * SEQ], lhs,
                                                PR[:, n % 4, g % 2, t * SEQ:(t + 1) * SEQ - lo],
                                                start=(i == 0 and t == 0), stop=(i == 3 and t == 1),
                                                skip_group_check=True)
                    ins.then_inc(sem(L + "weighed"), 1)

            def act_attend(act, at, ph, L, causal):
                scale = float(HD) ** -0.5
                for n in range(PAIRS):
                    yield at + n
                    act.wait_ge(*after(L + "scores_t", n + 1))
                    if causal:
                        v = ps[:, slot(n):slot(n) + 2, 0:SEQ + P]
                        link(act, ph + "act_chain", act.activation(v, v, ACT.Tanh, scale=scale / CAP))
                    if n >= 4:
                        act.wait_ge(*after(L + "weighed", (n - 4) // 2 + 1))
                    if causal:
                        act.activation(PR[:, n % 4, :, 0:SEQ + P], v, ACT.Exp, scale=CAP, bias=ZERO).then_inc(sem(L + "exp"), 1)
                    else:
                        act.activation(PR[:, n % 4, :, :], ps[:, slot(n):slot(n) + 2, :], ACT.Exp, scale=scale, bias=ZERO).then_inc(sem(L + "exp"), 1)

            def dve_attend(dve, at, ph, L):
                yield at + 2 * QUADS + 2
                dve.wait_ge(*after(L + "weighed", QUADS))
                link(dve, ph + "dve_chain", dve.reciprocal(tb[:, :], half(3, 0)))
                dve.tensor_tensor(y[:, :], half(2, 0), tb[:, :], ALU.mult).then_inc(sem(L + "y"), 1)

            def dve_values(dve, L, bank, bias):
                dst = VX[:, :, :].rearrange("p t (g c) -> p t g c", g=4)
                for i in range(4):
                    d = dst[:, :, :, 40 * i:40 * i + 8]
                    if bias is None:
                        s = half(bank, 0)[:, 0:TT * 32].rearrange("p (t g d) -> p t g d", t=TT, g=4)
                        dve.tensor_copy(d, s).then_inc(sem(L + "vx"), 1)
                    else:
                        s = half(bank, 0).rearrange("p (t g i d) -> p t g i d", t=TT, g=4, i=4)[:, :, :, i, :]
                        r = bias.rearrange("p (g i d) -> p g i d", g=4, i=4)[:, :, i, :].unsqueeze(1)\
                            .broadcast_to([P, TT, 4, HD])
                        dve.tensor_tensor(d, s, r, ALU.add).then_inc(sem(L + "vx"), 1)

            def a_layer(e, eng, n):
                ph, L = "A_", "a_"
                if eng == "pe":
                    yield from pe_norm(e, 0, ph, n, x[:, :], ("A_x",))
                    yield 6
                    e.wait_ge(*after(L + "xn"))
                    e.matmul(half(0, 0), W("a_q"), xn[:, :], start=True, stop=True)
                    e.matmul(half(0, 1), W("a_q2"), xn[:, :], start=True, stop=True).then_inc(sem(L + "q"), 1)
                    e.matmul(half(1, 0, 32), W("a_k"), xn[:, :], start=True, stop=True)
                    e.matmul(half(1, 1, 32), W("a_k2"), xn[:, :], start=True, stop=True).then_inc(sem(L + "k"), 1)
                    for t in range(TT):
                        ins = e.matmul(half(2, 0)[:, t * 32:(t + 1) * 32], xn[:, t * P:(t + 1) * P], W("a_v"),
                                       start=True, stop=True)
                    ins.then_inc(sem(L + "v"), 1)
                    yield 8
                    e.wait_ge(*after(L + "sq", 2))
                    e.matmul(half(3, 0), K("head_mean"), sq[:, :], start=True, stop=True)
                    e.matmul(half(3, 1, 32), K("kv_mean", 32), tb[0:32, :], start=True, stop=True).then_inc(sem(L + "ms"), 1)
                    yield from pe_attend(e, 20, L, True)
                    yield 20 + ATTEND_STEPS + 1
                    e.wait_ge(*after(L + "y"))
                    e.matmul(half(0, 0), W("a_o"), y[:, :], start=True, stop=True).then_inc(sem(L + "o"), 1)
                if eng == "act":
                    yield from act_norm(e, 0, ph, n, n, e=EPS5)
                    yield 7
                    e.wait_ge(*after(L + "q"))
                    e.activation(sq[:, :], half(0, 0), ACT.Square).then_inc(sem(L + "sq"), 1)
                    e.wait_ge(*after(L + "k"))
                    e.activation(tb[0:32, :], half(1, 0, 32), ACT.Square).then_inc(sem(L + "sq"), 1)
                    yield 9
                    e.wait_ge(*after(L + "ms"))
                    e.activation(lnv[:, :], half(3, 0), ACT.Ln, bias=EPS5)
                    link(e, ph + "act_chain",
                         e.activation(rk[0:32, :], half(3, 1, 32), ACT.Ln, bias=eps[0:32, 0:1]))
                    e.activation(rq[:, :], lnv[:, :], ACT.Exp, scale=-0.5, bias=ZERO)
                    e.activation(rk[0:32, :], rk[0:32, :], ACT.Exp, scale=-0.5, bias=eps[0:32, 2:3]).then_inc(sem(L + "rms"), 1)
                    yield from act_split_k(e, 11, L, 32)
                    yield from act_attend(e, 20, ph, L, True)
                    e.preload_act_table_set(LN_EXP_SET)
                if eng == "dve":
                    c = ph + "dve_chain"
                    yield from dve_norm(e, 0, ph, n, n, xn[:, :], L + "xn")
                    yield 8
                    e.wait_ge(*after(L + "sq", 2))
                    k0, k1 = seq2(half(1, 0, 32)), seq2(half(1, 1, 32))
                    e.tensor_tensor(seq2(kf[0:32, :]), k0, both(K("cos_ak", 32)), ALU.mult)
                    link(e, c, e.tensor_tensor(seq2(ta[0:32, :]), k1, both(K("sin_ak", 32)), ALU.mult))
                    link(e, c, e.tensor_tensor(kf[0:32, :], kf[0:32, :], ta[0:32, :], ALU.add))
                    yield 10
                    e.wait_ge(*after(L + "rms"))
                    e.tensor_tensor(kf[0:32, :], kf[0:32, :], rk[0:32, :], ALU.mult).then_inc(sem(L + "kf"), 1)
                    e.tensor_tensor(seq2(qf[:, :]), seq2(half(0, 0)), both(K("cos_a")), ALU.mult)
                    link(e, c, e.tensor_tensor(seq2(xc[:, :]), seq2(half(0, 1)), both(K("sin_a")), ALU.mult))
                    link(e, c, e.tensor_tensor(qf[:, :], qf[:, :], xc[:, :], ALU.add))
                    link(e, c, e.tensor_tensor(qf[:, :], qf[:, :], rq[:, :], ALU.mult))
                    dve_split_q(e, ph, L)
                    yield 12
                    e.wait_ge(*after(L + "v"))
                    dst = VX[:, :, :].rearrange("p t (g c) -> p t g c", g=4)
                    for i in range(4):
                        s = half(2, 0)[:, 0:TT * 32].rearrange("p (t g d) -> p t g d", t=TT, g=4)
                        ins = e.tensor_copy(dst[:, :, :, 40 * i:40 * i + 8], s)
                        ins.then_inc(sem(L + "vx"), 1)
                    e.memset(stat[:, 3, :], 0.0).then_inc(sem(L + "rope_done"), 1)
                    yield from dve_attend(e, 20, ph, L)
                    yield 20 + ATTEND_STEPS + 2
                    e.wait_ge(*after(L + "o"))
                    e.tensor_tensor(x[:, :], x[:, :], half(0, 0), ALU.add).then_inc(sem(L + "x"), 1)
                if eng == "pool":
                    yield from pool_split_k(e, 11, L, 32)
                    tri = K("causal")[:, 0:P].unsqueeze(1).unsqueeze(1).broadcast_to([P, 2, 2, P])
                    for n_ in range(PAIRS):
                        yield 20 + n_ + 1
                        e.wait_ge(*after(L + "exp", n_ + 1))
                        v = PR[:, n_ % 4, :, :].rearrange("p j (t k) -> p j t k", t=2)[:, :, :, 0:P]
                        e.tensor_tensor(v, v, tri, ALU.mult).then_inc(sem(L + "masked"), 1)
                if eng == "sp":
                    yield from sp_spread(e, 15, L, KV_A)

            def f_layer(e, eng, L, n, ready):
                ph = "A_"
                if eng == "pe":
                    yield from pe_norm(e, 0, ph, n, x[:, :], ready)
                    yield 6
                    e.wait_ge(*after(L + "xn"))
                    for t in range(TT):
                        ins = e.matmul(half(0, 0)[:, t * EXPERTS:(t + 1) * EXPERTS], xn[:, t * P:(t + 1) * P], W("f_r"),
                                       start=True, stop=True)
                    ins.then_inc(sem(L + "logits"), 1)
                    e.matmul(half(1, 0), W("f_base"), xn[:, :], start=True, stop=False)
                    e.matmul(half(2, 0), W("f_A"), xn[:, :], start=True, stop=True).then_inc(sem(L + "ax"), 1)
                    yield 10
                    e.wait_ge(*after(L + "spread"))
                    for t in range(TT):
                        ins = e.transpose(half(3, 0)[:, t * P:(t + 1) * P], y[:, t * P:(t + 1) * P], K("ident"))
                    ins.then_inc(sem(L + "weights_t"), 1)
                    yield 12
                    e.wait_ge(*after(L + "axw"))
                    e.matmul(half(1, 0), W("f_B"), tb[:, :], start=False, stop=True).then_inc(sem(L + "o"), 1)
                if eng == "act":
                    yield from act_norm(e, 0, ph, n, n, e=EPS5)
                    yield 7
                    e.wait_ge(*after(L + "ax"))
                    e.activation(ta[:, :], half(2, 0), ACT.Copy).then_inc(sem(L + "axs"), 1)
                    yield 8
                    e.wait_ge(*after(L + "e0"))
                    e.activation(small[:, 2, :], small[:, 1, :], ACT.Exp, bias=ZERO).then_inc(sem(L + "e1"), 1)
                if eng == "dve":
                    c = ph + "dve_chain"
                    yield from dve_norm(e, 0, ph, n, n, xn[:, :], L + "xn")
                    yield 7
                    e.wait_ge(*after(L + "logits"))
                    lg = small[:, 0, :].rearrange("p (t e) -> p t e", t=TT)

                    def by_token(ap):
                        return ap.unsqueeze(2).broadcast_to([P, TT, EXPERTS])

                    def tile(i):
                        return small[:, i, :].rearrange("p (t e) -> p t e", t=TT)

                    link(e, c, e.tensor_tensor(lg, half(0, 0)[:, 0:TT * EXPERTS].rearrange("p (t e) -> p t e", t=TT),
                                               R("f_rb").unsqueeze(1).broadcast_to([P, TT, EXPERTS]), ALU.add))
                    e.tensor_reduce(stat[:, 0, :], lg, AX_X, ALU.max)
                    for t in range(TT):
                        ins = e.max(top8[:, t, :], small[:, 0, t * EXPERTS:(t + 1) * EXPERTS])
                    link(e, c, ins)
                    e.tensor_tensor(tile(1), lg, by_token(stat[:, 0, :]), ALU.subtract).then_inc(sem(L + "e0"), 1)
                    e.tensor_tensor(tile(3), lg, top8[:, :, 1:2].broadcast_to([P, TT, EXPERTS]), ALU.is_ge)
                    yield 9
                    e.wait_ge(*after(L + "e1"))
                    link(e, c, e.tensor_copy(small[:, 5, :], small[:, 2, :]))
                    link(e, c, e.tensor_tensor(tile(4), tile(5), tile(3), ALU.mult))
                    link(e, c, e.tensor_reduce(stat[:, 1, :], tile(4), AX_X, ALU.add))
                    link(e, c, e.reciprocal(stat[:, 2, :], stat[:, 1, :]))
                    link(e, c, e.scalar_tensor_tensor(tile(6), tile(4), 2.0, by_token(stat[:, 2, :]),
                                                      ALU.mult, ALU.mult))
                    e.tensor_copy(y[:, :].rearrange("p (a r) -> p a r", r=RANK),
                                       small[:, 6, :].unsqueeze(2).broadcast_to([P, TT * EXPERTS, RANK])).then_inc(sem(L + "spread"), 1)
                    yield 11
                    e.wait_ge(*after(L + "axs"))
                    e.wait_ge(*after(L + "weights_t"))
                    e.tensor_tensor(tb[:, :], half(3, 0), ta[:, :], ALU.mult).then_inc(sem(L + "axw"), 1)
                    yield 13
                    e.wait_ge(*after(L + "o"))
                    e.scalar_tensor_tensor(x[:, :], half(1, 0), C("f_bb"), x[:, :], ALU.add, ALU.add).then_inc(sem(L + "x"), 1)

            def b_layer(e, eng, n, ready):
                ph, L = "A_", "b_"
                if eng == "pe":
                    yield from pe_norm(e, 0, ph, n, x[:, :], ready)
                    yield from pe_norm(e, 6, ph, n + 1, x1[:, :], (L + "x1",))
                    yield 12
                    e.wait_ge(*after(L + "xn"))
                    e.matmul(half(0, 0), W("b_q"), xn[:, :], start=True, stop=True)
                    e.matmul(half(0, 1), W("b_q2"), xn[:, :], start=True, stop=True).then_inc(sem(L + "q"), 1)
                    e.matmul(half(1, 0), W("b_k"), xn[:, :], start=True, stop=True)
                    e.matmul(half(1, 1), W("b_k2"), xn[:, :], start=True, stop=True).then_inc(sem(L + "k"), 1)
                    for t in range(TT):
                        ins = e.matmul(half(2, 0)[:, t * P:(t + 1) * P], xn[:, t * P:(t + 1) * P], W("b_v"),
                                       start=True, stop=True)
                    ins.then_inc(sem(L + "v"), 1)
                    yield 22
                    e.wait_ge(*after(L + "vx", 4))
                    yield from pe_scores(e, 22, L)
                    yield 23 + PAIRS
                    pe_max_rows(e, L)
                    yield from pe_attend(e, 28 + PAIRS, L, False)
                    yield 28 + PAIRS + ATTEND_STEPS + 1
                    e.wait_ge(*after(L + "y"))
                    e.matmul(half(0, 0), W("b_o"), y[:, :], start=True, stop=True).then_inc(sem(L + "o"), 1)
                if eng == "act":
                    yield from act_norm(e, 0, ph, n, n, e=EPS5)
                    yield from act_norm(e, 6, ph, n + 1, n + 1, e=EPS5)
                    yield from act_split_k(e, 14, L)
                    yield 24 + PAIRS
                    act_max_rows(e, L)
                    yield from act_attend(e, 28 + PAIRS, ph, L, False)
                if eng == "dve":
                    c = ph + "dve_chain"
                    yield from dve_norm(e, 0, ph, n, n, x1[:, :], L + "x1")
                    yield from dve_norm(e, 6, ph, n + 1, n + 1, xn[:, :], L + "xn", gamma=C("b_gamma"), beta=C("b_beta"))
                    yield 13
                    e.wait_ge(*after(L + "k"))
                    e.scalar_tensor_tensor(seq2(ta[:, :]), seq2(half(1, 0)), C("b_bk"), both(K("cos_b")), ALU.add, ALU.mult)
                    link(e, c, e.scalar_tensor_tensor(seq2(tb[:, :]), seq2(half(1, 1)), C("b_bk2"), both(K("sin_b")),
                                                      ALU.add, ALU.mult))
                    e.tensor_tensor(kf[:, :], ta[:, :], tb[:, :], ALU.add).then_inc(sem(L + "kf"), 1)
                    e.scalar_tensor_tensor(seq2(xc[:, :]), seq2(half(0, 0)), C("b_bq"), both(K("cos_b")), ALU.add, ALU.mult)
                    link(e, c, e.scalar_tensor_tensor(seq2(y[:, :]), seq2(half(0, 1)), C("b_bq2"), both(K("sin_b")),
                                                      ALU.add, ALU.mult))
                    link(e, c, e.tensor_tensor(qf[:, :], xc[:, :], y[:, :], ALU.add))
                    dve_split_q(e, ph, L)
                    yield 15
                    e.wait_ge(*after(L + "v"))
                    dve_values(e, L, 2, R("b_bv"))
                    yield from dve_max(e, 22, ph, L)
                    yield from dve_attend(e, 28 + PAIRS, ph, L)
                    yield 28 + PAIRS + ATTEND_STEPS + 2
                    e.wait_ge(*after(L + "o"))
                    link(e, c, e.scalar_tensor_tensor(ta[:, :], half(0, 0), C("b_bo"), x1[:, :], ALU.add, ALU.add))
                    e.tensor_tensor(x[:, :], x[:, :], ta[:, :], ALU.add).then_inc(sem(L + "x"), 1)
                if eng == "pool":
                    yield from pool_split_k(e, 14, L)
                if eng == "sp":
                    yield from sp_spread(e, 18, L)
                    yield from sp_max_rows(e, 25 + PAIRS, L)

            def d_layer(e, eng, n, ready):
                ph, L = "A_", "d_"
                if eng == "pe":
                    yield from pe_norm(e, 0, ph, n, x[:, :], ready)
                    yield 6
                    e.wait_ge(*after(L + "xn"))
                    e.matmul(half(0, 0), W("d_k"), xn[:, :], start=True, stop=True)
                    e.matmul(half(1, 0), W("d_v"), xn[:, :], start=True, stop=True)
                    e.matmul(half(1, 1, DH), W("d_b"), xn[:, :], start=True, stop=True).then_inc(sem(L + "kvb"), 1)
                    e.matmul(half(2, 0), W("d_q"), xn[:, :], start=True, stop=True).then_inc(sem(L + "q"), 1)
                    yield 8
                    e.wait_ge(*after(L + "sq"))
                    e.matmul(half(3, 0), K("head_sum"), sq[:, :], start=True, stop=True).then_inc(sem(L + "norm2"), 1)
                    yield 12
                    e.wait_ge(*after(L + "kvn"))
                    settle(e)
                if eng == "act":
                    yield from act_norm(e, 0, ph, n, n, e=EPS5)
                    yield 7
                    e.wait_ge(*after(L + "kvb"))
                    e.activation(sq[:, :], half(0, 0), ACT.Square).then_inc(sem(L + "sq"), 1)
                    e.activation(ta[:, :], half(1, 0), ACT.Exp, scale=-1.0, bias=ZERO)
                    e.activation(beta_sb[:, :], half(1, 1, DH), ACT.Exp, scale=-1.0, bias=eps[0:DH, 2:3]).then_inc(sem(L + "e"), 1)
                    e.wait_ge(*after(L + "q"))
                    e.activation(q_new[:, :], half(2, 0), ACT.Copy).then_inc(sem(L + "qs"), 1)
                    yield 10
                    e.wait_ge(*after(L + "norm2c"))
                    link(e, ph + "act_chain", e.activation(lnv[:, :], xc[:, :], ACT.Ln, bias=ZERO))
                    e.activation(rk[:, :], lnv[:, :], ACT.Exp, scale=-0.5, bias=ZERO).then_inc(sem(L + "rk"), 1)
                if eng == "dve":
                    c = ph + "dve_chain"
                    yield from dve_norm(e, 0, ph, n, n, xn[:, :], L + "xn")
                    yield 8
                    e.wait_ge(*after(L + "e"))
                    e.tensor_scalar(ta[:, :], ta[:, :], 1.0, None, ALU.add)
                    link(e, c, e.tensor_scalar(beta_sb[:, :], beta_sb[:, :], 1.0, None, ALU.add))
                    e.reciprocal(tb[:, :], ta[:, :])
                    link(e, c, e.reciprocal(beta_sb[:, :], beta_sb[:, :]))
                    e.tensor_tensor(v_sig[:, :], half(1, 0), tb[:, :], ALU.mult)
                    yield 9
                    e.wait_ge(*after(L + "norm2"))
                    e.tensor_scalar(xc[:, :], half(3, 0), 1e-24, None, ALU.max).then_inc(sem(L + "norm2c"), 1)
                    yield 11
                    e.wait_ge(*after(L + "rk"))
                    e.tensor_tensor(k_new[:, :], half(0, 0), rk[:, :], ALU.mult).then_inc(sem(L + "kvn"), 1)
                    e.wait_ge(*after(L + "x_out", 16))
                    settle(e)
                if eng == "sp":
                    it = turn[0]

                    def to(dram):
                        return dram.rearrange("(i b) p t -> i b p t", b=STREAMS)[it][lane]

                    yield 0
                    e.wait_ge(*after(*ready))
                    settle(e)
                    e.dma_start(to(x_dram), x[:, :]).then_inc(sem(L + "x_out"), 16)
                    yield 8
                    e.wait_ge(*after(L + "qs"))
                    settle(e)
                    e.dma_start(to(q_dram), q_new[:, :]).then_inc(sem(L + "stored"), 16)
                    yield 12
                    e.wait_ge(*after(L + "kvn"))
                    settle(e)
                    e.dma_start(to(k_dram), k_new[:, :]).then_inc(sem(L + "stored"), 16)
                    e.dma_start(to(v_dram), v_sig[:, :]).then_inc(sem(L + "stored"), 16)
                    e.dma_start(to(b_dram), beta_sb[:, :]).then_inc(sem(L + "stored"), 16)
                    yield 13
                    e.wait_ge(*after(L + "stored", 64))
                    settle(e)

            def r_layer(e, eng):
                ph, L = "C_", "r_"
                quads = G * 2

                def heads(n):
                    m = n % 4
                    i, half = m // 2, m % 2
                    return [2 * (2 * half + j) + i for j in range(2)]

                if eng == "pe":
                    yield 0
                    e.wait_ge(*after("C_readout", 16 * (3 + DH)))
                    for t in range(TT):
                        ins = e.transpose(half(3, 0)[:, t * P:(t + 1) * P], u_rows[:, t * P:(t + 1) * P], K("ident"))
                    ins.then_inc(sem(L + "u_t"), 1)
                    for m in range(quads + 1):
                        for n in (2 * m, 2 * m + 1) if m < quads else ():
                            yield 2 + n
                            b = n // 4
                            if n >= 1:
                                e.wait_ge(*after(L + "masked", n))
                            for j, h in enumerate(heads(n)):
                                for t in range(2):
                                    ins = e.matmul(ps[:, slot(n) + j, t * SEQ:(t + 1) * SEQ - t * P],
                                                   KZ[:, h, b * SEQ + t * P:b * SEQ + (t + 1) * P],
                                                   q_rows[:, b * SEQ + t * P:(b + 1) * SEQ], start=True, stop=True)
                            ins.then_inc(sem(L + "w"), 1)
                        if m == 0:
                            continue
                        yield 2 + 2 * m + 1
                        e.wait_ge(*after(L + "masked", 2 * m))
                        if m == 1:
                            e.wait_ge(*after(L + "ux", 2))
                        b, i = (m - 1) // 2, (m - 1) % 2
                        for t in range(2):
                            for g in range(4):
                                h, n = 2 * g + i, 2 * (m - 1) + g // 2
                                ins = e.matmul(ps[STRIP * g:STRIP * (g + 1), BANK + 2, b * SEQ + t * P:(b + 1) * SEQ],
                                               UX[:, 2 * b + t, h * STRIP:(h + 1) * STRIP],
                                               PRB[:, n % 4, g % 2, t * SEQ:(t + 1) * SEQ - t * P],
                                               start=(i == 0 and t == 0), stop=(i == 1 and t == 1),
                                               skip_group_check=True)
                        ins.then_inc(sem(L + "read"), 1)
                    yield from pe_norm(e, 9, ph, 0, o_rows, (L + "rows",))
                if eng == "act":
                    yield 8
                    e.wait_ge(*after(L + "read", quads))
                    e.activation(o_rows, half(2, 0), ACT.Copy).then_inc(sem(L + "rows"), 1)
                    yield from act_norm(e, 9, ph, 0, 0, e=EPS5)
                if eng == "dve":
                    c = ph + "dve_chain"
                    yield 1
                    e.wait_ge(*after(L + "u_t"))
                    dst = UX[:, :, :].rearrange("p t (g c) -> p t g c", g=4)
                    for i in range(2):
                        from_u = half(3, 0).rearrange("p (t g i d) -> p t g i d", t=TT, g=4, i=2)[:, :, :, i, :]
                        e.tensor_copy(dst[:, :, :, 48 * i:48 * i + DD], from_u).then_inc(sem(L + "ux"), 1)
                    for n in range(2 * quads):
                        yield 2 + n
                        e.wait_ge(*after(L + "w", n + 1))
                        if n >= 4:
                            e.wait_ge(*after(L + "read", (n - 4) // 2 + 1))
                        e.tensor_tensor(PRB[:, n % 4, :, 0:3 * P], ps[:, slot(n):slot(n) + 2, 0:3 * P],
                                             K("causal").unsqueeze(1).broadcast_to([P, 2, 3 * P]), ALU.mult).then_inc(sem(L + "masked"), 1)
                    yield from dve_norm(e, 9, ph, 0, 0, ta[:, :], L + "on", gamma=C("d_lnw"), beta=C("d_lnb"))
                    e.wait_ge(*after(L + "on"))
                    e.wait_ge(*after("C_readout", 16 * (3 + DH)))
                    e.tensor_tensor(x[:, :], x_next[:, :], ta[:, :], ALU.add).then_inc(sem(L + "x"), 1)


            def g_layer(e, eng, L, n, nc_n, ready):
                ph = "C_"
                q_tok = qf[:, :].rearrange("p (t h d) -> p t h d", t=TT, h=HEADS)
                kv_tok = VX[:, 0:TT // 2, :].rearrange("p a (b g c) -> p (a b) g c", b=2, g=HEADS)
                scores = VX[:, TT // 2:TT, :].rearrange("p a (b h g) -> p (a b) h g", b=2, h=HEADS)
                products = [PRB[:, 2 * i:2 * i + 2, :, :].rearrange("p a b c -> p (a b c)") for i in range(2)]

                def score_products(eng_, t):
                    return eng_.tensor_tensor(
                        products[t % 2].rearrange("p (h g d) -> p h g d", h=HEADS, g=HEADS),
                        q_tok[:, t].unsqueeze(2).broadcast_to([P, HEADS, HEADS, HD]),
                        kv_tok[:, t, :, 0:HD].unsqueeze(1).broadcast_to([P, HEADS, HEADS, HD]), ALU.mult)

                def value_products(eng_, t):
                    return eng_.tensor_tensor(
                        products[t % 2].rearrange("p (h d g) -> p h d g", h=HEADS, d=HD),
                        scores[:, t].unsqueeze(2).broadcast_to([P, HEADS, HD, HEADS]),
                        kv_tok[:, t, :, HD:2 * HD].rearrange("p g d -> p d g").unsqueeze(1)
                        .broadcast_to([P, HEADS, HD, HEADS]), ALU.mult)

                if eng == "pe":
                    yield from pe_norm(e, 0, ph, n, x[:, :], ready)
                    yield from pe_norm(e, 4, ph, n + 1, None, (L + "x1",), centered=False)
                    yield 10
                    e.wait_ge(*after(L + "xn"))
                    e.matmul(half(1, 0, LATENT), W("g_down"), xn[:, :], start=True, stop=True)
                    for t in range(TT):
                        ins = e.matmul(half(0, 0)[:, t * P:(t + 1) * P], xn[:, t * P:(t + 1) * P], W("g_q"),
                                       start=True, stop=True)
                    ins.then_inc(sem(L + "qd"), 1)
                    yield 12
                    e.wait_ge(*after(L + "down"))
                    for t in range(TT):
                        ins = e.matmul(half(2, t), tc[0:LATENT, t * P:(t + 1) * P],
                                       W("g_up", rows_=LATENT), start=True, stop=True)
                    ins.then_inc(sem(L + "kv"), 1)
                    yield 21
                    e.wait_ge(*after(L + "heads"))
                    for t in range(TT):
                        ins = e.transpose(half(3, 0)[:, t * P:(t + 1) * P], y[:, t * P:(t + 1) * P], K("ident"))
                    ins.then_inc(sem(L + "heads_t"), 1)
                    yield 23
                    e.wait_ge(*after(L + "y"))
                    e.matmul(half(1, 0), W("g_o"), ta[:, :], start=True, stop=True).then_inc(sem(L + "o"), 1)
                    yield from pe_norm(e, 23, ph, n + 2, None, (L + "x2",), centered=False)
                    yield 29
                    e.wait_ge(*after(L + "xm"))
                    for t in range(TT):
                        ins = e.matmul(half(3, 0)[:, t * EXPERTS:(t + 1) * EXPERTS], xn[:, t * P:(t + 1) * P], W("g_g"),
                                       start=True, stop=True)
                    ins.then_inc(sem(L + "logits"), 1)
                    for t in range(TT):
                        if t == 1:
                            yield 31
                            e.wait_ge(*after(L + "e0"))
                        for c in range(2):
                            ins = e.matmul(ps[:, turns_of_two(t) + c, :], xn[:, t * P:(t + 1) * P],
                                           W("g_e", c * 512, (c + 1) * 512), start=True, stop=True)
                        ins.then_inc(sem(L + "experts"), 1)
                    yield 36
                    e.wait_ge(*after(L + "mixed", TT))
                    for t in range(TT):
                        ins = e.transpose(half(2, 0)[:, t * P:(t + 1) * P], y[:, t * P:(t + 1) * P], K("ident"))
                    ins.then_inc(sem(L + "mixed_t"), 1)
                if eng == "act":
                    yield from act_norm(e, 0, ph, n, nc_n, e=EPS5)
                    yield from act_norm(e, 4, ph, n + 1, None, src=x1[:, :], ready=(L + "x1",), e=EPS6)
                    yield 11
                    e.wait_ge(*after(L + "qd"))
                    e.activation(tc[0:LATENT, :], half(1, 0, LATENT), ACT.Identity, bias=C("g_bdown", rows_=LATENT)).then_inc(sem(L + "down"), 1)
                    yield 17
                    e.wait_ge(*after(L + "shifted"))
                    e.activation(scores, scores, ACT.Exp, scale=float(HD) ** -0.5, bias=ZERO).then_inc(sem(L + "exp"), 1)
                    yield 22
                    e.wait_ge(*after(L + "heads_t"))
                    e.activation(ta[:, :], half(3, 0), ACT.Copy).then_inc(sem(L + "y"), 1)
                    yield from act_norm(e, 23, ph, n + 2, None, src=x1[:, :], ready=(L + "x2",), e=EPS6)
                    yield 31
                    e.wait_ge(*after(L + "e0"))
                    e.activation(small[:, 2, :], small[:, 1, :], ACT.Exp, bias=ZERO).then_inc(sem(L + "e1"), 1)
                if eng == "dve":
                    c = ph + "dve_chain"
                    yield from dve_norm(e, 0, ph, n, nc_n, x1[:, :], L + "x1")
                    e.wait_ge(*after(L + "x1"))
                    yield from dve_norm(e, 4, ph, n + 1, None, xn[:, :], L + "xn", src=x1[:, :], gamma=C("g_gamma1"))
                    yield 11
                    e.wait_ge(*after(L + "qd"))
                    e.tensor_tensor(qf[:, :].rearrange("p (t c) -> p t c", t=TT),
                                    half(0, 0).rearrange("p (t c) -> p t c", t=TT),
                                    R("g_bq").unsqueeze(1).broadcast_to([P, TT, P]), ALU.add)
                    yield 13
                    e.wait_ge(*after(L + "kv"))
                    e.tensor_tensor(VX[:, 0:TT // 2, :].rearrange("p a (b c) -> p (a b) c", b=2),
                                         ps[:, BANK + 2:BANK + 3, :].rearrange("p a (b c) -> p (a b) c", b=2),
                                         R("g_bup").unsqueeze(1).broadcast_to([P, TT, 2 * P]), ALU.add).then_inc(sem(L + "qkv"), 1)
                    yield 14
                    e.wait_ge(*after(L + "qkv"))

                    def sums(t, products_of, out_, sig):
                        if t % 2 == 0:
                            if t:
                                e.wait_ge(*after(sig, t - 1))
                            link(e, c, products_of(e, t))
                        else:
                            e.wait_ge(*after(sig + "_odd", (t + 1) // 2))
                        e.tensor_reduce(out_, products[t % 2].rearrange("p (a b) -> p a b", a=out_.shape[1]),
                                             AX_X, ALU.add).then_inc(sem(sig), 1)

                    for t in range(TT):
                        yield 14 + t
                        sums(t, score_products, scores[:, t].rearrange("p h g -> p (h g)"), L + "score")
                    yield 16
                    e.wait_ge(*after(L + "score", TT))
                    all_heads = scores.rearrange("p t h g -> p (t h) g")
                    link(e, c, e.tensor_reduce(small[:, 4:6, :].rearrange("p a b -> p (a b)"), all_heads, AX_X, ALU.max))
                    e.tensor_tensor(all_heads, all_heads,
                                         small[:, 4:6, :].rearrange("p a b -> p (a b)").unsqueeze(2)
                                         .broadcast_to([P, TT * HEADS, HEADS]), ALU.subtract).then_inc(sem(L + "shifted"), 1)
                    yield 18
                    e.wait_ge(*after(L + "exp"))
                    link(e, c, e.tensor_reduce(small[:, 6:8, :].rearrange("p a b -> p (a b)"), all_heads, AX_X, ALU.add))
                    link(e, c, e.reciprocal(small[:, 4:6, :], small[:, 6:8, :]))
                    for t in range(TT):
                        yield 18 + t
                        sums(t, value_products, y[:, t * P:(t + 1) * P], L + "value")
                    yield 20
                    e.wait_ge(*after(L + "value", TT))
                    heads = y[:, :].rearrange("p (a d) -> p a d", d=HD)
                    e.tensor_tensor(heads, heads, small[:, 4:6, :].rearrange("p a b -> p (a b)").unsqueeze(2)
                                         .broadcast_to([P, TT * HEADS, HD]), ALU.mult).then_inc(sem(L + "heads"), 1)
                    yield 24
                    e.wait_ge(*after(L + "o"))
                    e.scalar_tensor_tensor(x1[:, :], half(1, 0), C("g_bo"), x1[:, :], ALU.add, ALU.add).then_inc(sem(L + "x2"), 1)
                    e.wait_ge(*after(L + "x2"))
                    yield from dve_norm(e, 23, ph, n + 2, None, xn[:, :], L + "xm", src=x1[:, :], gamma=C("g_gamma2"))
                    e.tensor_tensor(x[:, :], x[:, :], x1[:, :], ALU.add)
                    yield 30
                    e.wait_ge(*after(L + "logits"))

                    def by_token(ap):
                        return ap.unsqueeze(2).broadcast_to([P, TT, EXPERTS])

                    def tile(i):
                        return small[:, i, :].rearrange("p (t e) -> p t e", t=TT)

                    link(e, c, e.tensor_tensor(tile(0), half(3, 0)[:, 0:TT * EXPERTS].rearrange("p (t e) -> p t e", t=TT),
                                               R("g_bg").unsqueeze(1).broadcast_to([P, TT, EXPERTS]), ALU.add))
                    link(e, c, e.tensor_reduce(stat[:, 0, :], tile(0), AX_X, ALU.max))
                    e.tensor_tensor(tile(1), tile(0), by_token(stat[:, 0, :]), ALU.subtract).then_inc(sem(L + "e0"), 1)
                    yield 32
                    e.wait_ge(*after(L + "e1"))
                    link(e, c, e.tensor_reduce(stat[:, 1, :], tile(2), AX_X, ALU.add))
                    link(e, c, e.reciprocal(stat[:, 2, :], stat[:, 1, :]))
                    link(e, c, e.tensor_tensor(tile(3), tile(2), by_token(stat[:, 2, :]), ALU.mult))
                    for t in range(TT):
                        yield 33 + t
                        e.wait_ge(*after(L + "experts", t + 1))
                        if t:
                            e.wait_ge(*after(L + "mixed", t))
                        ins = e.tensor_tensor(prod, ps[:, turns_of_two(t):turns_of_two(t) + 2, :].rearrange("p c (e f) -> p (c e) f", e=4),
                                              tile(3)[:, t, :].unsqueeze(2).broadcast_to([P, EXPERTS, P]), ALU.mult)
                        ins.then_inc(sem(L + "gated"), 1)
                        e.wait_ge(*after(L + "gated", t + 1))
                        e.tensor_reduce(y[:, t * P:(t + 1) * P], prod.rearrange("p e f -> p f e"), AX_X, ALU.add).then_inc(sem(L + "mixed"), 1)
                    yield 37
                    e.wait_ge(*after(L + "mixed_t"))
                    e.tensor_tensor(x[:, :], x[:, :], half(2, 0), ALU.add).then_inc(sem(L + "x"), 1)
                if eng == "pool":
                    yield 14
                    e.wait_ge(*after(L + "qkv"))
                    score_products(e, 1).then_inc(sem(L + "score_odd"), 1)
                    yield 18
                    e.wait_ge(*after(L + "exp"))
                    value_products(e, 1).then_inc(sem(L + "value_odd"), 1)

            def h_layer(e, eng, n, nc_n, ready):
                ph, L = "C_", "h_"
                if eng == "pe":
                    yield from pe_norm(e, 0, ph, n, x[:, :], ready)
                    yield 6
                    e.wait_ge(*after(L + "xn"))
                    for i in range(4):
                        ins = e.matmul(half(i // 2, i % 2, HH), W("h_proj", i * HH, (i + 1) * HH), xn[:, :], start=True, stop=True)
                    ins.then_inc(sem(L + "proj"), 1)
                    yield 9
                    e.wait_ge(*after(L + "conv", 2))
                    for name, bank in (("h_gate", 2), ("h_in", 3)):
                        for o in range(2):
                            for k in range(2):
                                ins = e.matmul(half(bank, o, HH),
                                               W(name, k * HID + o * HH, k * HID + (o + 1) * HH, HH), h_u[:, k, :],
                                               start=(k == 0), stop=(k == 1))
                        ins.then_inc(sem(L + "gates"), 1)
                    yield 16
                    e.wait_ge(*after(L + "m"))
                    for k in range(2):
                        ins = e.matmul(half(0, 0), W("h_out", k * P, (k + 1) * P, HH), h_gelu[:, k, :],
                                       start=(k == 0), stop=(k == 1))
                    ins.then_inc(sem(L + "o"), 1)
                if eng == "act":
                    yield from act_norm(e, 0, ph, n, nc_n, e=EPS5)
                    yield 7
                    e.wait_ge(*after(L + "proj"))
                    e.activation(u_pad[:, :, :, TAPS - 1:], ps[0:HH, BANK + 1, :].rearrange("p (a b t) -> p a b t", a=2, b=G),
                                      ACT.Copy).then_inc(sem(L + "pad"), 1)
                    e.activation(h_gelu, ps[0:HH, BANK, :].rearrange("p (a t) -> p a t", a=2), ACT.Gelu).then_inc(sem(L + "gelu"), 1)
                    e.preload_act_table_set(LN_EXP_SET)
                    yield 10
                    e.wait_ge(*after(L + "gates", 1))
                    for o in range(2):
                        ins = e.activation(h_sig_rec[:, o, :], half(2, o, HH), ACT.Exp, scale=-1.0,
                                           bias=neg_bias[0:HH, 2 + o:3 + o])
                    ins.then_inc(sem(L + "exps"), 1)
                    e.wait_ge(*after(L + "gates", 2))
                    for o in range(2):
                        ins = e.activation(h_sig_in[:, o, :], half(3, o, HH), ACT.Exp, scale=-1.0,
                                           bias=neg_bias[0:HH, o:o + 1])
                    ins.then_inc(sem(L + "exps"), 1)
                    yield 12
                    e.wait_ge(*after(L + "sig_rec"))
                    for o in range(2):
                        ins = e.activation(h_alpha[:, o, :], h_sig_rec[:, o, :], ACT.Exp, scale=decay[0:HH, o:o + 1],
                                           bias=eps[0:HH, 2:3])
                    ins.then_inc(sem(L + "alpha"), 1)
                    yield 14
                    e.wait_ge(*after(L + "one_less"))
                    link(e, ph + "act_chain", e.activation(h_beta, h_beta, ACT.Ln, bias=eps[0:HH, 1:2]))
                    e.activation(h_beta, h_beta, ACT.Exp, scale=0.5, bias=eps[0:HH, 2:3]).then_inc(sem(L + "beta"), 1)
                if eng == "dve":
                    c = ph + "dve_chain"
                    yield from dve_norm(e, 0, ph, n, nc_n, xn[:, :], L + "xn")
                    yield 8
                    e.wait_ge(*after(L + "pad"))
                    for k in range(TAPS):
                        for o in range(2):
                            src, dst = u_pad[:, o, :, k:k + SEQ], seq2(h_u[:, o, :])
                            tap = C("h_conv", o * TAPS + k, HH)
                            if k == 0:
                                ins = e.tensor_scalar(dst, src, tap, C("h_cb", o, HH), ALU.mult, ALU.add)
                            else:
                                ins = e.scalar_tensor_tensor(dst, src, tap, dst, ALU.mult, ALU.add)
                            if k == TAPS - 1:
                                ins.then_inc(sem(L + "conv"), 1)
                        if k < TAPS - 1:
                            link(e, c, ins)
                    yield 11
                    e.wait_ge(*after(L + "exps", 1))
                    link(e, c, e.tensor_scalar(h_sig_rec, h_sig_rec, 1.0, None, ALU.add))
                    e.reciprocal(h_sig_rec, h_sig_rec).then_inc(sem(L + "sig_rec"), 1)
                    yield 12
                    e.wait_ge(*after(L + "exps", 2))
                    link(e, c, e.tensor_scalar(h_sig_in, h_sig_in, 1.0, None, ALU.add))
                    link(e, c, e.reciprocal(h_sig_in, h_sig_in))
                    link(e, c, e.tensor_tensor(h_sig_in, h_sig_in, h_u, ALU.mult))
                    yield 13
                    e.wait_ge(*after(L + "alpha"))
                    link(e, c, e.tensor_tensor(h_beta, h_alpha, h_alpha, ALU.mult))
                    e.tensor_scalar(h_beta, h_beta, -1.0, 1.0, ALU.mult, ALU.add).then_inc(sem(L + "one_less"), 1)
                    yield 15
                    e.wait_ge(*after(L + "beta"))
                    link(e, c, e.tensor_tensor(h_beta, h_beta, h_sig_in, ALU.mult))
                    for o in range(2):
                        for b in range(G):
                            s = slice(b * SEQ, (b + 1) * SEQ)
                            ins = e.tensor_tensor_scan(h_u[:, o, s], h_alpha[:, o, s], h_beta[:, o, s], 0.0,
                                                       ALU.mult, ALU.add)
                    link(e, c, ins)
                    e.tensor_tensor(h_gelu, h_gelu, h_u, ALU.mult).then_inc(sem(L + "m"), 1)
                    yield 17
                    e.wait_ge(*after(L + "o"))
                    e.tensor_tensor(x[:, :], x[:, :], half(0, 0), ALU.add).then_inc(sem(L + "x"), 1)

            def out_layer(e, eng, ready):
                if eng == "pe":
                    yield 0
                    e.wait_ge(*after(*ready))
                    for t in range(TT):
                        ins = e.transpose(half(1, 0)[:, t * P:(t + 1) * P], x[:, t * P:(t + 1) * P], K("ident"))
                    ins.then_inc(sem("C_out_t"), 1)
                    yield 2
                    e.wait_ge(*after("C_out"))
                    settle(e)
                if eng == "act":
                    yield 1
                    e.wait_ge(*after("C_out_t"))
                    e.wait_ge(*after("C_stored", 0))
                    e.activation(x_tok[:, :, :].rearrange("p t d -> p (t d)"), half(1, 0), ACT.Copy).then_inc(sem("C_out"), 1)
                if eng == "sp":
                    yield 2
                    e.wait_ge(*after("C_out"))
                    settle(e)
                    e.dma_start(out.rearrange("(i s t p) d -> i s p t d", s=STREAMS, t=TT, p=P)[turn[0]][lane], x_tok[:, :, :]).then_inc(sem("C_stored"), 16)
                    yield 4
                    e.wait_ge(*after("C_stored", 16))
                    settle(e)

            def load_tokens(sp, i):
                sp.dma_start(x_tok[:, :, :], x_in.rearrange("(i s t p) d -> i s p t d", s=STREAMS, t=TT, p=P)[i][lane])\
                    .then_inc(sem("A_tokens"), 16)

            def load_readout(sp, i):
                def of(dram):
                    return dram.rearrange("(i b) p t -> i b p t", b=STREAMS)[i][lane]

                sp.dma_start(u_rows, of(u_dram)).then_inc(sem("C_readout"), 16)
                sp.dma_start(q_rows, of(q_dram)).then_inc(sem("C_readout"), 16)
                sp.dma_start(x_next[:, :], of(x_dram)).then_inc(sem("C_readout"), 16)
                for h in range(DH):
                    rows_ = slice(DD * h, DD * (h + 1))
                    sp.dma_start(KZ[rows_, h, :], of(k_dram)[rows_]).then_inc(sem("C_readout"), 16)

            def load_layer(e, eng):
                if eng == "pe":
                    yield 0
                    e.wait_ge(*after("A_tokens", 16))
                    for t in range(TT):
                        ins = e.transpose(half(0, 0)[:, t * P:(t + 1) * P], x_tok[:, t, :], K("ident"))
                    ins.then_inc(sem("A_x_t"), 1)
                if eng == "dve":
                    yield 1
                    e.wait_ge(*after("A_x_t"))
                    e.tensor_copy(x[:, :], half(0, 0)).then_inc(sem("A_x"), 1)
                if eng == "sp":
                    yield 1
                    e.wait_ge(*after("A_x_t"))
                    settle(e)
                    load_tokens(e, (turn[0] + 1) % TURNS)

            def prefetch_layer(e, eng):
                if eng == "sp":
                    yield 0
                    e.wait_ge(*after("r_x"))
                    settle(e)
                    load_readout(e, (turn[0] + 1) % TURNS)

            def in_turn(*layers_):
                at = 0
                for steps, layer in layers_:
                    for step in layer:
                        assert step < steps
                        yield at + step
                    at += steps

            def front(e, eng):
                return in_turn((2, load_layer(e, eng)), (A_STEPS, a_layer(e, eng, 0)),
                               (F_STEPS, f_layer(e, eng, "f1_", 1, ("a_x",))), (B_STEPS, b_layer(e, eng, 2, ("f1_x",))),
                               (F_STEPS, f_layer(e, eng, "f2_", 4, ("b_x",))), (D_STEPS, d_layer(e, eng, 5, ("f2_x",))))

            def back(e, eng):
                return in_turn((R_STEPS, r_layer(e, eng)), (1, prefetch_layer(e, eng)),
                               (G_STEPS, g_layer(e, eng, "g1_", 1, 1, ("r_x",))),
                               (H_STEPS, h_layer(e, eng, 4, 2, ("g1_x",))),
                               (G_STEPS, g_layer(e, eng, "g2_", 5, 3, ("h_x",))), (OUT_STEPS, out_layer(e, eng, ("g2_x",))))

            return Stream(front=front, back=back, load_tokens=load_tokens, load_readout=load_readout,
                          sem=sem, zeroed=(KZ, u_pad), UX=UX, VX=VX)

        streams = [stream(lane) for lane in range(STREAMS)]

        def begin(n=0):
            turn[0] = n
            for chain in chains:
                chain.clear()

        def side_by_side(programs):
            due = [next(program, None) for program in programs]
            step = 0
            while any(d is not None for d in due):
                for lane, program in enumerate(programs):
                    while due[lane] is not None and due[lane] + lane * LAG <= step:
                        due[lane] = next(program, None)
                step += 1

        def loop(e, half, eng):
            with e.Fori(0, TURNS) as it:
                begin(it)
                if half == "front":
                    side_by_side([st.front(e, eng) for st in streams])
                else:
                    side_by_side([st.back(e, eng) for st in streams])
            begin()

        block = ctx.enter_context(nc.Block())

        @block.sync
        def _(sp):
            for dst, src in ((w_sb, weights), (col_sb, columns), (const_sb, consts)):
                sp.dma_start(dst[:, :], src).then_inc(sem("params"), 16)
            sp.dma_start(row_sb[:, :], rows.partition_broadcast(P)).then_inc(sem("params"), 16)
            for st in streams:
                st.load_tokens(sp, 0)
            loop(sp, "front", "sp")
            for st in streams:
                sp.wait_ge(st.sem("A_tokens"), 16 * (TURNS + 1))
            for j in range(2):
                for dst, src in ((scan_k, k_dram), (scan_v, v_dram)):
                    sp.dma_start(dst[:, j, :, :], src.rearrange("(j b) (h d) t -> j (b h) d t", j=2, h=DH)[j])\
                        .then_inc(sem("scan_loaded"), 16)
                sp.dma_start(scan_b[:, j, :], b_dram.rearrange("(j b) h t -> j (b h) t", j=2)[j])\
                    .then_inc(sem("scan_loaded"), 16)
            sp.wait_ge(sem("scanned"), 1)
            for j in range(2):
                sp.dma_start(u_dram.rearrange("(j b) (h d) t -> j (b h) d t", j=2, h=DH)[j], scan_v[:, j, :, :])\
                    .then_inc(sem("updates_stored"), 16)
            sp.wait_ge(sem("updates_stored"), 32)
            sp.wait_ge(sem("zeroed"), 1)
            for st in streams:
                st.load_readout(sp, 0)
            loop(sp, "back", "sp")
            for st in streams:
                sp.wait_ge(st.sem("C_readout"), 16 * (3 + DH) * (TURNS + 1))

        @block.tensor
        def _(pe):
            pe.wait_ge(sem("params"), 64)
            pe.wait_ge(sem("ready"), 6 + 2 * STREAMS)
            loop(pe, "front", "pe")
            loop(pe, "back", "pe")

        @block.scalar
        def _(act):
            act.wait_ge(sem("params"), 64)
            act.wait_ge(sem("ready"), 6 + 2 * STREAMS)
            act.preload_act_table_set(LN_EXP_SET)
            act.activation(dec_t[:, 0:2], col_sb[:, C_AT["h_lambda"][0]:C_AT["h_lambda"][0] + 2], ACT.Abs)\
                .then_inc(sem("softplus"), 1)
            act.wait_ge(sem("softplus"), 1)
            act.activation(dec_t[:, 2:4], dec_t[:, 0:2], ACT.Exp, scale=-1.0, bias=ZERO).then_inc(sem("softplus"), 1)
            act.wait_ge(sem("softplus"), 2)
            act.activation(dec_t[:, 4:6], dec_t[:, 2:4], ACT.Ln, bias=eps[:, 3:4]).then_inc(sem("softplus"), 1)
            loop(act, "front", "act")
            loop(act, "back", "act")

        @block.gpsimd
        def _(pool):
            pool.memset(bands[:, 0], 0.0).then_inc(sem("ready"), 1)
            for st in streams:
                pool.memset(st.VX[:, :, :], 0.0).then_inc(sem("ready"), 1)
                pool.memset(st.UX[:, :, :], 0.0).then_inc(sem("ready"), 1)
            loop(pool, "front", "pool")
            loop(pool, "back", "pool")

        @block.vector
        def _(dve):
            for i in range(1, 2 * STREAMS):
                ins = dve.memset(bands[:, i], 0.0)
            ins.then_inc(sem("k_zeroed"), 1)
            dve.memset(eps[:, 0:1], 1e-5).then_inc(sem("ready"), 1)
            dve.memset(eps[:, 1:2], 1e-6).then_inc(sem("ready"), 1)
            dve.memset(eps[:, 2:3], 0.0)
            dve.memset(eps[:, 3:4], 1.0).then_inc(sem("ready"), 1)
            dve.wait_ge(sem("k_zeroed"), 1)
            for lane in range(STREAMS):
                ins = dve.memset(bands[SHIFT_ROW:P, 2 * lane + 1], 1.0)
            ins.then_inc(sem("ready"), 1)
            dve.wait_ge(sem("params"), 64)
            dve.tensor_copy(ident_b[:, :], K("ident")).then_inc(sem("ready"), 1)
            lam = C_AT["h_lambda"][0]
            dve.tensor_scalar(dec_t[:, 6:8], col_sb[:, lam:lam + 2], 0.0, None, ALU.max).then_inc(sem("dec"), 1)
            dve.wait_ge(sem("softplus"), 3)
            dve.wait_ge(sem("dec"), 1)
            dve.tensor_tensor(dec_t[:, 6:8], dec_t[:, 6:8], dec_t[:, 4:6], ALU.add).then_inc(sem("dec"), 1)
            dve.wait_ge(sem("dec"), 2)
            dve.tensor_scalar(decay[:, :], dec_t[:, 6:8], -8.0, None, ALU.mult).then_inc(sem("dec"), 1)
            b_in = C_AT["h_bin"][0]
            dve.tensor_scalar(neg_bias[:, :], col_sb[:, b_in:b_in + 4], -1.0, None, ALU.mult).then_inc(sem("dec"), 1)
            loop(dve, "front", "dve")

            dve.memset(state[:, :, :, :], 0.0).then_inc(sem("scan_step"), 1)
            dve.wait_ge(sem("scan_loaded"), 96)
            with dve.Fori(0, SEQ) as t:
                def along(ap, axis):
                    return ap.unsqueeze(axis).broadcast_to([P, 2, DD, DD])

                k_t = scan_k[:, :, :, bass.ds(t, 1)].rearrange("p j d o -> p j (d o)")
                v_t = scan_v[:, :, :, bass.ds(t, 1)].rearrange("p j d o -> p j (d o)")
                b_t = scan_b[:, :, bass.ds(t, 1)].broadcast_to([P, 2, DD])
                done_before = t * SCAN_STEPS + 1
                dve.wait_ge(sem("scan_step"), done_before)
                dve.tensor_tensor(outer[:, :, :, :], state[:, :, :, :], along(k_t, 2), ALU.mult)\
                    .then_inc(sem("scan_step"), 1)
                dve.wait_ge(sem("scan_step"), done_before + 1)
                dve.tensor_reduce(s_k[:, :, :], outer[:, :, :, :], AX_X, ALU.add).then_inc(sem("scan_step"), 1)
                dve.wait_ge(sem("scan_step"), done_before + 2)
                dve.tensor_tensor(s_k[:, :, :], v_t, s_k[:, :, :], ALU.subtract).then_inc(sem("scan_step"), 1)
                dve.wait_ge(sem("scan_step"), done_before + 3)
                dve.tensor_tensor(v_t, s_k[:, :, :], b_t, ALU.mult).then_inc(sem("scan_step"), 1)
                dve.wait_ge(sem("scan_step"), done_before + 4)
                dve.tensor_tensor(outer[:, :, :, :], along(v_t, 3), along(k_t, 2), ALU.mult)\
                    .then_inc(sem("scan_step"), 1)
                dve.wait_ge(sem("scan_step"), done_before + 5)
                dve.tensor_tensor(state[:, :, :, :], state[:, :, :, :], outer[:, :, :, :], ALU.add)\
                    .then_inc(sem("scan_step"), 1)
            dve.wait_ge(sem("scan_step"), SEQ * SCAN_STEPS + 1)
            dve.tensor_copy(s_k[:, :, :], state[:, :, 0, :]).then_inc(sem("scanned"), 1)
            dve.wait_ge(sem("updates_stored"), 32)
            for st in streams:
                for ap in st.zeroed:
                    ins = dve.memset(ap, 0.0)
            ins.then_inc(sem("zeroed"), 1)
            loop(dve, "back", "dve")


def layouts(a):
    def heads_last(w):
        n = w.shape[-1] // HD
        return w.reshape(w.shape[:-1] + (n, HD)).swapaxes(-1, -2).reshape(w.shape)

    def partner(w, order):
        n = w.shape[-1] // HD
        return w.reshape(w.shape[:-1] + (n, HD))[..., order].reshape(w.shape)

    half = [4, 5, 6, 7, 0, 1, 2, 3]
    inter = [1, 0, 3, 2, 4, 5, 6, 7]
    wi, bi = a["L0_attn_b_W_in"], a["L0_attn_b_b_in"]
    w = dict(
        a_q=heads_last(a["L0_attn_a_w_q"]), a_q2=heads_last(partner(a["L0_attn_a_w_q"], half)),
        a_k=heads_last(a["L0_attn_a_w_k"]), a_k2=heads_last(partner(a["L0_attn_a_w_k"], half)),
        a_v=a["L0_attn_a_w_v"], a_o=a["L0_attn_a_w_o"],
        f_base=a["L0_ffn_base_w"].T, f_A=a["L0_ffn_lora_A"].transpose(1, 0, 2).reshape(P, -1),
        f_B=a["L0_ffn_lora_B"].reshape(-1, P), f_r=a["L0_ffn_router_w"].T,
        b_q=heads_last(wi[:, :P]), b_q2=heads_last(partner(wi[:, :P], inter)),
        b_k=heads_last(wi[:, P:2 * P]), b_k2=heads_last(partner(wi[:, P:2 * P], inter)),
        b_v=wi[:, 2 * P:], b_o=a["L0_attn_b_W_out"],
        d_q=a["L1_attn_a_Wq"], d_k=a["L1_attn_a_Wk"], d_v=a["L1_attn_a_Wv"], d_b=a["L1_attn_a_Wb"],
        g_q=a["L1_ffn_Wq"], g_down=a["L1_ffn_Wdown"], g_up=a["L1_ffn_Wup"],
        g_o=a["L1_ffn_Wo"], g_g=a["L1_ffn_Wg"], g_e=a["L1_ffn_We"].transpose(1, 0, 2).reshape(P, -1),
        h_proj=a["L1_attn_b_W_proj"].T,
        h_in=a["L1_attn_b_W_in"].T.reshape(2, HH, HID).transpose(1, 0, 2).reshape(HH, -1),
        h_gate=a["L1_attn_b_W_gate"].T.reshape(2, HH, HID).transpose(1, 0, 2).reshape(HH, -1),
        h_out=a["L1_attn_b_W_out"].T.reshape(2, HH, P).transpose(1, 0, 2).reshape(HH, -1))

    def halves(v):
        return v.reshape(2, HH, -1).transpose(1, 0, 2).reshape(HH, -1)

    c = dict(
        f_bb=a["L0_ffn_base_b"], b_bq=heads_last(bi[:P]), b_bq2=heads_last(partner(bi[:P], inter)),
        b_bk=heads_last(bi[P:2 * P]), b_bk2=heads_last(partner(bi[P:2 * P], inter)),
        b_bo=a["L0_attn_b_b_out"], b_gamma=a["L0_attn_b_gamma"], b_beta=a["L0_attn_b_beta"],
        d_lnw=a["L1_attn_a_ln_w"], d_lnb=a["L1_attn_a_ln_b"], g_gamma1=a["L1_ffn_gamma1"],
        g_bdown=a["L1_ffn_bdown"],
        g_bo=a["L1_ffn_bo"], g_gamma2=a["L1_ffn_gamma2"],
        h_conv=halves(a["L1_attn_b_conv_w"].reshape(HID, TAPS)), h_cb=halves(a["L1_attn_b_conv_b"]),
        h_bin=halves(a["L1_attn_b_b_in"]), h_bgate=halves(a["L1_attn_b_b_gate"]),
        h_lambda=halves(a["L1_attn_b_forget_lambda"]))
    r = dict(f_rb=a["L0_ffn_router_b"], b_bv=bi[2 * P:], g_bq=a["L1_ffn_bq"], g_bup=a["L1_ffn_bup"], g_bg=a["L1_ffn_bg"])

    def pack(table, parts):
        at, n = offsets(table)
        out = np.zeros((P, n), np.float32)
        for name, (lo, m) in at.items():
            v = np.asarray(parts[name])
            v = v.reshape(v.shape[0], -1)
            out[0:v.shape[0], lo:lo + m] = v
        return out

    row = np.concatenate([np.asarray(r[name]) for name in ROWS]).astype(np.float32)
    return pack(WEIGHTS, w), pack(COLUMNS, c), row


def constants():
    i = np.arange(P)
    pos = np.arange(SEQ, dtype=np.float32)

    def rotary(freq, sign, heads):
        cos = np.ones((HD, SEQ), np.float32)
        sin = np.zeros((HD, SEQ), np.float32)
        for d in range(HD):
            if freq[d] is not None:
                cos[d], sin[d] = np.cos(pos * freq[d]), sign[d] * np.sin(pos * freq[d])
        return np.repeat(cos, heads, 0), np.repeat(sin, heads, 0)

    fa = (1.0 / np.float32(10000.0) ** (np.arange(0, HD, 2, dtype=np.float32) / HD)).astype(np.float32)
    fb = (1.0 / np.float32(10000.0) ** (np.arange(0, 4, 2, dtype=np.float32) / 4)).astype(np.float32)
    sa = [-1] * 4 + [1] * 4
    cos_a, sin_a = rotary(list(fa) + list(fa), sa, HEADS)
    cos_ak, sin_ak = rotary(list(fa) + list(fa), sa, KV_A)
    cos_b, sin_b = rotary([fb[0], fb[0], fb[1], fb[1]] + [None] * 4, [-1, 1, -1, 1] + [0] * 4, HEADS)
    tri = (i[:, None] <= i[None, :]).astype(np.float32)
    den = np.zeros((P, 4, STRIP), np.float32)
    for n in range(4):
        den[:, n, HD * n:HD * n + HD] = 1.0
    j = np.arange(KV_A * HD)
    parts = dict(
        ident=np.eye(P), center=np.eye(P) - 1.0 / P, mean=np.full((P, P), 1.0 / P),
        head_mean=(i[:, None] % HEADS == i[None, :] % HEADS) / HD,
        kv_mean=(j[:, None] % KV_A == j[None, :] % KV_A) / HD,
        head_sum=(i[:, None] // DD == i[None, :] // DD),
        cos_a=cos_a, sin_a=sin_a, cos_ak=cos_ak, sin_ak=sin_ak, cos_b=cos_b, sin_b=sin_b,
        causal=np.concatenate([tri, np.ones((P, P)), tri], 1), den=den.reshape(P, -1))
    at, n = offsets(CONSTS)
    out = np.zeros((P, n), np.float32)
    for name, (lo, m) in at.items():
        v = parts[name]
        out[0:v.shape[0], lo:lo + m] = v
    return out


def kernel(**inputs):
    import concourse.bacc as bacc
    from concourse.bass_utils import run_bass_kernel_spmd

    a = {k: np.asarray(v) for k, v in inputs.items()}
    w, c, r = layouts(a)
    arrays = dict(x_dram_in=np.ascontiguousarray(a["L0_attn_a_x"]).reshape(SEQS * SEQ, P),
                  weights_dram=w, columns_dram=c, rows_dram=r, consts_dram=constants())
    nc = bacc.Bacc("TRN2", target_bir_lowering=False, num_devices=1)
    args = [nc.dram_tensor(n, v.shape, mybir.dt.from_np(v.dtype), kind="ExternalInput").ap()
            for n, v in arrays.items()]
    out = nc.dram_tensor("out_dram", (SEQS * SEQ, P), F32, kind="ExternalOutput").ap()
    build(nc, *args, out)
    got = run_bass_kernel_spmd(nc, [arrays], core_ids=[0]).results[0]["out_dram"]
    return got.reshape(SEQS, SEQ, P)
```

```python
from collections import namedtuple
from contextlib import ExitStack

import numpy as np

import concourse.bass as bass
from concourse import mybir

F32 = mybir.dt.float32
BF16 = mybir.dt.bfloat16
ALU = mybir.AluOpType
ACT = mybir.ActivationFunctionType
AX_X = mybir.AxisListType.X
LN_EXP_SET = "natural_log_exp_and_others"

P = 128
SEQS, SEQ = 32, 256
STREAMS = 2
G = 1
TOK = G * SEQ
TT = TOK // P
TURNS = SEQS // (G * STREAMS)
HEADS, HD = 16, 8
KV_A = 4
DH, DD = 8, 16
EXPERTS = 8
RANK = 16
LATENT = 64
HID, HH = 192, 96
TAPS = 4
PARTS = 3
Q_BANDS = ((0, 0, 3), (3, 1, 2), (5, 2, 1))
K_BANDS = ((0, 0, 3), (3, 0, 2), (5, 0, 1))
SHIFT_ROW = 96
SROWS = SHIFT_ROW + PARTS
PAIRS = G * HEADS // 2
QUADS = PAIRS // 2
ATTEND_STEPS = 2 * QUADS + 2
STEPS = dict(LOAD=2, A=23 + ATTEND_STEPS, F=14, B=31 + PAIRS + ATTEND_STEPS, D=14,
             R=15, NEXT=1, G=38, H=18, OUT=5)
NEAR_ROWS = 11
NEAR_STEPS = 5
FAR_PRODUCTS = 3
CAP = 50.0
STRIP = 32

WEIGHTS = dict(a_q=P, a_q2=P, a_k=32, a_k2=32, a_v=32, a_o=P,
               f_base=P, f_A=P, f_B=P, f_r=EXPERTS,
               b_q=P, b_q2=P, b_k=P, b_k2=P, b_v=P, b_o=P,
               d_q=P, d_k=P, d_v=P, d_b=DH,
               g_q=P, g_down=LATENT, g_up=2 * P, g_o=P, g_g=EXPERTS, g_e=EXPERTS * P,
               h_proj=2 * HID, h_in=2 * HID, h_gate=2 * HID, h_out=2 * P)
COLUMNS = dict(f_bb=1, b_bq=1, b_bq2=1, b_bk=1, b_bk2=1, b_bo=1, b_gamma=1, b_beta=1,
               d_lnw=1, d_lnb=1, g_gamma1=1, g_bdown=1, g_bo=1, g_gamma2=1,
               h_conv=2 * TAPS, h_cb=2, h_bin=2, h_bgate=2, h_lambda=2)
ROWS = dict(f_rb=EXPERTS, b_bv=P, g_bq=P, g_bup=2 * P, g_bg=EXPERTS)
CONSTS = dict(ident=P, center=P, mean=P, head_mean=P, kv_mean=KV_A * HD, head_sum=P,
              cos_a=SEQ, sin_a=SEQ, cos_ak=SEQ, sin_ak=SEQ, cos_b=SEQ, sin_b=SEQ,
              causal=3 * P, den=4 * STRIP)


def offsets(table):
    out, at = {}, 0
    for name, n in table.items():
        out[name] = (at, n)
        at += n
    return out, at


PER_TURN = dict(
    A_tokens=16, A_x_t=1, A_centered=6, A_variance=6, A_squared=6, A_act_chain=20, A_rstd=6,
    A_x=1, A_dve_chain=29, a_k_out=16, a_q_out=16, a_kx=48, a_q=1, a_k=1, a_v=1, a_ms=1,
    a_scores_t=8, a_weighed=4, a_o=1, a_sq=2, a_rms=1, a_k_round=2, a_qx=48, a_exp=8,
    a_inverse=1, a_k_rest=2, a_masked=8, a_xn=1, a_kf=1, a_q_part=3, a_vx=4, a_rope_done=1,
    a_y=1, a_x=1, f1_logits=1, f1_ax=1, f1_weights_t=1, f1_o=1, f1_axs=1, f1_e1=1, f1_xn=1,
    f1_e0=1, f1_spread=1, f1_axw=1, f1_x=1, b_k_out=16, b_q_out=16, b_kx=48, b_m_out=16,
    b_shift=16, b_q=1, b_k=1, b_v=1, b_scores=8, b_max_turned=1, b_scores_t=8, b_weighed=4,
    b_o=1, b_k_round=2, b_qx=48, b_max_rows=1, b_exp=8, b_inverse=1, b_k_rest=2, b_summed=8,
    b_x1=1, b_xn=1, b_kf=1, b_q_part=3, b_vx=4, b_row_max=8, b_max_parts=1, b_y=1, b_x=1,
    f2_logits=1, f2_ax=1, f2_weights_t=1, f2_o=1, f2_axs=1, f2_e1=1, f2_xn=1, f2_e0=1,
    f2_spread=1, f2_axw=1, f2_x=1, d_x_out=16, d_stored=64, d_kvb=1, d_q=1, d_norm2=1, d_sq=1,
    d_e=1, d_qs=1, d_rk=1, d_xn=1, d_norm2c=1, d_kvn=1, C_readout=176, C_stored=16,
    C_centered=4, C_variance=8, C_out_t=1, C_squared=8, C_act_chain=14, C_rstd=8, C_out=1,
    C_dve_chain=28, r_u_t=1, r_w=4, r_read=2, r_rows=1, r_ux=2, r_masked=4, r_on=1, r_x=1,
    g1_qd=1, g1_kv=1, g1_heads_t=1, g1_o=1, g1_logits=1, g1_experts=2, g1_mixed_t=1, g1_down=1,
    g1_exp=1, g1_y=1, g1_e1=1, g1_score_odd=1, g1_value_odd=1, g1_x1=1, g1_xn=1, g1_qkv=1,
    g1_score=2, g1_shifted=1, g1_value=2, g1_heads=1, g1_x2=1, g1_xm=1, g1_e0=1, g1_gated=2,
    g1_x=1, h_proj=1, h_gates=2, h_o=1, h_pad=1, h_gelu=1, h_alpha=1, h_sig_in=1, h_beta=1,
    h_xn=1, h_conv=2, h_one_less=1, h_m=1, h_x=1, g2_qd=1, g2_kv=1, g2_heads_t=1, g2_o=1,
    g2_logits=1, g2_experts=2, g2_mixed_t=1, g2_down=1, g2_exp=1, g2_y=1, g2_e1=1,
    g2_score_odd=1, g2_value_odd=1, g2_x1=1, g2_xn=1, g2_qkv=1, g2_score=2, g2_shifted=1,
    g2_value=2, g2_heads=1, g2_x2=1, g2_xm=1, g2_e0=1, g2_gated=2, g2_x=1)

FRONT, BACK = ("A", "a", "f1", "b", "f2", "d"), ("C", "r", "g1", "h", "g2")


def parts_of(name):
    return name.partition("_")[::2]


def signals_of(loop):
    return dict.fromkeys(parts_of(n)[1] for n in PER_TURN if parts_of(n)[0] in loop)


LOADS = ("tokens", "readout")
BACK_SHARES = dict(zip([n for n in signals_of(BACK) if n not in signals_of(FRONT) and n not in LOADS],
                       [n for n in signals_of(FRONT) if n not in signals_of(BACK) and n not in LOADS]))
FRONT_SHARED = {front: back for back, front in BACK_SHARES.items()}


def total(loop, what):
    return sum(PER_TURN[n] for n in PER_TURN if parts_of(n)[0] in loop and parts_of(n)[1] == what)


def before(name):
    layer, what = parts_of(name)
    loop = FRONT if layer in FRONT else BACK
    earlier = loop[:loop.index(layer)]
    front = 0 if loop is FRONT else TURNS * total(FRONT, BACK_SHARES.get(what, what))
    return front + total(earlier, what), total(loop, what)


def build(nc, x_in, weights, columns, rows, consts, out):
    W_AT, W_N = offsets(WEIGHTS)
    C_AT, C_N = offsets(COLUMNS)
    R_AT, R_N = offsets(ROWS)
    K_AT, K_N = offsets(CONSTS)
    ctx = ExitStack()

    def sb(name, shape, dt=F32):
        return ctx.enter_context(nc.sbuf_tensor(name, shape, dt))

    with ctx:
        w_sb = sb("w_sb", [P, W_N])
        col_sb = sb("col_sb", [P, C_N])
        row_sb = sb("row_sb", [P, R_N])
        const_sb = sb("const_sb", [P, K_N])

        def W(name, lo=0, hi=None, rows_=P):
            at, n = W_AT[name]
            return w_sb[0:rows_, at + lo:at + (n if hi is None else hi)]

        def C(name, i=0, rows_=P):
            return col_sb[0:rows_, C_AT[name][0] + i:C_AT[name][0] + i + 1]

        def R(name):
            at, n = R_AT[name]
            return row_sb[:, at:at + n]

        def K(name, rows_=P):
            at, n = K_AT[name]
            return const_sb[0:rows_, at:at + n]

        Stream = namedtuple("Stream", "front back load_tokens load_readout sem zeroed UX VX")
        ident_b = sb("ident_b", [P, P], BF16)
        eps = sb("eps", [P, 4])
        EPS5, EPS6, ZERO, ONE = [eps[:, i:i + 1] for i in range(4)]
        neg_bias = sb("neg_bias", [P, 4])
        decay = sb("decay", [P, 2])
        dec_t = sb("dec_t", [P, 8])

        bands = sb("bands", [P, 2 * STREAMS, HEADS, TOK], BF16)
        scan_k = sb("scan_k", [P, 2, DD, SEQ])
        scan_v = sb("scan_v", [P, 2, DD, SEQ])
        scan_b = sb("scan_b", [P, 2, SEQ])
        state = sb("state", [P, 2, DD, DD])
        outer = sb("outer", [P, 2, DD, DD])
        s_k = sb("s_k", [P, 2, DD])

        ps = ctx.enter_context(nc.psum_tensor("ps", [P, 8, 512], F32))

        q_dram = nc.dram_tensor("q_dram", [SEQS, P, SEQ], F32).ap()
        k_dram = nc.dram_tensor("k_dram", [SEQS, P, SEQ], F32).ap()
        v_dram = nc.dram_tensor("v_dram", [SEQS, P, SEQ], F32).ap()
        b_dram = nc.dram_tensor("b_dram", [SEQS, DH, SEQ], F32).ap()
        x_dram = nc.dram_tensor("x_dram", [SEQS, P, SEQ], F32).ap()
        u_dram = nc.dram_tensor("u_dram", [SEQS, P, SEQ], F32).ap()

        sems = {}

        def sem(name):
            if name not in sems:
                sems[name] = ctx.enter_context(nc.semaphore(name))
            return sems[name]

        def signal(lane, name):
            what = parts_of(name)[1]
            what = BACK_SHARES.get(what, what)
            if what in FRONT_SHARED:
                return sem(f"s{lane}_{what}_then_{FRONT_SHARED[what]}")
            return sem(f"s{lane}_{what}")

        turn = [0]
        chains = [{} for _ in range(STREAMS)]

        def value(name, k):
            first, per = before(name)
            return turn[0] * per + (first + k)

        def stream(lane):
            def tile(name, shape, dt=F32):
                return sb(f"{name}_{lane}", shape, dt)

            QX, KX = bands[:, 2 * lane], bands[:, 2 * lane + 1]
            arena = (scan_k, scan_v)[lane][:, :, :, :].rearrange("p a b c -> p (a b c)")
            PR = arena[:, 0:4096].rearrange("p (a b c) -> p a b c", a=4, b=2)
            PS = arena[:, 4096:6144].rearrange("p (a b c) -> p a b c", a=4, b=2)
            PRB = bands[:, 2 * lane:2 * lane + 2].rearrange("p a h t -> p (a h t)").bitcast(F32)\
                .rearrange("p (a b c) -> p a b c", a=4, b=2)
            VX = tile("VX", [P, TT, HEADS * STRIP])
            UX = tile("UX", [P, TT, DH * STRIP])
            q_parts = tile("q_parts", [P, PARTS, TOK], BF16)
            k_parts = tile("k_parts", [P, PARTS, TOK], BF16)
            neg_max = tile("neg_max", [P, TT, HEADS])
            max_parts = tile("max_parts", [P, TT, PARTS, HEADS], BF16)
            max_rest = tile("max_rest", [P, 2, TT, HEADS])
            max_rows = tile("max_rows", [PARTS * HEADS, TOK], BF16)
            x, x1, x_next, xc, xn, sq, lnv, rstd, ta, tb, tc, qf, kf, rq, rk, y, q_new, k_new, v_sig = [
                tile(n, [P, TOK]) for n in
                "x x1 x_next xc xn sq lnv rstd ta tb tc qf kf rq rk y q_new k_new v_sig".split()]
            x_tok = tile("x_tok", [P, TT, P])
            small = tile("small", [P, 8, TT * EXPERTS])
            top8 = tile("top8", [P, TT, 8])
            stat = tile("stat", [P, 4, TT])
            beta_sb = tile("beta_sb", [DH, TOK])

            cuts = [0]

            def piece(n, rows_=P):
                cuts[0] += n
                return arena[0:rows_, cuts[0] - n:cuts[0]]

            KZ = piece(DH * TOK).rearrange("p (h t) -> p h t", h=DH)
            h_gelu, h_u, h_sig_in, h_sig_rec, h_alpha, h_beta = [
                piece(2 * TOK, HH).rearrange("p (a t) -> p a t", a=2) for _ in range(6)]
            u_pad = piece(2 * G * (SEQ + TAPS - 1), HH).rearrange("p (a b t) -> p a b t", a=2, b=G)
            u_rows, q_rows, o_rows = [piece(TOK) for _ in range(3)]

            q_scratch = nc.dram_tensor(f"q_scratch_{lane}", [PARTS, P, TOK], BF16).ap()
            k_scratch = nc.dram_tensor(f"k_scratch_{lane}", [PARTS, P, TOK], BF16).ap()
            m_scratch = nc.dram_tensor(f"m_scratch_{lane}", [PARTS * HEADS, TOK], BF16).ap()

            def sem(name):
                return signal(lane, name)

            def after(name, k=1):
                return signal(lane, name), value(name, k)

            def settle(eng):
                eng.nop(nofuse=True)

            chain = chains[lane]

            def link(eng, name, ins):
                chain[name] = chain.get(name, 0) + 1
                ins.then_inc(sem(name), 1)
                eng.wait_ge(*after(name, chain[name]))

            BANK = 4 * lane

            def turns_of_two(n):
                return BANK + 2 * (n % 2)

            def half(bank, i, rows_=P):
                return ps[0:rows_, BANK + bank, i * TOK:(i + 1) * TOK]

            def seq2(ap):
                return ap.rearrange("p (b t) -> p b t", b=G)

            def both(ap):
                return ap.unsqueeze(1).broadcast_to([ap.shape[0], G, SEQ])

            def heads_of(n):
                m = n % (PAIRS // G)
                i, half = m // 2, m % 2
                return [4 * (2 * half + j) + i for j in range(2)]


            def pe_norm(pe, at, ph, n, src, ready, centered=True):
                if centered:
                    yield at
                    pe.wait_ge(*after(*ready))
                    pe.matmul(half(2, 0), K("center"), src, start=True, stop=True).then_inc(sem(ph + "centered"), 1)
                yield at + (2 if centered else 3)
                pe.wait_ge(*after(ph + "squared", n + 1))
                pe.matmul(half(3, 0), K("mean"), sq[:, :], start=True, stop=True).then_inc(sem(ph + "variance"), 1)

            def act_norm(act, at, ph, n, nc_n, src=None, ready=None, e=None):
                yield at + (1 if src is None else 2)
                if src is None:
                    act.wait_ge(*after(ph + "centered", nc_n + 1))
                    act.activation(sq[:, :], half(2, 0), ACT.Square).then_inc(sem(ph + "squared"), 1)
                else:
                    act.wait_ge(*after(*ready))
                    act.activation(sq[:, :], src, ACT.Square).then_inc(sem(ph + "squared"), 1)
                yield at + 4
                act.wait_ge(*after(ph + "variance", n + 1))
                link(act, ph + "act_chain", act.activation(lnv[:, :], half(3, 0), ACT.Ln, bias=e))
                act.activation(rstd[:, :], lnv[:, :], ACT.Exp, scale=-0.5, bias=ZERO).then_inc(sem(ph + "rstd"), 1)

            def dve_norm(dve, at, ph, n, nc_n, dst, name, src=None, gamma=None, beta=None):
                if src is None:
                    src = half(2, 0)
                yield at + 5
                dve.wait_ge(*after(ph + "rstd", n + 1))
                if gamma is None:
                    dve.tensor_tensor(dst, src, rstd[:, :], ALU.mult).then_inc(sem(name), 1)
                elif beta is None:
                    dve.scalar_tensor_tensor(dst, src, gamma, rstd[:, :], ALU.mult, ALU.mult).then_inc(sem(name), 1)
                else:
                    link(dve, ph + "dve_chain", dve.tensor_tensor(xc[:, :], src, rstd[:, :], ALU.mult))
                    dve.tensor_scalar(dst, xc[:, :], gamma, beta, ALU.mult, ALU.add).then_inc(sem(name), 1)


            def dve_split_q(dve, ph, L):
                c = ph + "dve_chain"
                ins = dve.tensor_copy(q_parts[:, 0, :], qf[:, :])
                ins.then_inc(sem(L + "q_part"), 1)
                dve.wait_ge(*after(L + "q_part", 1))
                link(dve, c, dve.tensor_tensor(ta[:, :], qf[:, :], q_parts[:, 0, :], ALU.subtract))
                dve.tensor_copy(q_parts[:, 1, :], ta[:, :]).then_inc(sem(L + "q_part"), 1)
                dve.wait_ge(*after(L + "q_part", 2))
                dve.tensor_tensor(q_parts[:, 2, :], ta[:, :], q_parts[:, 1, :], ALU.subtract).then_inc(sem(L + "q_part"), 1)

            def act_split_k(act, at, L, n=P):
                yield at
                act.wait_ge(*after(L + "kf"))
                act.activation(k_parts[0:n, 0, :], kf[0:n, :], ACT.Copy).then_inc(sem(L + "k_round"), 1)
                yield at + 2
                act.wait_ge(*after(L + "k_rest", 1))
                act.activation(k_parts[0:n, 1, :], tc[0:n, :], ACT.Copy).then_inc(sem(L + "k_round"), 1)

            def pool_split_k(pool, at, L, n=P):
                yield at + 1
                pool.wait_ge(*after(L + "k_round", 1))
                pool.tensor_tensor(tc[0:n, :], kf[0:n, :], k_parts[0:n, 0, :], ALU.subtract).then_inc(sem(L + "k_rest"), 1)
                yield at + 3
                pool.wait_ge(*after(L + "k_round", 2))
                pool.tensor_tensor(k_parts[0:n, 2, :], tc[0:n, :], k_parts[0:n, 1, :], ALU.subtract).then_inc(sem(L + "k_rest"), 1)

            def sp_spread(sp, at, L, kv=HEADS):
                yield at
                sp.wait_ge(*after(L + "k_rest", 2))
                k_of = k_scratch[:, 0:kv * HD, :]
                sp.dma_start(k_of.rearrange("c p t -> p c t"), k_parts[0:kv * HD, :, :]).then_inc(sem(L + "k_out"), 16)
                sp.wait_ge(*after(L + "q_part", PARTS))
                sp.dma_start(q_scratch.rearrange("c p t -> p c t"), q_parts[:, :, :]).then_inc(sem(L + "q_out"), 16)
                yield at + 2
                sp.wait_ge(*after(L + "k_out", 16))
                for band, part, n in K_BANDS:
                    src = k_scratch[part:part + n, 0:kv * HD, :].rearrange("c (d h) t -> c d (h t)", d=HD)
                    sp.dma_start(KX[HD * band:HD * (band + n), 0:kv, :].rearrange("p h t -> p (h t)"), src)\
                        .then_inc(sem(L + "kx"), 16)

            def act_load_q(act, at, L):
                yield at + 2
                act.wait_ge(*after(L + "q_out", 16))
                settle(act)
                for band, part, n in Q_BANDS:
                    src = q_scratch[part].rearrange("(d h) t -> d (h t)", d=HD).unsqueeze(0)\
                        .broadcast_to([n, HD, HEADS * TOK])
                    act.dma_start(QX[HD * band:HD * (band + n), :, :].rearrange("p h t -> p (h t)"), src)\
                        .then_inc(sem(L + "qx"), 16)

            def pe_scores(pe, at, L):
                for n in range(PAIRS):
                    yield at + n
                    b = n // (PAIRS // G)
                    if n == 0:
                        pe.wait_ge(*after(L + "kx", 16 * len(K_BANDS)))
                        pe.wait_ge(*after(L + "qx", 16 * len(Q_BANDS)))
                    if n >= 2:
                        pe.wait_ge(*after(L + "row_max", n - 1))
                    for j, h in enumerate(heads_of(n)):
                        for t in range(2):
                            ins = pe.matmul(ps[:, turns_of_two(n) + j, t * SEQ:(t + 1) * SEQ],
                                            QX[0:SHIFT_ROW, h, b * SEQ + t * P:b * SEQ + (t + 1) * P],
                                            KX[0:SHIFT_ROW, h, b * SEQ:(b + 1) * SEQ], start=True, stop=True)
                    ins.then_inc(sem(L + "scores"), 1)

            def dve_max(dve, at, ph, L):
                for n in range(PAIRS):
                    yield at + n
                    b, h = n // (PAIRS // G), heads_of(n)[0]
                    dve.wait_ge(*after(L + "scores", n + 1))
                    dve.tensor_reduce(
                        neg_max[:, 2 * b:2 * b + 2, h:h + 5:4].rearrange("p t j -> p j t"),
                        ps[:, turns_of_two(n):turns_of_two(n) + 2, :].rearrange("p j (t k) -> p j t k", t=2),
                        AX_X, ALU.max, negate=True).then_inc(sem(L + "row_max"), 1)
                yield at + PAIRS
                dve.wait_ge(*after(L + "row_max", PAIRS))
                c = ph + "dve_chain"
                link(dve, c, dve.tensor_copy(max_parts[:, :, 0, :], neg_max[:, :, :]))
                link(dve, c, dve.tensor_tensor(max_rest[:, 0], neg_max[:, :, :], max_parts[:, :, 0, :], ALU.subtract))
                link(dve, c, dve.tensor_copy(max_parts[:, :, 1, :], max_rest[:, 0]))
                dve.tensor_tensor(max_parts[:, :, 2, :], max_rest[:, 0], max_parts[:, :, 1, :], ALU.subtract).then_inc(sem(L + "max_parts"), 1)

            def pe_max_rows(pe, L):
                pe.wait_ge(*after(L + "max_parts"))
                settle(pe)
                psb = ps[0:PARTS * HEADS, BANK + 3, :].bitcast(BF16)
                for t in range(TT):
                    ins = pe.transpose(psb[:, t * P:(t + 1) * P],
                                       max_parts[:, t, :, :].rearrange("p c h -> p (c h)"), ident_b[:, :])
                ins.then_inc(sem(L + "max_turned"), 1)

            def act_max_rows(act, L):
                act.wait_ge(*after(L + "max_turned"))
                act.activation(max_rows[:, :], ps[0:PARTS * HEADS, BANK + 3, :].bitcast(BF16)[:, 0:TOK], ACT.Copy).then_inc(sem(L + "max_rows"), 1)

            def sp_max_rows(sp, at, L):
                yield at
                sp.wait_ge(*after(L + "max_rows"))
                sp.dma_start(m_scratch, max_rows[:, :]).then_inc(sem(L + "m_out"), 16)
                yield at + 1
                sp.wait_ge(*after(L + "m_out", 16))
                sp.dma_start(QX[SHIFT_ROW:SROWS, :, :], m_scratch.rearrange("(c h) t -> c h t", c=PARTS)).then_inc(sem(L + "shift"), 16)

            def pe_attend(pe, at, L, causal):
                for m in range(QUADS + 1):
                    for n in (2 * m, 2 * m + 1) if m < QUADS else ():
                        yield at + n
                        b = n // (PAIRS // G)
                        if n == 0 and causal:
                            pe.wait_ge(*after(L + "kx", 16 * len(K_BANDS)))
                            pe.wait_ge(*after(L + "qx", 16 * len(Q_BANDS)))
                            pe.wait_ge(*after(L + "rope_done"))
                        if n == 0 and not causal:
                            pe.wait_ge(*after(L + "shift", 16))
                        if n >= 1:
                            pe.wait_ge(*after(L + "exp", n))
                        for j, h in enumerate(heads_of(n)):
                            for t in range(2):
                                lo = t * P if causal else 0
                                hk = h // (HEADS // KV_A) if causal else h
                                rows_ = SHIFT_ROW if causal else SROWS
                                ins = pe.matmul(ps[:, BANK + j, t * SEQ:(t + 1) * SEQ - lo],
                                                KX[0:rows_, hk, b * SEQ + t * P:b * SEQ + (t + 1) * P],
                                                QX[0:rows_, h, b * SEQ + lo:(b + 1) * SEQ], start=True, stop=True)
                        ins.then_inc(sem(L + "scores_t"), 1)
                    if m == 0:
                        continue
                    yield at + 2 * m + (2 if causal else 1)
                    pe.wait_ge(*after(L + ("masked" if causal else "exp"), 2 * m))
                    if m == 1:
                        pe.wait_ge(*after(L + "vx", 4))
                    b = (m - 1) // (QUADS // G)
                    i = (m - 1) % (QUADS // G)
                    for bank in (2, 3):
                        if bank == 3 and not causal:
                            pe.wait_ge(*after(L + "summed", 2 * m))
                        for t in range(2) if bank == 2 or causal else (0,):
                            lo = t * P if causal else 0
                            for g in range(4):
                                h, n = 4 * g + i, 2 * (m - 1) + g // 2
                                lhs = VX[:, 2 * b + t, h * STRIP:(h + 1) * STRIP] if bank == 2 else \
                                    K("den")[:, i * STRIP:(i + 1) * STRIP]
                                rhs = PR[:, n % 4, g % 2, t * SEQ:(t + 1) * SEQ - lo] if bank == 2 or causal else \
                                    PS[:, n % 4, g % 2, :]
                                ins = pe.matmul(ps[STRIP * g:STRIP * (g + 1), BANK + bank, b * SEQ + lo:(b + 1) * SEQ],
                                                lhs, rhs, start=(i == 0 and t == 0),
                                                stop=(i == 3 and (t == 1 or (bank == 3 and not causal))),
                                                skip_group_check=True)
                    ins.then_inc(sem(L + "weighed"), 1)

            def act_attend(act, at, ph, L, causal):
                scale = float(HD) ** -0.5
                for n in range(PAIRS):
                    yield at + n
                    act.wait_ge(*after(L + "scores_t", n + 1))
                    if causal:
                        v = ps[:, BANK:BANK + 2, 0:SEQ + P]
                        link(act, ph + "act_chain", act.activation(v, v, ACT.Tanh, scale=scale / CAP))
                    if n >= 4:
                        act.wait_ge(*after(L + "weighed", (n - 4) // 2 + 1))
                    if causal:
                        act.activation(PR[:, n % 4, :, 0:SEQ + P], v, ACT.Exp, scale=CAP, bias=ZERO).then_inc(sem(L + "exp"), 1)
                    else:
                        act.activation(PR[:, n % 4, :, :], ps[:, BANK:BANK + 2, :], ACT.Exp, scale=scale, bias=ZERO).then_inc(sem(L + "exp"), 1)

            def act_invert(act, at, L):
                yield at + 2 * QUADS + 2
                act.wait_ge(*after(L + "weighed", QUADS))
                link(act, "A_act_chain", act.activation(lnv[:, :], half(3, 0), ACT.Ln, bias=ZERO))
                act.activation(tb[:, :], lnv[:, :], ACT.Exp, scale=-1.0, bias=ZERO).then_inc(sem(L + "inverse"), 1)

            def dve_attend(dve, at, ph, L):
                yield at + 2 * QUADS + 2
                dve.wait_ge(*after(L + "inverse"))
                dve.tensor_tensor(y[:, :], half(2, 0), tb[:, :], ALU.mult).then_inc(sem(L + "y"), 1)

            def dve_values(dve, L, bank, bias):
                dst = VX[:, :, :].rearrange("p t (g c) -> p t g c", g=4)
                for i in range(4):
                    d = dst[:, :, :, 40 * i:40 * i + 8]
                    if bias is None:
                        s = half(bank, 0)[:, 0:TT * 32].rearrange("p (t g d) -> p t g d", t=TT, g=4)
                        dve.tensor_copy(d, s).then_inc(sem(L + "vx"), 1)
                    else:
                        s = half(bank, 0).rearrange("p (t g i d) -> p t g i d", t=TT, g=4, i=4)[:, :, :, i, :]
                        r = bias.rearrange("p (g i d) -> p g i d", g=4, i=4)[:, :, i, :].unsqueeze(1)\
                            .broadcast_to([P, TT, 4, HD])
                        dve.tensor_tensor(d, s, r, ALU.add).then_inc(sem(L + "vx"), 1)

            def a_layer(e, eng, n):
                ph, L = "A_", "a_"
                if eng == "pe":
                    yield from pe_norm(e, 0, ph, n, x[:, :], ("A_x",))
                    yield 6
                    e.wait_ge(*after(L + "xn"))
                    e.matmul(half(0, 0), W("a_q"), xn[:, :], start=True, stop=True)
                    e.matmul(half(0, 1), W("a_q2"), xn[:, :], start=True, stop=True).then_inc(sem(L + "q"), 1)
                    e.matmul(half(1, 0, 32), W("a_k"), xn[:, :], start=True, stop=True)
                    e.matmul(half(1, 1, 32), W("a_k2"), xn[:, :], start=True, stop=True).then_inc(sem(L + "k"), 1)
                    for t in range(TT):
                        ins = e.matmul(half(2, 0)[:, t * 32:(t + 1) * 32], xn[:, t * P:(t + 1) * P], W("a_v"),
                                       start=True, stop=True)
                    ins.then_inc(sem(L + "v"), 1)
                    yield 8
                    e.wait_ge(*after(L + "sq", 2))
                    e.matmul(half(3, 0), K("head_mean"), sq[:, :], start=True, stop=True)
                    e.matmul(half(3, 1, 32), K("kv_mean", 32), tb[0:32, :], start=True, stop=True).then_inc(sem(L + "ms"), 1)
                    yield from pe_attend(e, 20, L, True)
                    yield 20 + ATTEND_STEPS + 1
                    e.wait_ge(*after(L + "y"))
                    e.matmul(half(0, 0), W("a_o"), y[:, :], start=True, stop=True).then_inc(sem(L + "o"), 1)
                if eng == "act":
                    yield from act_norm(e, 0, ph, n, n, e=EPS5)
                    yield 7
                    e.wait_ge(*after(L + "q"))
                    e.activation(sq[:, :], half(0, 0), ACT.Square).then_inc(sem(L + "sq"), 1)
                    e.wait_ge(*after(L + "k"))
                    e.activation(tb[0:32, :], half(1, 0, 32), ACT.Square).then_inc(sem(L + "sq"), 1)
                    yield 9
                    e.wait_ge(*after(L + "ms"))
                    e.activation(lnv[:, :], half(3, 0), ACT.Ln, bias=EPS5)
                    link(e, ph + "act_chain",
                         e.activation(rk[0:32, :], half(3, 1, 32), ACT.Ln, bias=eps[0:32, 0:1]))
                    e.activation(rq[:, :], lnv[:, :], ACT.Exp, scale=-0.5, bias=ZERO)
                    e.activation(rk[0:32, :], rk[0:32, :], ACT.Exp, scale=-0.5, bias=eps[0:32, 2:3]).then_inc(sem(L + "rms"), 1)
                    yield from act_split_k(e, 11, L, 32)
                    yield from act_load_q(e, 15, L)
                    yield from act_attend(e, 20, ph, L, True)
                    e.preload_act_table_set(LN_EXP_SET)
                    yield from act_invert(e, 20, L)
                if eng == "dve":
                    c = ph + "dve_chain"
                    yield from dve_norm(e, 0, ph, n, n, xn[:, :], L + "xn")
                    yield 8
                    e.wait_ge(*after(L + "sq", 2))
                    k0, k1 = seq2(half(1, 0, 32)), seq2(half(1, 1, 32))
                    e.tensor_tensor(seq2(kf[0:32, :]), k0, both(K("cos_ak", 32)), ALU.mult)
                    link(e, c, e.tensor_tensor(seq2(ta[0:32, :]), k1, both(K("sin_ak", 32)), ALU.mult))
                    link(e, c, e.tensor_tensor(kf[0:32, :], kf[0:32, :], ta[0:32, :], ALU.add))
                    yield 10
                    e.wait_ge(*after(L + "rms"))
                    e.tensor_tensor(kf[0:32, :], kf[0:32, :], rk[0:32, :], ALU.mult).then_inc(sem(L + "kf"), 1)
                    e.tensor_tensor(seq2(qf[:, :]), seq2(half(0, 0)), both(K("cos_a")), ALU.mult)
                    link(e, c, e.tensor_tensor(seq2(xc[:, :]), seq2(half(0, 1)), both(K("sin_a")), ALU.mult))
                    link(e, c, e.tensor_tensor(qf[:, :], qf[:, :], xc[:, :], ALU.add))
                    link(e, c, e.tensor_tensor(qf[:, :], qf[:, :], rq[:, :], ALU.mult))
                    dve_split_q(e, ph, L)
                    yield 12
                    e.wait_ge(*after(L + "v"))
                    dst = VX[:, :, :].rearrange("p t (g c) -> p t g c", g=4)
                    for i in range(4):
                        s = half(2, 0)[:, 0:TT * 32].rearrange("p (t g d) -> p t g d", t=TT, g=4)
                        ins = e.tensor_copy(dst[:, :, :, 40 * i:40 * i + 8], s)
                        ins.then_inc(sem(L + "vx"), 1)
                    e.memset(stat[:, 3, :], 0.0).then_inc(sem(L + "rope_done"), 1)
                    yield from dve_attend(e, 20, ph, L)
                    yield 20 + ATTEND_STEPS + 2
                    e.wait_ge(*after(L + "o"))
                    e.tensor_tensor(x[:, :], x[:, :], half(0, 0), ALU.add).then_inc(sem(L + "x"), 1)
                if eng == "pool":
                    yield from pool_split_k(e, 11, L, 32)
                    tri = K("causal")[:, 0:P].unsqueeze(1).unsqueeze(1).broadcast_to([P, 2, 2, P])
                    for pair in range(PAIRS):
                        yield 20 + pair + 1
                        e.wait_ge(*after(L + "exp", pair + 1))
                        v = PR[:, pair % 4, :, :].rearrange("p j (t k) -> p j t k", t=2)[:, :, :, 0:P]
                        e.tensor_tensor(v, v, tri, ALU.mult).then_inc(sem(L + "masked"), 1)
                if eng == "sp":
                    yield from sp_spread(e, 15, L, KV_A)

            def f_layer(e, eng, L, n, ready):
                ph = "A_"
                if eng == "pe":
                    yield from pe_norm(e, 0, ph, n, x[:, :], ready)
                    yield 6
                    e.wait_ge(*after(L + "xn"))
                    for t in range(TT):
                        ins = e.matmul(half(0, 0)[:, t * EXPERTS:(t + 1) * EXPERTS], xn[:, t * P:(t + 1) * P], W("f_r"),
                                       start=True, stop=True)
                    ins.then_inc(sem(L + "logits"), 1)
                    e.matmul(half(1, 0), W("f_base"), xn[:, :], start=True, stop=False)
                    e.matmul(half(2, 0), W("f_A"), xn[:, :], start=True, stop=True).then_inc(sem(L + "ax"), 1)
                    yield 10
                    e.wait_ge(*after(L + "spread"))
                    for t in range(TT):
                        ins = e.transpose(half(3, 0)[:, t * P:(t + 1) * P], y[:, t * P:(t + 1) * P], K("ident"))
                    ins.then_inc(sem(L + "weights_t"), 1)
                    yield 12
                    e.wait_ge(*after(L + "axw"))
                    e.matmul(half(1, 0), W("f_B"), tb[:, :], start=False, stop=True).then_inc(sem(L + "o"), 1)
                if eng == "act":
                    yield from act_norm(e, 0, ph, n, n, e=EPS5)
                    yield 7
                    e.wait_ge(*after(L + "ax"))
                    e.activation(ta[:, :], half(2, 0), ACT.Copy).then_inc(sem(L + "axs"), 1)
                    yield 8
                    e.wait_ge(*after(L + "e0"))
                    e.activation(small[:, 2, :], small[:, 1, :], ACT.Exp, bias=ZERO).then_inc(sem(L + "e1"), 1)
                if eng == "dve":
                    c = ph + "dve_chain"
                    yield from dve_norm(e, 0, ph, n, n, xn[:, :], L + "xn")
                    yield 7
                    e.wait_ge(*after(L + "logits"))
                    lg = small[:, 0, :].rearrange("p (t e) -> p t e", t=TT)

                    def by_token(ap):
                        return ap.unsqueeze(2).broadcast_to([P, TT, EXPERTS])

                    def tile(i):
                        return small[:, i, :].rearrange("p (t e) -> p t e", t=TT)

                    link(e, c, e.tensor_tensor(lg, half(0, 0)[:, 0:TT * EXPERTS].rearrange("p (t e) -> p t e", t=TT),
                                               R("f_rb").unsqueeze(1).broadcast_to([P, TT, EXPERTS]), ALU.add))
                    e.tensor_reduce(stat[:, 0, :], lg, AX_X, ALU.max)
                    for t in range(TT):
                        ins = e.max(top8[:, t, :], small[:, 0, t * EXPERTS:(t + 1) * EXPERTS])
                    link(e, c, ins)
                    e.tensor_tensor(tile(1), lg, by_token(stat[:, 0, :]), ALU.subtract).then_inc(sem(L + "e0"), 1)
                    e.tensor_tensor(tile(3), lg, top8[:, :, 1:2].broadcast_to([P, TT, EXPERTS]), ALU.is_ge)
                    yield 9
                    e.wait_ge(*after(L + "e1"))
                    link(e, c, e.tensor_copy(small[:, 5, :], small[:, 2, :]))
                    link(e, c, e.tensor_tensor(tile(4), tile(5), tile(3), ALU.mult))
                    link(e, c, e.tensor_reduce(stat[:, 1, :], tile(4), AX_X, ALU.add))
                    link(e, c, e.reciprocal(stat[:, 2, :], stat[:, 1, :]))
                    link(e, c, e.scalar_tensor_tensor(tile(6), tile(4), 2.0, by_token(stat[:, 2, :]),
                                                      ALU.mult, ALU.mult))
                    e.tensor_copy(y[:, :].rearrange("p (a r) -> p a r", r=RANK),
                                       small[:, 6, :].unsqueeze(2).broadcast_to([P, TT * EXPERTS, RANK])).then_inc(sem(L + "spread"), 1)
                    yield 11
                    e.wait_ge(*after(L + "axs"))
                    e.wait_ge(*after(L + "weights_t"))
                    e.tensor_tensor(tb[:, :], half(3, 0), ta[:, :], ALU.mult).then_inc(sem(L + "axw"), 1)
                    yield 13
                    e.wait_ge(*after(L + "o"))
                    e.scalar_tensor_tensor(x[:, :], half(1, 0), C("f_bb"), x[:, :], ALU.add, ALU.add).then_inc(sem(L + "x"), 1)

            def b_layer(e, eng, n, ready):
                ph, L = "A_", "b_"
                if eng == "pe":
                    yield from pe_norm(e, 0, ph, n, x[:, :], ready)
                    yield from pe_norm(e, 6, ph, n + 1, x1[:, :], (L + "x1",))
                    yield 12
                    e.wait_ge(*after(L + "xn"))
                    e.matmul(half(0, 0), W("b_q"), xn[:, :], start=True, stop=True)
                    e.matmul(half(0, 1), W("b_q2"), xn[:, :], start=True, stop=True).then_inc(sem(L + "q"), 1)
                    e.matmul(half(1, 0), W("b_k"), xn[:, :], start=True, stop=True)
                    e.matmul(half(1, 1), W("b_k2"), xn[:, :], start=True, stop=True).then_inc(sem(L + "k"), 1)
                    for t in range(TT):
                        ins = e.matmul(half(2, 0)[:, t * P:(t + 1) * P], xn[:, t * P:(t + 1) * P], W("b_v"),
                                       start=True, stop=True)
                    ins.then_inc(sem(L + "v"), 1)
                    yield 22
                    e.wait_ge(*after(L + "vx", 4))
                    yield from pe_scores(e, 22, L)
                    yield 23 + PAIRS
                    pe_max_rows(e, L)
                    yield from pe_attend(e, 28 + PAIRS, L, False)
                    yield 28 + PAIRS + ATTEND_STEPS + 1
                    e.wait_ge(*after(L + "y"))
                    e.matmul(half(0, 0), W("b_o"), y[:, :], start=True, stop=True).then_inc(sem(L + "o"), 1)
                if eng == "act":
                    yield from act_norm(e, 0, ph, n, n, e=EPS5)
                    yield from act_norm(e, 6, ph, n + 1, n + 1, e=EPS5)
                    yield from act_split_k(e, 14, L)
                    yield from act_load_q(e, 18, L)
                    yield 24 + PAIRS
                    act_max_rows(e, L)
                    yield from act_attend(e, 28 + PAIRS, ph, L, False)
                    yield from act_invert(e, 28 + PAIRS, L)
                if eng == "dve":
                    c = ph + "dve_chain"
                    yield from dve_norm(e, 0, ph, n, n, x1[:, :], L + "x1")
                    yield from dve_norm(e, 6, ph, n + 1, n + 1, xn[:, :], L + "xn", gamma=C("b_gamma"), beta=C("b_beta"))
                    yield 13
                    e.wait_ge(*after(L + "k"))
                    e.scalar_tensor_tensor(seq2(ta[:, :]), seq2(half(1, 0)), C("b_bk"), both(K("cos_b")), ALU.add, ALU.mult)
                    link(e, c, e.scalar_tensor_tensor(seq2(tb[:, :]), seq2(half(1, 1)), C("b_bk2"), both(K("sin_b")),
                                                      ALU.add, ALU.mult))
                    e.tensor_tensor(kf[:, :], ta[:, :], tb[:, :], ALU.add).then_inc(sem(L + "kf"), 1)
                    e.scalar_tensor_tensor(seq2(xc[:, :]), seq2(half(0, 0)), C("b_bq"), both(K("cos_b")), ALU.add, ALU.mult)
                    link(e, c, e.scalar_tensor_tensor(seq2(y[:, :]), seq2(half(0, 1)), C("b_bq2"), both(K("sin_b")),
                                                      ALU.add, ALU.mult))
                    link(e, c, e.tensor_tensor(qf[:, :], xc[:, :], y[:, :], ALU.add))
                    dve_split_q(e, ph, L)
                    yield 15
                    e.wait_ge(*after(L + "v"))
                    dve_values(e, L, 2, R("b_bv"))
                    yield from dve_max(e, 22, ph, L)
                    yield from dve_attend(e, 28 + PAIRS, ph, L)
                    yield 28 + PAIRS + ATTEND_STEPS + 2
                    e.wait_ge(*after(L + "o"))
                    link(e, c, e.scalar_tensor_tensor(ta[:, :], half(0, 0), C("b_bo"), x1[:, :], ALU.add, ALU.add))
                    e.tensor_tensor(x[:, :], x[:, :], ta[:, :], ALU.add).then_inc(sem(L + "x"), 1)
                if eng == "pool":
                    yield from pool_split_k(e, 14, L)
                    for pair in range(PAIRS):
                        yield 28 + PAIRS + pair + 1
                        e.wait_ge(*after(L + "exp", pair + 1))
                        if pair >= 4:
                            e.wait_ge(*after(L + "weighed", (pair - 4) // 2 + 1))
                        e.tensor_tensor(PS[:, pair % 4], PR[:, pair % 4, :, 0:SEQ], PR[:, pair % 4, :, SEQ:2 * SEQ],
                                        ALU.add).then_inc(sem(L + "summed"), 1)
                if eng == "sp":
                    yield from sp_spread(e, 18, L)
                    yield from sp_max_rows(e, 25 + PAIRS, L)

            def d_layer(e, eng, n, ready):
                ph, L = "A_", "d_"
                if eng == "pe":
                    yield from pe_norm(e, 0, ph, n, x[:, :], ready)
                    yield 6
                    e.wait_ge(*after(L + "xn"))
                    e.matmul(half(0, 0), W("d_k"), xn[:, :], start=True, stop=True)
                    e.matmul(half(1, 0), W("d_v"), xn[:, :], start=True, stop=True)
                    e.matmul(half(1, 1, DH), W("d_b"), xn[:, :], start=True, stop=True).then_inc(sem(L + "kvb"), 1)
                    e.matmul(half(2, 0), W("d_q"), xn[:, :], start=True, stop=True).then_inc(sem(L + "q"), 1)
                    yield 8
                    e.wait_ge(*after(L + "sq"))
                    e.matmul(half(3, 0), K("head_sum"), sq[:, :], start=True, stop=True).then_inc(sem(L + "norm2"), 1)
                    yield 12
                    e.wait_ge(*after(L + "kvn"))
                    settle(e)
                if eng == "act":
                    yield from act_norm(e, 0, ph, n, n, e=EPS5)
                    yield 7
                    e.wait_ge(*after(L + "kvb"))
                    e.activation(sq[:, :], half(0, 0), ACT.Square).then_inc(sem(L + "sq"), 1)
                    e.activation(ta[:, :], half(1, 0), ACT.Exp, scale=-1.0, bias=ZERO)
                    link(e, ph + "act_chain",
                         e.activation(beta_sb[:, :], half(1, 1, DH), ACT.Exp, scale=-1.0, bias=eps[0:DH, 2:3]))
                    e.activation(ta[:, :], ta[:, :], ACT.Ln, bias=ONE)
                    link(e, ph + "act_chain", e.activation(beta_sb[:, :], beta_sb[:, :], ACT.Ln, bias=eps[0:DH, 3:4]))
                    e.activation(tb[:, :], ta[:, :], ACT.Exp, scale=-1.0, bias=ZERO)
                    e.activation(beta_sb[:, :], beta_sb[:, :], ACT.Exp, scale=-1.0, bias=eps[0:DH, 2:3]).then_inc(sem(L + "e"), 1)
                    e.wait_ge(*after(L + "q"))
                    e.activation(q_new[:, :], half(2, 0), ACT.Copy).then_inc(sem(L + "qs"), 1)
                    yield 10
                    e.wait_ge(*after(L + "norm2c"))
                    link(e, ph + "act_chain", e.activation(lnv[:, :], xc[:, :], ACT.Ln, bias=ZERO))
                    e.activation(rk[:, :], lnv[:, :], ACT.Exp, scale=-0.5, bias=ZERO).then_inc(sem(L + "rk"), 1)
                if eng == "dve":
                    c = ph + "dve_chain"
                    yield from dve_norm(e, 0, ph, n, n, xn[:, :], L + "xn")
                    yield 8
                    e.wait_ge(*after(L + "e"))
                    e.tensor_tensor(v_sig[:, :], half(1, 0), tb[:, :], ALU.mult)
                    yield 9
                    e.wait_ge(*after(L + "norm2"))
                    e.tensor_scalar(xc[:, :], half(3, 0), 1e-24, None, ALU.max).then_inc(sem(L + "norm2c"), 1)
                    yield 11
                    e.wait_ge(*after(L + "rk"))
                    e.tensor_tensor(k_new[:, :], half(0, 0), rk[:, :], ALU.mult).then_inc(sem(L + "kvn"), 1)
                    e.wait_ge(*after(L + "x_out", 16))
                    settle(e)
                if eng == "sp":
                    it = turn[0]

                    def to(dram):
                        return dram.rearrange("(i b) p t -> i b p t", b=STREAMS)[it][lane]

                    yield 0
                    e.wait_ge(*after(*ready))
                    settle(e)
                    e.dma_start(to(x_dram), x[:, :]).then_inc(sem(L + "x_out"), 16)
                    yield 8
                    e.wait_ge(*after(L + "qs"))
                    settle(e)
                    e.dma_start(to(q_dram), q_new[:, :]).then_inc(sem(L + "stored"), 16)
                    yield 12
                    e.wait_ge(*after(L + "kvn"))
                    settle(e)
                    e.dma_start(to(k_dram), k_new[:, :]).then_inc(sem(L + "stored"), 16)
                    e.dma_start(to(v_dram), v_sig[:, :]).then_inc(sem(L + "stored"), 16)
                    e.dma_start(to(b_dram), beta_sb[:, :]).then_inc(sem(L + "stored"), 16)
                    yield 13
                    e.wait_ge(*after(L + "stored", 64))
                    settle(e)

            def r_layer(e, eng):
                ph, L = "C_", "r_"
                quads = G * 2

                def heads(n):
                    m = n % 4
                    i, half = m // 2, m % 2
                    return [2 * (2 * half + j) + i for j in range(2)]

                if eng == "pe":
                    yield 0
                    e.wait_ge(*after("C_readout", 16 * (3 + DH)))
                    for t in range(TT):
                        ins = e.transpose(half(3, 0)[:, t * P:(t + 1) * P], u_rows[:, t * P:(t + 1) * P], K("ident"))
                    ins.then_inc(sem(L + "u_t"), 1)
                    for m in range(quads + 1):
                        for n in (2 * m, 2 * m + 1) if m < quads else ():
                            yield 2 + n
                            b = n // 4
                            if n >= 1:
                                e.wait_ge(*after(L + "masked", n))
                            for j, h in enumerate(heads(n)):
                                for t in range(2):
                                    ins = e.matmul(ps[:, BANK + j, t * SEQ:(t + 1) * SEQ - t * P],
                                                   KZ[:, h, b * SEQ + t * P:b * SEQ + (t + 1) * P],
                                                   q_rows[:, b * SEQ + t * P:(b + 1) * SEQ], start=True, stop=True)
                            ins.then_inc(sem(L + "w"), 1)
                        if m == 0:
                            continue
                        yield 2 + 2 * m + 1
                        e.wait_ge(*after(L + "masked", 2 * m))
                        if m == 1:
                            e.wait_ge(*after(L + "ux", 2))
                        b, i = (m - 1) // 2, (m - 1) % 2
                        for t in range(2):
                            for g in range(4):
                                h, n = 2 * g + i, 2 * (m - 1) + g // 2
                                ins = e.matmul(ps[STRIP * g:STRIP * (g + 1), BANK + 2, b * SEQ + t * P:(b + 1) * SEQ],
                                               UX[:, 2 * b + t, h * STRIP:(h + 1) * STRIP],
                                               PRB[:, n % 4, g % 2, t * SEQ:(t + 1) * SEQ - t * P],
                                               start=(i == 0 and t == 0), stop=(i == 1 and t == 1),
                                               skip_group_check=True)
                        ins.then_inc(sem(L + "read"), 1)
                    yield from pe_norm(e, 9, ph, 0, o_rows, (L + "rows",))
                if eng == "act":
                    yield 8
                    e.wait_ge(*after(L + "read", quads))
                    e.activation(o_rows, half(2, 0), ACT.Copy).then_inc(sem(L + "rows"), 1)
                    yield from act_norm(e, 9, ph, 0, 0, e=EPS5)
                if eng == "dve":
                    c = ph + "dve_chain"
                    yield 1
                    e.wait_ge(*after(L + "u_t"))
                    dst = UX[:, :, :].rearrange("p t (g c) -> p t g c", g=4)
                    for i in range(2):
                        from_u = half(3, 0).rearrange("p (t g i d) -> p t g i d", t=TT, g=4, i=2)[:, :, :, i, :]
                        e.tensor_copy(dst[:, :, :, 48 * i:48 * i + DD], from_u).then_inc(sem(L + "ux"), 1)
                    for n in range(2 * quads):
                        yield 2 + n
                        e.wait_ge(*after(L + "w", n + 1))
                        if n >= 4:
                            e.wait_ge(*after(L + "read", (n - 4) // 2 + 1))
                        e.tensor_tensor(PRB[:, n % 4, :, 0:3 * P], ps[:, BANK:BANK + 2, 0:3 * P],
                                             K("causal").unsqueeze(1).broadcast_to([P, 2, 3 * P]), ALU.mult).then_inc(sem(L + "masked"), 1)
                    yield from dve_norm(e, 9, ph, 0, 0, ta[:, :], L + "on", gamma=C("d_lnw"), beta=C("d_lnb"))
                    e.wait_ge(*after(L + "on"))
                    e.wait_ge(*after("C_readout", 16 * (3 + DH)))
                    e.tensor_tensor(x[:, :], x_next[:, :], ta[:, :], ALU.add).then_inc(sem(L + "x"), 1)


            def g_layer(e, eng, L, n, nc_n, ready):
                ph = "C_"
                q_tok = qf[:, :].rearrange("p (t h d) -> p t h d", t=TT, h=HEADS)
                k_tok, v_tok = [VX[:, 0:TT // 2, :].rearrange("p a (b c r) -> p (a b) c r", b=2, c=2)[:, :, c] for c in range(2)]
                k_tok = k_tok.rearrange("p t (g d) -> p t g d", g=HEADS)
                v_tok = v_tok.rearrange("p t (d g) -> p t d g", g=HEADS)
                scores = VX[:, TT // 2:TT, :].rearrange("p a (b h g) -> p (a b) h g", b=2, h=HEADS)
                products = [PRB[:, 2 * i:2 * i + 2, :, :].rearrange("p a b c -> p (a b c)") for i in range(2)]

                gated = [PRB[:, i, :, :].rearrange("p b (e f) -> p (b e) f", f=P) for i in range(TT)]

                def score_products(eng_, t):
                    return eng_.tensor_tensor(
                        products[t % 2].rearrange("p (h g d) -> p h g d", h=HEADS, g=HEADS),
                        q_tok[:, t].unsqueeze(2).broadcast_to([P, HEADS, HEADS, HD]),
                        k_tok[:, t].unsqueeze(1).broadcast_to([P, HEADS, HEADS, HD]), ALU.mult)

                def value_products(eng_, t):
                    return eng_.tensor_tensor(
                        products[t % 2].rearrange("p (h d g) -> p h d g", h=HEADS, d=HD),
                        scores[:, t].unsqueeze(2).broadcast_to([P, HEADS, HD, HEADS]),
                        v_tok[:, t].unsqueeze(1)
                        .broadcast_to([P, HEADS, HD, HEADS]), ALU.mult)

                if eng == "pe":
                    yield from pe_norm(e, 0, ph, n, x[:, :], ready)
                    yield from pe_norm(e, 4, ph, n + 1, None, (L + "x1",), centered=False)
                    yield 10
                    e.wait_ge(*after(L + "xn"))
                    e.matmul(half(1, 0, LATENT), W("g_down"), xn[:, :], start=True, stop=True)
                    for t in range(TT):
                        ins = e.matmul(half(0, 0)[:, t * P:(t + 1) * P], xn[:, t * P:(t + 1) * P], W("g_q"),
                                       start=True, stop=True)
                    ins.then_inc(sem(L + "qd"), 1)
                    yield 12
                    e.wait_ge(*after(L + "down"))
                    for t in range(TT):
                        ins = e.matmul(half(2, t), tc[0:LATENT, t * P:(t + 1) * P],
                                       W("g_up", rows_=LATENT), start=True, stop=True)
                    ins.then_inc(sem(L + "kv"), 1)
                    yield 21
                    e.wait_ge(*after(L + "heads"))
                    for t in range(TT):
                        ins = e.transpose(half(3, 0)[:, t * P:(t + 1) * P], y[:, t * P:(t + 1) * P], K("ident"))
                    ins.then_inc(sem(L + "heads_t"), 1)
                    yield 23
                    e.wait_ge(*after(L + "y"))
                    e.matmul(half(1, 0), W("g_o"), ta[:, :], start=True, stop=True).then_inc(sem(L + "o"), 1)
                    yield from pe_norm(e, 23, ph, n + 2, None, (L + "x2",), centered=False)
                    yield 29
                    e.wait_ge(*after(L + "xm"))
                    for t in range(TT):
                        ins = e.matmul(half(3, 0)[:, t * EXPERTS:(t + 1) * EXPERTS], xn[:, t * P:(t + 1) * P], W("g_g"),
                                       start=True, stop=True)
                    ins.then_inc(sem(L + "logits"), 1)
                    for t in range(TT):
                        if t == 1:
                            yield 31
                            e.wait_ge(*after(L + "e0"))
                        for c in range(2):
                            ins = e.matmul(ps[:, turns_of_two(t) + c, :], xn[:, t * P:(t + 1) * P],
                                           W("g_e", c * 512, (c + 1) * 512), start=True, stop=True)
                        ins.then_inc(sem(L + "experts"), 1)
                    yield 36
                    for t in range(TT):
                        e.wait_ge(*after(L + "gated", t + 1))
                        for expert in range(EXPERTS):
                            ins = e.matmul(half(0, 0)[:, t * P:(t + 1) * P], gated[t][:, expert, :], K("ident"),
                                           start=(expert == 0), stop=(expert == EXPERTS - 1))
                    ins.then_inc(sem(L + "mixed_t"), 1)
                if eng == "act":
                    yield from act_norm(e, 0, ph, n, nc_n, e=EPS5)
                    yield from act_norm(e, 4, ph, n + 1, None, src=x1[:, :], ready=(L + "x1",), e=EPS6)
                    yield 11
                    e.wait_ge(*after(L + "qd"))
                    e.activation(tc[0:LATENT, :], half(1, 0, LATENT), ACT.Identity, bias=C("g_bdown", rows_=LATENT)).then_inc(sem(L + "down"), 1)
                    yield 17
                    e.wait_ge(*after(L + "shifted"))
                    e.activation(scores, scores, ACT.Exp, scale=float(HD) ** -0.5, bias=ZERO).then_inc(sem(L + "exp"), 1)
                    yield 22
                    e.wait_ge(*after(L + "heads_t"))
                    e.activation(ta[:, :], half(3, 0), ACT.Copy).then_inc(sem(L + "y"), 1)
                    yield from act_norm(e, 23, ph, n + 2, None, src=x1[:, :], ready=(L + "x2",), e=EPS6)
                    yield 31
                    e.wait_ge(*after(L + "e0"))
                    e.activation(small[:, 2, :], small[:, 1, :], ACT.Exp, bias=ZERO).then_inc(sem(L + "e1"), 1)
                if eng == "dve":
                    c = ph + "dve_chain"
                    yield from dve_norm(e, 0, ph, n, nc_n, x1[:, :], L + "x1")
                    e.wait_ge(*after(L + "x1"))
                    yield from dve_norm(e, 4, ph, n + 1, None, xn[:, :], L + "xn", src=x1[:, :], gamma=C("g_gamma1"))
                    yield 11
                    e.wait_ge(*after(L + "qd"))
                    e.tensor_tensor(qf[:, :].rearrange("p (t c) -> p t c", t=TT),
                                    half(0, 0).rearrange("p (t c) -> p t c", t=TT),
                                    R("g_bq").unsqueeze(1).broadcast_to([P, TT, P]), ALU.add)
                    yield 13
                    e.wait_ge(*after(L + "kv"))
                    kv = ps[:, BANK + 2, :].rearrange("p (t g c d) -> p t g c d", t=TT, g=HEADS, c=2)
                    bias = R("g_bup").rearrange("p (g c d) -> p g c d", g=HEADS, c=2)
                    for t in range(TT):
                        e.tensor_tensor(k_tok[:, t], kv[:, t, :, 0], bias[:, :, 0], ALU.add)
                        ins = e.tensor_tensor(v_tok[:, t].rearrange("p d g -> p g d"), kv[:, t, :, 1], bias[:, :, 1], ALU.add)
                    ins.then_inc(sem(L + "qkv"), 1)
                    yield 14
                    e.wait_ge(*after(L + "qkv"))

                    def sums(t, products_of, out_, sig):
                        if t % 2 == 0:
                            if t:
                                e.wait_ge(*after(sig, t - 1))
                            link(e, c, products_of(e, t))
                        else:
                            e.wait_ge(*after(sig + "_odd", (t + 1) // 2))
                        e.tensor_reduce(out_, products[t % 2].rearrange("p (a b) -> p a b", a=out_.shape[1]),
                                             AX_X, ALU.add).then_inc(sem(sig), 1)

                    for t in range(TT):
                        yield 14 + t
                        sums(t, score_products, scores[:, t].rearrange("p h g -> p (h g)"), L + "score")
                    yield 16
                    e.wait_ge(*after(L + "score", TT))
                    all_heads = scores.rearrange("p t h g -> p (t h) g")
                    link(e, c, e.tensor_reduce(small[:, 4:6, :].rearrange("p a b -> p (a b)"), all_heads, AX_X, ALU.max))
                    e.tensor_tensor(all_heads, all_heads,
                                         small[:, 4:6, :].rearrange("p a b -> p (a b)").unsqueeze(2)
                                         .broadcast_to([P, TT * HEADS, HEADS]), ALU.subtract).then_inc(sem(L + "shifted"), 1)
                    yield 18
                    e.wait_ge(*after(L + "exp"))
                    link(e, c, e.tensor_reduce(small[:, 6:8, :].rearrange("p a b -> p (a b)"), all_heads, AX_X, ALU.add))
                    link(e, c, e.reciprocal(small[:, 4:6, :], small[:, 6:8, :]))
                    for t in range(TT):
                        yield 18 + t
                        sums(t, value_products, y[:, t * P:(t + 1) * P], L + "value")
                    yield 20
                    e.wait_ge(*after(L + "value", TT))
                    heads = y[:, :].rearrange("p (a d) -> p a d", d=HD)
                    e.tensor_tensor(heads, heads, small[:, 4:6, :].rearrange("p a b -> p (a b)").unsqueeze(2)
                                         .broadcast_to([P, TT * HEADS, HD]), ALU.mult).then_inc(sem(L + "heads"), 1)
                    yield 24
                    e.wait_ge(*after(L + "o"))
                    e.scalar_tensor_tensor(x1[:, :], half(1, 0), C("g_bo"), x1[:, :], ALU.add, ALU.add).then_inc(sem(L + "x2"), 1)
                    e.wait_ge(*after(L + "x2"))
                    yield from dve_norm(e, 23, ph, n + 2, None, xn[:, :], L + "xm", src=x1[:, :], gamma=C("g_gamma2"))
                    e.tensor_tensor(x[:, :], x[:, :], x1[:, :], ALU.add)
                    yield 30
                    e.wait_ge(*after(L + "logits"))

                    def by_token(ap):
                        return ap.unsqueeze(2).broadcast_to([P, TT, EXPERTS])

                    def tile(i):
                        return small[:, i, :].rearrange("p (t e) -> p t e", t=TT)

                    link(e, c, e.tensor_tensor(tile(0), half(3, 0)[:, 0:TT * EXPERTS].rearrange("p (t e) -> p t e", t=TT),
                                               R("g_bg").unsqueeze(1).broadcast_to([P, TT, EXPERTS]), ALU.add))
                    link(e, c, e.tensor_reduce(stat[:, 0, :], tile(0), AX_X, ALU.max))
                    e.tensor_tensor(tile(1), tile(0), by_token(stat[:, 0, :]), ALU.subtract).then_inc(sem(L + "e0"), 1)
                    yield 32
                    e.wait_ge(*after(L + "e1"))
                    link(e, c, e.tensor_reduce(stat[:, 1, :], tile(2), AX_X, ALU.add))
                    link(e, c, e.reciprocal(stat[:, 2, :], stat[:, 1, :]))
                    link(e, c, e.tensor_tensor(tile(3), tile(2), by_token(stat[:, 2, :]), ALU.mult))
                    for t in range(TT):
                        yield 33 + t
                        e.wait_ge(*after(L + "experts", t + 1))
                        e.tensor_tensor(gated[t], ps[:, turns_of_two(t):turns_of_two(t) + 2, :].rearrange("p c (e f) -> p (c e) f", e=4),
                                        tile(3)[:, t, :].unsqueeze(2).broadcast_to([P, EXPERTS, P]), ALU.mult)\
                            .then_inc(sem(L + "gated"), 1)
                    yield 37
                    e.wait_ge(*after(L + "mixed_t"))
                    e.tensor_tensor(x[:, :], x[:, :], half(0, 0), ALU.add).then_inc(sem(L + "x"), 1)
                if eng == "pool":
                    yield 14
                    e.wait_ge(*after(L + "qkv"))
                    score_products(e, 1).then_inc(sem(L + "score_odd"), 1)
                    yield 18
                    e.wait_ge(*after(L + "exp"))
                    value_products(e, 1).then_inc(sem(L + "value_odd"), 1)

            def h_layer(e, eng, n, nc_n, ready):
                ph, L = "C_", "h_"
                if eng == "pe":
                    yield from pe_norm(e, 0, ph, n, x[:, :], ready)
                    yield 6
                    e.wait_ge(*after(L + "xn"))
                    for i in range(4):
                        ins = e.matmul(half(i // 2, i % 2, HH), W("h_proj", i * HH, (i + 1) * HH), xn[:, :], start=True, stop=True)
                    ins.then_inc(sem(L + "proj"), 1)
                    yield 9
                    e.wait_ge(*after(L + "conv", 2))
                    for name, bank in (("h_gate", 2), ("h_in", 3)):
                        for o in range(2):
                            for k in range(2):
                                ins = e.matmul(half(bank, o, HH),
                                               W(name, k * HID + o * HH, k * HID + (o + 1) * HH, HH), h_u[:, k, :],
                                               start=(k == 0), stop=(k == 1))
                        ins.then_inc(sem(L + "gates"), 1)
                    yield 16
                    e.wait_ge(*after(L + "m"))
                    for k in range(2):
                        ins = e.matmul(half(0, 0), W("h_out", k * P, (k + 1) * P, HH), h_gelu[:, k, :],
                                       start=(k == 0), stop=(k == 1))
                    ins.then_inc(sem(L + "o"), 1)
                if eng == "act":
                    yield from act_norm(e, 0, ph, n, nc_n, e=EPS5)
                    yield 7
                    e.wait_ge(*after(L + "proj"))
                    e.activation(u_pad[:, :, :, TAPS - 1:], ps[0:HH, BANK + 1, :].rearrange("p (a b t) -> p a b t", a=2, b=G),
                                      ACT.Copy).then_inc(sem(L + "pad"), 1)
                    e.activation(h_gelu, ps[0:HH, BANK, :].rearrange("p (a t) -> p a t", a=2), ACT.Gelu).then_inc(sem(L + "gelu"), 1)
                    e.preload_act_table_set(LN_EXP_SET)
                    yield 10
                    e.wait_ge(*after(L + "gates", 1))
                    for o in range(2):
                        ins = e.activation(h_sig_rec[:, o, :], half(2, o, HH), ACT.Exp, scale=-1.0,
                                           bias=neg_bias[0:HH, 2 + o:3 + o])
                    link(e, ph + "act_chain", ins)
                    link(e, ph + "act_chain", e.activation(h_sig_rec, h_sig_rec, ACT.Ln, bias=eps[0:HH, 3:4]))
                    link(e, ph + "act_chain",
                         e.activation(h_sig_rec, h_sig_rec, ACT.Exp, scale=-1.0, bias=eps[0:HH, 2:3]))
                    for o in range(2):
                        ins = e.activation(h_alpha[:, o, :], h_sig_rec[:, o, :], ACT.Exp, scale=decay[0:HH, o:o + 1],
                                           bias=eps[0:HH, 2:3])
                    ins.then_inc(sem(L + "alpha"), 1)
                    yield 12
                    e.wait_ge(*after(L + "gates", 2))
                    for o in range(2):
                        ins = e.activation(h_sig_in[:, o, :], half(3, o, HH), ACT.Exp, scale=-1.0,
                                           bias=neg_bias[0:HH, o:o + 1])
                    link(e, ph + "act_chain", ins)
                    link(e, ph + "act_chain", e.activation(h_sig_in, h_sig_in, ACT.Ln, bias=eps[0:HH, 3:4]))
                    e.activation(h_sig_in, h_sig_in, ACT.Exp, scale=-1.0, bias=eps[0:HH, 2:3]).then_inc(sem(L + "sig_in"), 1)
                    yield 14
                    e.wait_ge(*after(L + "one_less"))
                    link(e, ph + "act_chain", e.activation(h_beta, h_beta, ACT.Ln, bias=eps[0:HH, 1:2]))
                    e.activation(h_beta, h_beta, ACT.Exp, scale=0.5, bias=eps[0:HH, 2:3]).then_inc(sem(L + "beta"), 1)
                if eng == "dve":
                    c = ph + "dve_chain"
                    yield from dve_norm(e, 0, ph, n, nc_n, xn[:, :], L + "xn")
                    yield 8
                    e.wait_ge(*after(L + "pad"))
                    for k in range(TAPS):
                        for o in range(2):
                            src, dst = u_pad[:, o, :, k:k + SEQ], seq2(h_u[:, o, :])
                            tap = C("h_conv", o * TAPS + k, HH)
                            if k == 0:
                                ins = e.tensor_scalar(dst, src, tap, C("h_cb", o, HH), ALU.mult, ALU.add)
                            else:
                                ins = e.scalar_tensor_tensor(dst, src, tap, dst, ALU.mult, ALU.add)
                            if k == TAPS - 1:
                                ins.then_inc(sem(L + "conv"), 1)
                        if k < TAPS - 1:
                            link(e, c, ins)
                    yield 12
                    e.wait_ge(*after(L + "alpha"))
                    link(e, c, e.tensor_tensor(h_beta, h_alpha, h_alpha, ALU.mult))
                    e.tensor_scalar(h_beta, h_beta, -1.0, 1.0, ALU.mult, ALU.add).then_inc(sem(L + "one_less"), 1)
                    yield 15
                    e.wait_ge(*after(L + "sig_in"))
                    link(e, c, e.tensor_tensor(h_sig_in, h_sig_in, h_u, ALU.mult))
                    e.wait_ge(*after(L + "beta"))
                    link(e, c, e.tensor_tensor(h_beta, h_beta, h_sig_in, ALU.mult))
                    for o in range(2):
                        for b in range(G):
                            s = slice(b * SEQ, (b + 1) * SEQ)
                            ins = e.tensor_tensor_scan(h_u[:, o, s], h_alpha[:, o, s], h_beta[:, o, s], 0.0,
                                                       ALU.mult, ALU.add)
                    link(e, c, ins)
                    e.tensor_tensor(h_gelu, h_gelu, h_u, ALU.mult).then_inc(sem(L + "m"), 1)
                    yield 17
                    e.wait_ge(*after(L + "o"))
                    e.tensor_tensor(x[:, :], x[:, :], half(0, 0), ALU.add).then_inc(sem(L + "x"), 1)

            def out_layer(e, eng, ready):
                if eng == "pe":
                    yield 0
                    e.wait_ge(*after(*ready))
                    for t in range(TT):
                        ins = e.transpose(half(1, 0)[:, t * P:(t + 1) * P], x[:, t * P:(t + 1) * P], K("ident"))
                    ins.then_inc(sem("C_out_t"), 1)
                    yield 2
                    e.wait_ge(*after("C_out"))
                    settle(e)
                if eng == "act":
                    yield 1
                    e.wait_ge(*after("C_out_t"))
                    e.wait_ge(*after("C_stored", 0))
                    e.activation(x_tok[:, :, :].rearrange("p t d -> p (t d)"), half(1, 0), ACT.Copy).then_inc(sem("C_out"), 1)
                if eng == "sp":
                    yield 2
                    e.wait_ge(*after("C_out"))
                    settle(e)
                    e.dma_start(out.rearrange("(i s t p) d -> i s p t d", s=STREAMS, t=TT, p=P)[turn[0]][lane], x_tok[:, :, :]).then_inc(sem("C_stored"), 16)
                    yield 4
                    e.wait_ge(*after("C_stored", 16))
                    settle(e)

            def load_tokens(sp, i):
                sp.dma_start(x_tok[:, :, :], x_in.rearrange("(i s t p) d -> i s p t d", s=STREAMS, t=TT, p=P)[i][lane])\
                    .then_inc(sem("A_tokens"), 16)

            def load_readout(sp, i):
                def of(dram):
                    return dram.rearrange("(i b) p t -> i b p t", b=STREAMS)[i][lane]

                sp.dma_start(u_rows, of(u_dram)).then_inc(sem("C_readout"), 16)
                sp.dma_start(q_rows, of(q_dram)).then_inc(sem("C_readout"), 16)
                sp.dma_start(x_next[:, :], of(x_dram)).then_inc(sem("C_readout"), 16)
                for h in range(DH):
                    rows_ = slice(DD * h, DD * (h + 1))
                    sp.dma_start(KZ[rows_, h, :], of(k_dram)[rows_]).then_inc(sem("C_readout"), 16)

            def load_layer(e, eng):
                if eng == "pe":
                    yield 0
                    e.wait_ge(*after("A_tokens", 16))
                    for t in range(TT):
                        ins = e.transpose(half(0, 0)[:, t * P:(t + 1) * P], x_tok[:, t, :], K("ident"))
                    ins.then_inc(sem("A_x_t"), 1)
                if eng == "dve":
                    yield 1
                    e.wait_ge(*after("A_x_t"))
                    e.tensor_copy(x[:, :], half(0, 0)).then_inc(sem("A_x"), 1)
                if eng == "sp":
                    yield 1
                    e.wait_ge(*after("A_x_t"))
                    settle(e)
                    load_tokens(e, (turn[0] + 1) % TURNS)

            def prefetch_layer(e, eng):
                if eng == "sp":
                    yield 0
                    e.wait_ge(*after("r_x"))
                    settle(e)
                    load_readout(e, (turn[0] + 1) % TURNS)

            def in_turn(*layers_):
                at = 0
                for steps, layer in layers_:
                    for step in layer:
                        yield at + step
                    at += steps

            def front(e, eng):
                return in_turn((STEPS["LOAD"], load_layer(e, eng)), (STEPS["A"], a_layer(e, eng, 0)),
                               (STEPS["F"], f_layer(e, eng, "f1_", 1, ("a_x",))),
                               (STEPS["B"], b_layer(e, eng, 2, ("f1_x",))),
                               (STEPS["F"], f_layer(e, eng, "f2_", 4, ("b_x",))),
                               (STEPS["D"], d_layer(e, eng, 5, ("f2_x",))))

            def back(e, eng):
                return in_turn((STEPS["R"], r_layer(e, eng)), (STEPS["NEXT"], prefetch_layer(e, eng)),
                               (STEPS["G"], g_layer(e, eng, "g1_", 1, 1, ("r_x",))),
                               (STEPS["H"], h_layer(e, eng, 4, 2, ("g1_x",))),
                               (STEPS["G"], g_layer(e, eng, "g2_", 5, 3, ("h_x",))),
                               (STEPS["OUT"], out_layer(e, eng, ("g2_x",))))

            return Stream(front=front, back=back, load_tokens=load_tokens, load_readout=load_readout,
                          sem=sem, zeroed=(KZ, u_pad), UX=UX, VX=VX)

        streams = [stream(lane) for lane in range(STREAMS)]

        def side_by_side(*programs):
            due = [next(program, None) for program in programs]
            step = 0
            while any(d is not None for d in due):
                for i, program in enumerate(programs):
                    while due[i] is not None and due[i] <= step:
                        due[i] = next(program, None)
                step += 1

        def loop(e, which, eng):
            with e.Fori(0, TURNS) as it:
                turn[0] = it
                for chain in chains:
                    chain.clear()
                side_by_side(*[st.front(e, eng) if which == "front" else st.back(e, eng) for st in streams])

        beta_k = bands[:, :, :, :].rearrange("p a h t -> p (a h t)").bitcast(F32)\
            .rearrange("p (j d t) -> p j d t", j=2, d=DD)

        def beta_of(j):
            return scan_b[:, j, :].unsqueeze(1).broadcast_to([P, DD, SEQ])

        def at_step(array, t):
            return array[:, :, :, bass.ds(t, 1)].rearrange("p j d o -> p j (d o)")

        def over_values(k, rows_):
            return k.unsqueeze(2).broadcast_to([P, 2, rows_, DD])

        def over_keys(u):
            return u.unsqueeze(3).broadcast_to([P, 2, u.shape[2], DD])

        block = ctx.enter_context(nc.Block())

        @block.sync
        def _(sp):
            for dst, src in ((w_sb, weights), (col_sb, columns), (const_sb, consts)):
                sp.dma_start(dst[:, :], src).then_inc(sem("params"), 16)
            sp.dma_start(row_sb[:, :], rows.partition_broadcast(P)).then_inc(sem("params"), 16)
            for st in streams:
                st.load_tokens(sp, 0)
            loop(sp, "front", "sp")
            for st in streams:
                sp.wait_ge(st.sem("A_tokens"), 16 * (TURNS + 1))
            for j in range(2):
                for dst, src in ((scan_k, k_dram), (scan_v, v_dram)):
                    sp.dma_start(dst[:, j, :, :], src.rearrange("(j b) (h d) t -> j (b h) d t", j=2, h=DH)[j])\
                        .then_inc(sem("scan_loaded"), 16)
                sp.dma_start(scan_b[:, j, :], b_dram.rearrange("(j b) h t -> j (b h) t", j=2)[j])\
                    .then_inc(sem("scan_loaded"), 16)
            sp.wait_ge(sem("scanned"), 1)
            for j in range(2):
                sp.dma_start(u_dram.rearrange("(j b) (h d) t -> j (b h) d t", j=2, h=DH)[j], scan_v[:, j, :, :])\
                    .then_inc(sem("updates_stored"), 16)
            sp.wait_ge(sem("updates_stored"), 32)
            sp.wait_ge(sem("zeroed"), 1)
            for st in streams:
                st.load_readout(sp, 0)
            loop(sp, "back", "sp")
            for st in streams:
                sp.wait_ge(st.sem("C_readout"), 16 * (3 + DH) * (TURNS + 1))

        @block.tensor
        def _(pe):
            pe.wait_ge(sem("params"), 64)
            pe.wait_ge(sem("ready"), 6 + 2 * STREAMS)
            loop(pe, "front", "pe")
            loop(pe, "back", "pe")

        @block.scalar
        def _(act):
            act.wait_ge(sem("params"), 64)
            act.wait_ge(sem("ready"), 6 + 2 * STREAMS)
            act.preload_act_table_set(LN_EXP_SET)
            act.activation(dec_t[:, 0:2], col_sb[:, C_AT["h_lambda"][0]:C_AT["h_lambda"][0] + 2], ACT.Abs)\
                .then_inc(sem("softplus"), 1)
            act.wait_ge(sem("softplus"), 1)
            act.activation(dec_t[:, 2:4], dec_t[:, 0:2], ACT.Exp, scale=-1.0, bias=ZERO).then_inc(sem("softplus"), 1)
            act.wait_ge(sem("softplus"), 2)
            act.activation(dec_t[:, 4:6], dec_t[:, 2:4], ACT.Ln, bias=eps[:, 3:4]).then_inc(sem("softplus"), 1)
            loop(act, "front", "act")
            loop(act, "back", "act")

        @block.gpsimd
        def _(pool):
            pool.memset(bands[:, 0], 0.0).then_inc(sem("ready"), 1)
            for st in streams:
                pool.memset(st.VX[:, :, :], 0.0).then_inc(sem("ready"), 1)
                pool.memset(st.UX[:, :, :], 0.0).then_inc(sem("ready"), 1)
            loop(pool, "front", "pool")
            far = slice(NEAR_ROWS, DD)
            pool.memset(state[:, :, far], 0.0).then_inc(sem("far_products"), 1)
            pool.wait_ge(sem("scan_loaded"), 96)
            pool.tensor_tensor(beta_k[:, 1], scan_k[:, 1], beta_of(1), ALU.mult).then_inc(sem("beta_k"), 1)
            pool.wait_ge(sem("beta_k"), 2)
            with pool.Fori(0, SEQ) as t:
                far_before = t * FAR_PRODUCTS + 1
                pool.wait_ge(sem("far_products"), far_before)
                pool.tensor_tensor(outer[:, :, far], state[:, :, far],
                                   over_values(at_step(beta_k, t), DD - NEAR_ROWS), ALU.mult)\
                    .then_inc(sem("far_products"), 1)
                pool.wait_ge(sem("far_updates"), t * 2 + 2)
                pool.tensor_tensor(outer[:, :, far], over_keys(at_step(scan_v, t)[:, :, far]),
                                   over_values(at_step(scan_k, t), DD - NEAR_ROWS), ALU.mult)\
                    .then_inc(sem("far_products"), 1)
                pool.wait_ge(sem("far_products"), far_before + 2)
                pool.tensor_tensor(state[:, :, far], state[:, :, far], outer[:, :, far], ALU.add)\
                    .then_inc(sem("far_products"), 1)
            loop(pool, "back", "pool")

        @block.vector
        def _(dve):
            for i in range(1, 2 * STREAMS):
                ins = dve.memset(bands[:, i], 0.0)
            ins.then_inc(sem("k_zeroed"), 1)
            dve.memset(eps[:, 0:1], 1e-5).then_inc(sem("ready"), 1)
            dve.memset(eps[:, 1:2], 1e-6).then_inc(sem("ready"), 1)
            dve.memset(eps[:, 2:3], 0.0)
            dve.memset(eps[:, 3:4], 1.0).then_inc(sem("ready"), 1)
            dve.wait_ge(sem("k_zeroed"), 1)
            for lane in range(STREAMS):
                ins = dve.memset(bands[SHIFT_ROW:P, 2 * lane + 1], 1.0)
            ins.then_inc(sem("ready"), 1)
            dve.wait_ge(sem("params"), 64)
            dve.tensor_copy(ident_b[:, :], K("ident")).then_inc(sem("ready"), 1)
            lam = C_AT["h_lambda"][0]
            dve.tensor_scalar(dec_t[:, 6:8], col_sb[:, lam:lam + 2], 0.0, None, ALU.max).then_inc(sem("dec"), 1)
            dve.wait_ge(sem("softplus"), 3)
            dve.wait_ge(sem("dec"), 1)
            dve.tensor_tensor(dec_t[:, 6:8], dec_t[:, 6:8], dec_t[:, 4:6], ALU.add).then_inc(sem("dec"), 1)
            dve.wait_ge(sem("dec"), 2)
            dve.tensor_scalar(decay[:, :], dec_t[:, 6:8], -8.0, None, ALU.mult).then_inc(sem("dec"), 1)
            b_in = C_AT["h_bin"][0]
            dve.tensor_scalar(neg_bias[:, :], col_sb[:, b_in:b_in + 4], -1.0, None, ALU.mult).then_inc(sem("dec"), 1)
            loop(dve, "front", "dve")

            near, far = slice(0, NEAR_ROWS), slice(NEAR_ROWS, DD)
            dve.memset(state[:, :, near], 0.0)
            dve.wait_ge(sem("scan_loaded"), 96)
            dve.tensor_tensor(beta_k[:, 0], scan_k[:, 0], beta_of(0), ALU.mult).then_inc(sem("beta_k"), 1)
            for j in range(2):
                ins = dve.tensor_tensor(scan_v[:, j], scan_v[:, j], beta_of(j), ALU.mult)
            ins.then_inc(sem("near_step"), 1)
            dve.wait_ge(sem("beta_k"), 2)
            with dve.Fori(0, SEQ) as t:
                near_before = t * NEAR_STEPS + 1
                dve.wait_ge(sem("near_step"), near_before)
                dve.tensor_tensor(outer[:, :, near], state[:, :, near], over_values(at_step(beta_k, t), NEAR_ROWS),
                                  ALU.mult).then_inc(sem("near_step"), 1)
                dve.wait_ge(sem("far_products"), t * FAR_PRODUCTS + 2)
                dve.tensor_reduce(s_k[:, :, far], outer[:, :, far], AX_X, ALU.add).then_inc(sem("far_updates"), 1)
                dve.wait_ge(sem("near_step"), near_before + 1)
                dve.tensor_reduce(s_k[:, :, near], outer[:, :, near], AX_X, ALU.add).then_inc(sem("near_step"), 1)
                dve.wait_ge(sem("far_updates"), t * 2 + 1)
                u_far = at_step(scan_v, t)[:, :, far]
                dve.tensor_tensor(u_far, u_far, s_k[:, :, far], ALU.subtract).then_inc(sem("far_updates"), 1)
                dve.wait_ge(sem("near_step"), near_before + 2)
                u_near = at_step(scan_v, t)[:, :, near]
                dve.tensor_tensor(u_near, u_near, s_k[:, :, near], ALU.subtract).then_inc(sem("near_step"), 1)
                dve.wait_ge(sem("near_step"), near_before + 3)
                dve.tensor_tensor(outer[:, :, near], over_keys(u_near), over_values(at_step(scan_k, t), NEAR_ROWS),
                                  ALU.mult).then_inc(sem("near_step"), 1)
                dve.wait_ge(sem("near_step"), near_before + 4)
                dve.tensor_tensor(state[:, :, near], state[:, :, near], outer[:, :, near], ALU.add)\
                    .then_inc(sem("near_step"), 1)
            dve.wait_ge(sem("near_step"), SEQ * NEAR_STEPS + 1)
            dve.wait_ge(sem("far_products"), SEQ * FAR_PRODUCTS + 1)
            dve.tensor_copy(s_k[:, :, :], state[:, :, 0, :]).then_inc(sem("scanned"), 1)
            dve.wait_ge(sem("updates_stored"), 32)
            for st in streams:
                for ap in st.zeroed:
                    ins = dve.memset(ap, 0.0)
            ins.then_inc(sem("zeroed"), 1)
            loop(dve, "back", "dve")


def layouts(a):
    def heads_last(w):
        n = w.shape[-1] // HD
        return w.reshape(w.shape[:-1] + (n, HD)).swapaxes(-1, -2).reshape(w.shape)

    def partner(w, order):
        n = w.shape[-1] // HD
        return w.reshape(w.shape[:-1] + (n, HD))[..., order].reshape(w.shape)

    half = [4, 5, 6, 7, 0, 1, 2, 3]
    inter = [1, 0, 3, 2, 4, 5, 6, 7]
    wi, bi = a["L0_attn_b_W_in"], a["L0_attn_b_b_in"]
    w = dict(
        a_q=heads_last(a["L0_attn_a_w_q"]), a_q2=heads_last(partner(a["L0_attn_a_w_q"], half)),
        a_k=heads_last(a["L0_attn_a_w_k"]), a_k2=heads_last(partner(a["L0_attn_a_w_k"], half)),
        a_v=a["L0_attn_a_w_v"], a_o=a["L0_attn_a_w_o"],
        f_base=a["L0_ffn_base_w"].T, f_A=a["L0_ffn_lora_A"].transpose(1, 0, 2).reshape(P, -1),
        f_B=a["L0_ffn_lora_B"].reshape(-1, P), f_r=a["L0_ffn_router_w"].T,
        b_q=heads_last(wi[:, :P]), b_q2=heads_last(partner(wi[:, :P], inter)),
        b_k=heads_last(wi[:, P:2 * P]), b_k2=heads_last(partner(wi[:, P:2 * P], inter)),
        b_v=wi[:, 2 * P:], b_o=a["L0_attn_b_W_out"],
        d_q=a["L1_attn_a_Wq"], d_k=a["L1_attn_a_Wk"], d_v=a["L1_attn_a_Wv"], d_b=a["L1_attn_a_Wb"],
        g_q=a["L1_ffn_Wq"], g_down=a["L1_ffn_Wdown"], g_up=a["L1_ffn_Wup"],
        g_o=a["L1_ffn_Wo"], g_g=a["L1_ffn_Wg"], g_e=a["L1_ffn_We"].transpose(1, 0, 2).reshape(P, -1),
        h_proj=a["L1_attn_b_W_proj"].T,
        h_in=a["L1_attn_b_W_in"].T.reshape(2, HH, HID).transpose(1, 0, 2).reshape(HH, -1),
        h_gate=a["L1_attn_b_W_gate"].T.reshape(2, HH, HID).transpose(1, 0, 2).reshape(HH, -1),
        h_out=a["L1_attn_b_W_out"].T.reshape(2, HH, P).transpose(1, 0, 2).reshape(HH, -1))

    def halves(v):
        return v.reshape(2, HH, -1).transpose(1, 0, 2).reshape(HH, -1)

    c = dict(
        f_bb=a["L0_ffn_base_b"], b_bq=heads_last(bi[:P]), b_bq2=heads_last(partner(bi[:P], inter)),
        b_bk=heads_last(bi[P:2 * P]), b_bk2=heads_last(partner(bi[P:2 * P], inter)),
        b_bo=a["L0_attn_b_b_out"], b_gamma=a["L0_attn_b_gamma"], b_beta=a["L0_attn_b_beta"],
        d_lnw=a["L1_attn_a_ln_w"], d_lnb=a["L1_attn_a_ln_b"], g_gamma1=a["L1_ffn_gamma1"],
        g_bdown=a["L1_ffn_bdown"],
        g_bo=a["L1_ffn_bo"], g_gamma2=a["L1_ffn_gamma2"],
        h_conv=halves(a["L1_attn_b_conv_w"].reshape(HID, TAPS)), h_cb=halves(a["L1_attn_b_conv_b"]),
        h_bin=halves(a["L1_attn_b_b_in"]), h_bgate=halves(a["L1_attn_b_b_gate"]),
        h_lambda=halves(a["L1_attn_b_forget_lambda"]))
    r = dict(f_rb=a["L0_ffn_router_b"], b_bv=bi[2 * P:], g_bq=a["L1_ffn_bq"], g_bup=a["L1_ffn_bup"], g_bg=a["L1_ffn_bg"])

    def pack(table, parts):
        at, n = offsets(table)
        out = np.zeros((P, n), np.float32)
        for name, (lo, m) in at.items():
            v = np.asarray(parts[name])
            v = v.reshape(v.shape[0], -1)
            out[0:v.shape[0], lo:lo + m] = v
        return out

    row = np.concatenate([np.asarray(r[name]) for name in ROWS]).astype(np.float32)
    return pack(WEIGHTS, w), pack(COLUMNS, c), row


def constants():
    i = np.arange(P)
    pos = np.arange(SEQ, dtype=np.float32)

    def rotary(freq, sign, heads):
        cos = np.ones((HD, SEQ), np.float32)
        sin = np.zeros((HD, SEQ), np.float32)
        for d in range(HD):
            if freq[d] is not None:
                cos[d], sin[d] = np.cos(pos * freq[d]), sign[d] * np.sin(pos * freq[d])
        return np.repeat(cos, heads, 0), np.repeat(sin, heads, 0)

    fa = (1.0 / np.float32(10000.0) ** (np.arange(0, HD, 2, dtype=np.float32) / HD)).astype(np.float32)
    fb = (1.0 / np.float32(10000.0) ** (np.arange(0, 4, 2, dtype=np.float32) / 4)).astype(np.float32)
    sa = [-1] * 4 + [1] * 4
    cos_a, sin_a = rotary(list(fa) + list(fa), sa, HEADS)
    cos_ak, sin_ak = rotary(list(fa) + list(fa), sa, KV_A)
    cos_b, sin_b = rotary([fb[0], fb[0], fb[1], fb[1]] + [None] * 4, [-1, 1, -1, 1] + [0] * 4, HEADS)
    tri = (i[:, None] <= i[None, :]).astype(np.float32)
    den = np.zeros((P, 4, STRIP), np.float32)
    for n in range(4):
        den[:, n, HD * n:HD * n + HD] = 1.0
    j = np.arange(KV_A * HD)
    parts = dict(
        ident=np.eye(P), center=np.eye(P) - 1.0 / P, mean=np.full((P, P), 1.0 / P),
        head_mean=(i[:, None] % HEADS == i[None, :] % HEADS) / HD,
        kv_mean=(j[:, None] % KV_A == j[None, :] % KV_A) / HD,
        head_sum=(i[:, None] // DD == i[None, :] // DD),
        cos_a=cos_a, sin_a=sin_a, cos_ak=cos_ak, sin_ak=sin_ak, cos_b=cos_b, sin_b=sin_b,
        causal=np.concatenate([tri, np.ones((P, P)), tri], 1), den=den.reshape(P, -1))
    at, n = offsets(CONSTS)
    out = np.zeros((P, n), np.float32)
    for name, (lo, m) in at.items():
        v = parts[name]
        out[0:v.shape[0], lo:lo + m] = v
    return out


def kernel(**inputs):
    import concourse.bacc as bacc
    from concourse.bass_utils import run_bass_kernel_spmd

    a = {k: np.asarray(v) for k, v in inputs.items()}
    w, c, r = layouts(a)
    arrays = dict(x_dram_in=np.ascontiguousarray(a["L0_attn_a_x"]).reshape(SEQS * SEQ, P),
                  weights_dram=w, columns_dram=c, rows_dram=r, consts_dram=constants())
    nc = bacc.Bacc("TRN2", target_bir_lowering=False, num_devices=1)
    args = [nc.dram_tensor(n, v.shape, mybir.dt.from_np(v.dtype), kind="ExternalInput").ap()
            for n, v in arrays.items()]
    out = nc.dram_tensor("out_dram", (SEQS * SEQ, P), F32, kind="ExternalOutput").ap()
    build(nc, *args, out)
    got = run_bass_kernel_spmd(nc, [arrays], core_ids=[0]).results[0]["out_dram"]
    return got.reshape(SEQS, SEQ, P)
```
